# Optimizing a Trainium2 kernel written in Bass

```python
import numpy as np
import jax
import jax.numpy as jnp

def _softmax(x, axis=-1):
    return jax.nn.softmax(x, axis=axis)

def _gelu(x):
    return jax.nn.gelu(x, approximate=True)

def _silu(x):
    return jax.nn.silu(x)

def _sigmoid(x):
    return jax.nn.sigmoid(x)

def _layernorm(x, axis=-1, eps=1e-05):
    m = jnp.mean(x, axis=axis, keepdims=True)
    v = jnp.var(x, axis=axis, keepdims=True)
    return (x - m) / jnp.sqrt(v + eps)

def _scatter_add(tgt, idx, src, axis=0):
    return tgt.at[idx].add(src)

def _segment_sum(src, seg, n):
    return jax.ops.segment_sum(src, seg, n)
kernel_name = 'mk_xattn_ffn_d4_seqx_r4_6ae6fc'

def setup_inputs(seed: int=0):
    np.random.seed(seed)
    _w = jnp.asarray

    def _rec_inputs():
        import jax
        import jax.numpy as jnp
        _rk = jax.random.key(seed)
        x = -0.0002928 + 1 * jax.random.normal(jax.random.fold_in(_rk, 1), (16, 128, 256), jnp.float32)
        _lenS = 128 - jax.random.randint(jax.random.fold_in(_rk, 7), (16,), 0, max(1, 128 // 4) + 1, jnp.int32)
        _lenS2 = 128 - jax.random.randint(jax.random.fold_in(_rk, 8), (16,), 0, max(1, 128 // 4) + 1, jnp.int32)
        _ctx_1024P = jax.random.normal(jax.random.fold_in(_rk, 11), (16, 16, 256), jnp.float32)
        _ctx_1024c = jax.random.dirichlet(jax.random.fold_in(_rk, 511), 0.3 * jnp.ones((16,), jnp.float32), (16, 128))
        _ctx_1024t = jnp.einsum('bsk,bkd->bsd', _ctx_1024c, _ctx_1024P)
        _ctx_1024t = _ctx_1024t * jax.lax.rsqrt(jnp.mean(jnp.square(_ctx_1024t)) + 1e-12) * 0.953939
        ctx_1024 = -1.39393e-06 + 0.999914 * (_ctx_1024t + 0.3 * jax.random.normal(jax.random.fold_in(_rk, 611), (16, 128, 256), jnp.float32))
        _validS = jnp.arange(128)[None, :] < _lenS[:, None]
        _validS2 = jnp.arange(128)[None, :] < _lenS2[:, None]
        _causal = jnp.tril(jnp.ones((128, 128), dtype=bool))
        mask_BxS2_bk0 = jnp.logical_not(jnp.broadcast_to(_validS2[:, :], (16, 128)))
        return (x, ctx_1024, mask_BxS2_bk0)
    x, ctx_1024, mask_BxS2_bk0 = _rec_inputs()

    def _L0_xattn_setup():
        import jax, jax.numpy as jnp
        import numpy as np
        import math
        EPS = 1e-08
        LN_EPS = 1e-05
        B, S, E, NH = (2, 512, 256, 4)
        DH = E // NH

        def _mlstm_cell(q, k, v, igate_w, igate_b, fgate_w, fgate_b, out_w):
            Bq, Sq, Eq = q.shape
            if_in = jnp.concatenate([q, k, v], axis=-1)
            ig = jnp.einsum('bsf,hf->bsh', if_in, igate_w) + igate_b
            fg = jnp.einsum('bsf,hf->bsh', if_in, fgate_w) + fgate_b
            ig = jnp.transpose(ig, (0, 2, 1))[..., None]
            fg = jnp.transpose(fg, (0, 2, 1))[..., None]
            qh = q.reshape(Bq, Sq, NH, DH).transpose(0, 2, 1, 3)
            kh = k.reshape(Bq, Sq, NH, DH).transpose(0, 2, 1, 3)
            vh = v.reshape(Bq, Sq, NH, DH).transpose(0, 2, 1, 3)
            log_fg = jax.nn.log_sigmoid(fg)
            cs = jnp.cumsum(log_fg, axis=2)
            cs_shift = jnp.concatenate([jnp.zeros_like(cs[:, :, :1]), cs[:, :, :-1]], axis=2)
            logfg_mat = cs - jnp.swapaxes(cs_shift, -2, -1)
            ltr = jnp.tril(jnp.ones((Sq, Sq), dtype=bool))
            logfg_mat = jnp.where(ltr, logfg_mat, -jnp.inf)
            log_D = logfg_mat + jnp.swapaxes(ig, -2, -1)
            max_log_D = jnp.max(log_D, axis=-1, keepdims=True)
            D = jnp.exp(log_D - max_log_D)
            qk = jnp.einsum('bhsd,bhtd->bhst', qh, kh / math.sqrt(DH))
            C = qk * D
            sum_C_abs = jnp.abs(jnp.sum(C, axis=-1, keepdims=True))
            normaliser = jnp.maximum(sum_C_abs, jnp.exp(-max_log_D))
            C_norm = C / (normaliser + EPS)
            h = jnp.einsum('bhst,bhtd->bhsd', C_norm, vh)
            mean = jnp.mean(h, axis=-1, keepdims=True)
            var = jnp.mean((h - mean) ** 2, axis=-1, keepdims=True)
            h_norm = (h - mean) / jnp.sqrt(var + LN_EPS)
            scale = (1.0 + out_w).reshape(1, NH, 1, DH)
            h_norm = h_norm * scale
            return h_norm.transpose(0, 2, 1, 3).reshape(Bq, Sq, Eq)
        key = jax.random.key(seed)
        ks = jax.random.split(key, 7)
        std_g = math.sqrt(2.0 / (5.0 * 3 * E))
        return {'q': jax.random.normal(ks[0], (B, S, E), dtype=jnp.float32), 'k': jax.random.normal(ks[1], (B, S, E), dtype=jnp.float32), 'v': jax.random.normal(ks[2], (B, S, E), dtype=jnp.float32), 'igate_w': jax.random.normal(ks[3], (NH, 3 * E), dtype=jnp.float32) * std_g, 'igate_b': jax.random.normal(ks[4], (NH,), dtype=jnp.float32) * 0.1, 'fgate_w': jax.random.normal(ks[5], (NH, 3 * E), dtype=jnp.float32) * std_g, 'fgate_b': jnp.linspace(3.4, 6.0, NH, dtype=jnp.float32), 'out_w': jnp.zeros((E,), dtype=jnp.float32)}
    _L0_xattn_all = _L0_xattn_setup()
    _L0_xattn_in = {k: v for k, v in _L0_xattn_all.items() if k in ('igate_w', 'igate_b', 'fgate_w', 'fgate_b', 'out_w')}
    del _L0_xattn_all

    def _L0_ffn_setup():
        import jax, jax.numpy as jnp
        import numpy as np
        N_EXPERTS = 8
        TOP_K = 2
        N_EMBD = 256
        EXPERT_DIM = 512
        key = jax.random.key(seed)
        k_x, k_r, k_f1, k_f2 = jax.random.split(key, 4)
        x = jax.random.normal(k_x, (4, 512, N_EMBD), dtype=jnp.float32)
        router_w = jax.random.normal(k_r, (N_EXPERTS, N_EMBD), dtype=jnp.float32) * 0.02
        fc1_w = jax.random.normal(k_f1, (N_EXPERTS, EXPERT_DIM, N_EMBD), dtype=jnp.float32) * 0.02
        fc2_w = jax.random.normal(k_f2, (N_EXPERTS, N_EMBD, EXPERT_DIM), dtype=jnp.float32) * 0.02
        return {'x': x, 'router_w': router_w, 'fc1_w': fc1_w, 'fc2_w': fc2_w}
    _L0_ffn_all = _L0_ffn_setup()
    _L0_ffn_in = {k: v for k, v in _L0_ffn_all.items() if k in ('router_w', 'fc1_w', 'fc2_w')}
    del _L0_ffn_all

    def _L1_xattn_setup():
        import jax, jax.numpy as jnp
        import numpy as np
        NUM_HEADS, NUM_KV, HEAD_DIM, WIDTH = (4, 1, 64, 256)
        MASK_FILL = -2.3819763e+38

        def _apply_rope(x, positions, max_wavelength=10000.0):
            d = x.shape[-1]
            freq_exp = 2.0 / d * jnp.arange(d // 2, dtype=jnp.float32)
            timescale = max_wavelength ** freq_exp
            radians = positions[..., None].astype(jnp.float32) / timescale
            radians = radians[..., None, :]
            sin, cos = (jnp.sin(radians), jnp.cos(radians))
            x1, x2 = jnp.split(x, 2, axis=-1)
            out = jnp.concatenate([x1 * cos - x2 * sin, x2 * cos + x1 * sin], axis=-1)
            return out.astype(x.dtype)

        def _rmsnorm(x, scale):
            var = jnp.mean(jnp.square(x.astype(jnp.float32)), axis=-1, keepdims=True)
            normed = x * jax.lax.rsqrt(var + 1e-06)
            return (normed * (1 + scale)).astype(x.dtype)
        key = jax.random.key(seed)
        ks = jax.random.split(key, 7)
        B, T, S = (8, 128, 512)
        return {'x': jax.random.normal(ks[0], (B, T, WIDTH), jnp.float32), 'mem_seq': jax.random.normal(ks[1], (B, S, WIDTH), jnp.float32), 'mem_mask': jax.random.randint(ks[2], (B, S), 0, 2).astype(bool), 'rms_scale': jax.random.normal(ks[3], (WIDTH,), jnp.float32) * 0.02, 'q_w': jax.random.normal(ks[4], (NUM_HEADS, WIDTH, HEAD_DIM), jnp.float32) / np.sqrt(WIDTH), 'kv_w': jax.random.normal(ks[5], (2, NUM_KV, WIDTH, HEAD_DIM), jnp.float32) / np.sqrt(WIDTH), 'out_w': jax.random.normal(ks[6], (NUM_HEADS, HEAD_DIM, WIDTH), jnp.float32) / np.sqrt(NUM_HEADS * HEAD_DIM)}
    _L1_xattn_all = _L1_xattn_setup()
    _L1_xattn_in = {k: v for k, v in _L1_xattn_all.items() if k in ('rms_scale', 'q_w', 'kv_w', 'out_w')}
    del _L1_xattn_all

    def _L1_ffn_setup():
        import jax, jax.numpy as jnp
        import numpy as np
        B, S, D = (2, 512, 256)
        H, E, P, K = (8, 8, 128, 2)
        SCALE = 1.0 / np.sqrt(P)

        def _get_sel_gate(x, w, route_scale):
            logits = jnp.einsum('bsd,ed->bse', x, w).astype(jnp.float32)
            raw = logits.reshape(x.shape[0], x.shape[1], H, E)
            probs = jax.nn.sigmoid(raw)
            vals, idx = jax.lax.top_k(probs, K)
            vals = vals / jnp.clip(vals.sum(-1, keepdims=True), 1e-09)
            vals = vals * route_scale
            gate = (jax.nn.one_hot(idx, E, dtype=vals.dtype) * vals[..., None]).sum(-2)
            return gate
        key = jax.random.key(seed)
        ks = jax.random.split(key, 8)
        std = 1.0 / np.sqrt(D)
        return {'x': jax.random.normal(ks[0], (B, S, D), jnp.float32), 'q_w': jax.random.normal(ks[1], (H * P, D), jnp.float32) * std, 'k_w': jax.random.normal(ks[2], (H * P, D), jnp.float32) * std, 'v_w': jax.random.normal(ks[3], (H * E, D, P), jnp.float32) * std, 'o_w': jax.random.normal(ks[4], (H * E, P, D), jnp.float32) * (1.0 / np.sqrt(H * P)), 'sel_v_w': jax.random.normal(ks[5], (H * E, D), jnp.float32) * std, 'sel_o_w': jax.random.normal(ks[6], (H * E, D), jnp.float32) * std, 'route_scale': jnp.ones((1,), jnp.float32)}
    _L1_ffn_all = _L1_ffn_setup()
    _L1_ffn_in = {k: v for k, v in _L1_ffn_all.items() if k in ('q_w', 'k_w', 'v_w', 'o_w', 'sel_v_w', 'sel_o_w', 'route_scale')}
    del _L1_ffn_all

    def _L2_xattn_setup():
        import jax, jax.numpy as jnp
        import numpy as np
        D_MODEL = 256
        FFN = 1024
        E = 8
        K = 2
        B, S = (4, 128)
        key = jax.random.key(seed)
        ks = jax.random.split(key, 8)
        scale_in = 1.0 / np.sqrt(D_MODEL)
        scale_ffn = 1.0 / np.sqrt(FFN)
        return {'x': jax.random.normal(ks[0], (B, S, D_MODEL), jnp.float32), 'context': jax.random.normal(ks[1], (B, S, D_MODEL), jnp.float32), 'Wg': jax.random.normal(ks[2], (D_MODEL, E), jnp.float32) * scale_in, 'bg': jnp.zeros((E,), jnp.float32), 'W1': jax.random.normal(ks[3], (E, D_MODEL, FFN), jnp.float32) * scale_in, 'b1': jnp.zeros((E, FFN), jnp.float32), 'W2': jax.random.normal(ks[4], (E, FFN, D_MODEL), jnp.float32) * scale_ffn, 'b2': jnp.zeros((E, D_MODEL), jnp.float32)}
    _L2_xattn_all = _L2_xattn_setup()
    _L2_xattn_in = {k: v for k, v in _L2_xattn_all.items() if k in ('Wg', 'bg', 'W1', 'b1', 'W2', 'b2')}
    del _L2_xattn_all

    def _L2_ffn_setup():
        import jax, jax.numpy as jnp
        import numpy as np
        LN_EPS = 1e-05

        def entmax15(z):
            z = z / 2.0
            z = z - jnp.max(z, axis=-1, keepdims=True)
            zs = -jnp.sort(-z, axis=-1)
            k = jnp.arange(1, z.shape[-1] + 1, dtype=z.dtype)
            mean = jnp.cumsum(zs, axis=-1) / k
            meansq = jnp.cumsum(zs * zs, axis=-1) / k
            ss = k * (meansq - jnp.square(mean))
            delta = (1.0 - ss) / k
            tau = mean - jnp.sqrt(jnp.clip(delta, 0.0))
            support = jnp.sum((tau <= zs).astype(jnp.int32), axis=-1, keepdims=True)
            tau_star = jnp.take_along_axis(tau, support - 1, axis=-1)
            return jnp.square(jnp.clip(z - tau_star, 0.0))

        def layernorm_noaffine(v):
            m = jnp.mean(v, axis=-1, keepdims=True)
            var = jnp.mean(jnp.square(v - m), axis=-1, keepdims=True)
            return (v - m) / jnp.sqrt(var + LN_EPS)

        def cp_mumoe(x, gate, Win, Wout):
            ones = jnp.ones(x.shape[:-1] + (1,), x.dtype)
            xb = jnp.concatenate([x, ones], axis=-1)
            z = jnp.einsum('btd,dr->btr', xb, Win) * gate
            return jnp.einsum('btr,or->bto', z, Wout)
        key = jax.random.key(seed)
        ks = jax.random.split(key, 8)
        B, T, D, O, D2, E, R = (8, 512, 256, 1024, 256, 16, 128)
        s = lambda k, shape, scale: jax.random.normal(k, shape, jnp.float32) * scale
        return {'x': s(ks[0], (B, T, D), 1.0), 'proj': s(ks[1], (D, E), D ** (-0.5)), 'C1': s(ks[2], (E, R), E ** (-0.5)), 'Win1': s(ks[3], (D + 1, R), D ** (-0.5)), 'Wout1': s(ks[4], (O, R), R ** (-0.5)), 'C2': s(ks[5], (E, R), E ** (-0.5)), 'Win2': s(ks[6], (O + 1, R), O ** (-0.5)), 'Wout2': s(ks[7], (D2, R), R ** (-0.5))}
    _L2_ffn_all = _L2_ffn_setup()
    _L2_ffn_in = {k: v for k, v in _L2_ffn_all.items() if k in ('proj', 'C1', 'Win1', 'Wout1', 'C2', 'Win2', 'Wout2')}
    del _L2_ffn_all

    def _L3_xattn_setup():
        import jax, jax.numpy as jnp
        import numpy as np
        HEAD_DIM = 64
        D_MODEL = 256
        key = jax.random.key(seed)
        ks = jax.random.split(key, 6)
        B, S_NEW, S_CACHE, D = (4, 512, 1536, D_MODEL)
        w_scale = 1.0 / np.sqrt(D)
        return {'hidden_states': jax.random.normal(ks[0], (B, S_NEW, D), dtype=jnp.float32), 'cached_key': jax.random.normal(ks[1], (B, S_CACHE, D), dtype=jnp.float32), 'cached_value': jax.random.normal(ks[2], (B, S_CACHE, D), dtype=jnp.float32), 'Wq': jax.random.normal(ks[3], (D, D), dtype=jnp.float32) * w_scale, 'bq': jnp.zeros((D,), dtype=jnp.float32), 'Wk': jax.random.normal(ks[4], (D, D), dtype=jnp.float32) * w_scale, 'bk': jnp.zeros((D,), dtype=jnp.float32), 'Wv': jax.random.normal(ks[5], (D, D), dtype=jnp.float32) * w_scale, 'bv': jnp.zeros((D,), dtype=jnp.float32)}
    _L3_xattn_all = _L3_xattn_setup()
    _L3_xattn_in = {k: v for k, v in _L3_xattn_all.items() if k in ('Wq', 'bq', 'Wk', 'bk', 'Wv', 'bv')}
    del _L3_xattn_all

    def _L3_ffn_setup():
        import jax, jax.numpy as jnp
        import numpy as np
        TOP_K = 2

        def _mlp(x, w1, b1, w2, b2):
            h = jax.nn.gelu(jnp.einsum('bsd,di->bsi', x, w1) + b1)
            return jnp.einsum('bsi,id->bsd', h, w2) + b2
        key = jax.random.key(seed)
        ks = jax.random.split(key, 8)
        B, S, D, I, E = (2, 512, 256, 1024, 8)
        s_in = 1.0 / np.sqrt(D)
        s_mid = 1.0 / np.sqrt(I)
        return {'x': jax.random.normal(ks[0], (B, S, D), jnp.float32), 'gate_w': jax.random.normal(ks[1], (D, E), jnp.float32) * s_in, 'gate_b': jnp.zeros((E,), jnp.float32), 'sh_w1': jax.random.normal(ks[2], (D, I), jnp.float32) * s_in, 'sh_b1': jnp.zeros((I,), jnp.float32), 'sh_w2': jax.random.normal(ks[3], (I, D), jnp.float32) * s_mid, 'sh_b2': jnp.zeros((D,), jnp.float32), 'ew1': jax.random.normal(ks[4], (E, D, I), jnp.float32) * s_in, 'eb1': jnp.zeros((E, I), jnp.float32), 'ew2': jax.random.normal(ks[5], (E, I, D), jnp.float32) * s_mid, 'eb2': jnp.zeros((E, D), jnp.float32)}
    _L3_ffn_all = _L3_ffn_setup()
    _L3_ffn_in = {k: v for k, v in _L3_ffn_all.items() if k in ('gate_w', 'gate_b', 'sh_w1', 'sh_b1', 'sh_w2', 'sh_b2', 'ew1', 'eb1', 'ew2', 'eb2')}
    del _L3_ffn_all
    return {'x': x, 'ctx_1024': ctx_1024, 'mask_BxS2_bk0': mask_BxS2_bk0, 'L0_xattn_igate_w': _L0_xattn_in['igate_w'], 'L0_xattn_igate_b': _L0_xattn_in['igate_b'], 'L0_xattn_fgate_w': _L0_xattn_in['fgate_w'], 'L0_xattn_fgate_b': _L0_xattn_in['fgate_b'], 'L0_xattn_out_w': _L0_xattn_in['out_w'], 'L0_ffn_router_w': _L0_ffn_in['router_w'], 'L0_ffn_fc1_w': _L0_ffn_in['fc1_w'], 'L0_ffn_fc2_w': _L0_ffn_in['fc2_w'], 'L1_xattn_rms_scale': _L1_xattn_in['rms_scale'], 'L1_xattn_q_w': _L1_xattn_in['q_w'], 'L1_xattn_kv_w': _L1_xattn_in['kv_w'], 'L1_xattn_out_w': _L1_xattn_in['out_w'], 'L1_ffn_q_w': _L1_ffn_in['q_w'], 'L1_ffn_k_w': _L1_ffn_in['k_w'], 'L1_ffn_v_w': _L1_ffn_in['v_w'], 'L1_ffn_o_w': _L1_ffn_in['o_w'], 'L1_ffn_sel_v_w': _L1_ffn_in['sel_v_w'], 'L1_ffn_sel_o_w': _L1_ffn_in['sel_o_w'], 'L1_ffn_route_scale': _L1_ffn_in['route_scale'], 'L2_xattn_Wg': _L2_xattn_in['Wg'], 'L2_xattn_bg': _L2_xattn_in['bg'], 'L2_xattn_W1': _L2_xattn_in['W1'], 'L2_xattn_b1': _L2_xattn_in['b1'], 'L2_xattn_W2': _L2_xattn_in['W2'], 'L2_xattn_b2': _L2_xattn_in['b2'], 'L2_ffn_proj': _L2_ffn_in['proj'], 'L2_ffn_C1': _L2_ffn_in['C1'], 'L2_ffn_Win1': _L2_ffn_in['Win1'], 'L2_ffn_Wout1': _L2_ffn_in['Wout1'], 'L2_ffn_C2': _L2_ffn_in['C2'], 'L2_ffn_Win2': _L2_ffn_in['Win2'], 'L2_ffn_Wout2': _L2_ffn_in['Wout2'], 'L3_xattn_Wq': _L3_xattn_in['Wq'], 'L3_xattn_bq': _L3_xattn_in['bq'], 'L3_xattn_Wk': _L3_xattn_in['Wk'], 'L3_xattn_bk': _L3_xattn_in['bk'], 'L3_xattn_Wv': _L3_xattn_in['Wv'], 'L3_xattn_bv': _L3_xattn_in['bv'], 'L3_ffn_gate_w': _L3_ffn_in['gate_w'], 'L3_ffn_gate_b': _L3_ffn_in['gate_b'], 'L3_ffn_sh_w1': _L3_ffn_in['sh_w1'], 'L3_ffn_sh_b1': _L3_ffn_in['sh_b1'], 'L3_ffn_sh_w2': _L3_ffn_in['sh_w2'], 'L3_ffn_sh_b2': _L3_ffn_in['sh_b2'], 'L3_ffn_ew1': _L3_ffn_in['ew1'], 'L3_ffn_eb1': _L3_ffn_in['eb1'], 'L3_ffn_ew2': _L3_ffn_in['ew2'], 'L3_ffn_eb2': _L3_ffn_in['eb2']}

def reference(x, ctx_1024, mask_BxS2_bk0, L0_xattn_igate_w, L0_xattn_igate_b, L0_xattn_fgate_w, L0_xattn_fgate_b, L0_xattn_out_w, L0_ffn_router_w, L0_ffn_fc1_w, L0_ffn_fc2_w, L1_xattn_rms_scale, L1_xattn_q_w, L1_xattn_kv_w, L1_xattn_out_w, L1_ffn_q_w, L1_ffn_k_w, L1_ffn_v_w, L1_ffn_o_w, L1_ffn_sel_v_w, L1_ffn_sel_o_w, L1_ffn_route_scale, L2_xattn_Wg, L2_xattn_bg, L2_xattn_W1, L2_xattn_b1, L2_xattn_W2, L2_xattn_b2, L2_ffn_proj, L2_ffn_C1, L2_ffn_Win1, L2_ffn_Wout1, L2_ffn_C2, L2_ffn_Win2, L2_ffn_Wout2, L3_xattn_Wq, L3_xattn_bq, L3_xattn_Wk, L3_xattn_bk, L3_xattn_Wv, L3_xattn_bv, L3_ffn_gate_w, L3_ffn_gate_b, L3_ffn_sh_w1, L3_ffn_sh_b1, L3_ffn_sh_w2, L3_ffn_sh_b2, L3_ffn_ew1, L3_ffn_eb1, L3_ffn_ew2, L3_ffn_eb2):
    import jax
    import jax.numpy as jnp

    def _L0_xattn_ref(q, k, v, igate_w, igate_b, fgate_w, fgate_b, out_w):
        import jax, jax.numpy as jnp
        import numpy as np
        import math
        EPS = 1e-08
        LN_EPS = 1e-05
        B, S, E, NH = (2, 512, 256, 4)
        DH = E // NH

        def _mlstm_cell(q, k, v, igate_w, igate_b, fgate_w, fgate_b, out_w):
            Bq, Sq, Eq = q.shape
            if_in = jnp.concatenate([q, k, v], axis=-1)
            ig = jnp.einsum('bsf,hf->bsh', if_in, igate_w) + igate_b
            fg = jnp.einsum('bsf,hf->bsh', if_in, fgate_w) + fgate_b
            ig = jnp.transpose(ig, (0, 2, 1))[..., None]
            fg = jnp.transpose(fg, (0, 2, 1))[..., None]
            qh = q.reshape(Bq, Sq, NH, DH).transpose(0, 2, 1, 3)
            kh = k.reshape(Bq, Sq, NH, DH).transpose(0, 2, 1, 3)
            vh = v.reshape(Bq, Sq, NH, DH).transpose(0, 2, 1, 3)
            log_fg = jax.nn.log_sigmoid(fg)
            cs = jnp.cumsum(log_fg, axis=2)
            cs_shift = jnp.concatenate([jnp.zeros_like(cs[:, :, :1]), cs[:, :, :-1]], axis=2)
            logfg_mat = cs - jnp.swapaxes(cs_shift, -2, -1)
            ltr = jnp.tril(jnp.ones((Sq, Sq), dtype=bool))
            logfg_mat = jnp.where(ltr, logfg_mat, -jnp.inf)
            log_D = logfg_mat + jnp.swapaxes(ig, -2, -1)
            max_log_D = jnp.max(log_D, axis=-1, keepdims=True)
            D = jnp.exp(log_D - max_log_D)
            qk = jnp.einsum('bhsd,bhtd->bhst', qh, kh / math.sqrt(DH))
            C = qk * D
            sum_C_abs = jnp.abs(jnp.sum(C, axis=-1, keepdims=True))
            normaliser = jnp.maximum(sum_C_abs, jnp.exp(-max_log_D))
            C_norm = C / (normaliser + EPS)
            h = jnp.einsum('bhst,bhtd->bhsd', C_norm, vh)
            mean = jnp.mean(h, axis=-1, keepdims=True)
            var = jnp.mean((h - mean) ** 2, axis=-1, keepdims=True)
            h_norm = (h - mean) / jnp.sqrt(var + LN_EPS)
            scale = (1.0 + out_w).reshape(1, NH, 1, DH)
            h_norm = h_norm * scale
            return h_norm.transpose(0, 2, 1, 3).reshape(Bq, Sq, Eq)
        return _mlstm_cell(q, k, v, igate_w, igate_b, fgate_w, fgate_b, out_w)

    def _L0_ffn_ref(x, router_w, fc1_w, fc2_w):
        import jax, jax.numpy as jnp
        import numpy as np
        N_EXPERTS = 8
        TOP_K = 2
        N_EMBD = 256
        EXPERT_DIM = 512
        B, T, D = x.shape
        E = router_w.shape[0]
        x_flat = x.reshape(B * T, D)
        logits = x_flat @ router_w.T
        probs = jax.nn.softmax(logits, axis=-1)
        top_vals, top_idx = jax.lax.top_k(probs, TOP_K)
        top_vals = top_vals / jnp.sum(top_vals, axis=-1, keepdims=True)
        onehot = jax.nn.one_hot(top_idx, E, dtype=x.dtype)
        weights = jnp.einsum('nk,nke->ne', top_vals, onehot)
        out = jnp.zeros_like(x_flat)
        for e in range(E):
            h = jnp.square(jnp.maximum(x_flat @ fc1_w[e].T, 0.0))
            out = out + weights[:, e:e + 1] * (h @ fc2_w[e].T)
        return out.reshape(B, T, D)

    def _L1_xattn_ref(x, mem_seq, mem_mask, rms_scale, q_w, kv_w, out_w):
        import jax, jax.numpy as jnp
        import numpy as np
        NUM_HEADS, NUM_KV, HEAD_DIM, WIDTH = (4, 1, 64, 256)
        MASK_FILL = -2.3819763e+38

        def _apply_rope(x, positions, max_wavelength=10000.0):
            d = x.shape[-1]
            freq_exp = 2.0 / d * jnp.arange(d // 2, dtype=jnp.float32)
            timescale = max_wavelength ** freq_exp
            radians = positions[..., None].astype(jnp.float32) / timescale
            radians = radians[..., None, :]
            sin, cos = (jnp.sin(radians), jnp.cos(radians))
            x1, x2 = jnp.split(x, 2, axis=-1)
            out = jnp.concatenate([x1 * cos - x2 * sin, x2 * cos + x1 * sin], axis=-1)
            return out.astype(x.dtype)

        def _rmsnorm(x, scale):
            var = jnp.mean(jnp.square(x.astype(jnp.float32)), axis=-1, keepdims=True)
            normed = x * jax.lax.rsqrt(var + 1e-06)
            return (normed * (1 + scale)).astype(x.dtype)
        B, S, _ = mem_seq.shape
        T = x.shape[1]
        G = NUM_HEADS // NUM_KV
        xn = _rmsnorm(x, rms_scale)
        mn = _rmsnorm(mem_seq, rms_scale)
        q = jnp.einsum('BTD,NDH->BTNH', xn, q_w)
        kv = jnp.einsum('BSD,cKDH->cBSKH', mn, kv_w)
        k, v = (kv[0], kv[1])
        q_pos = jnp.broadcast_to(jnp.arange(S, T + S), (B, T))
        k_pos = jnp.broadcast_to(jnp.arange(S), (B, S))
        q = _apply_rope(q, q_pos) * HEAD_DIM ** (-0.5)
        k = _apply_rope(k, k_pos)
        q = q.reshape(B, T, NUM_KV, G, HEAD_DIM)
        logits = jnp.einsum('BTKGH,BSKH->BKGTS', q, k, preferred_element_type=jnp.float32)
        masked = jnp.where(mem_mask[:, None, None, None, :], logits, MASK_FILL)
        probs = jax.nn.softmax(masked, axis=-1).astype(x.dtype)
        enc = jnp.einsum('BKGTS,BSKH->BTKGH', probs, v).reshape(B, T, NUM_HEADS, HEAD_DIM)
        return jnp.einsum('BTNH,NHD->BTD', enc, out_w)

    def _L1_ffn_ref(x, q_w, k_w, v_w, o_w, sel_v_w, sel_o_w, route_scale):
        import jax, jax.numpy as jnp
        import numpy as np
        B, S, D = (2, 512, 256)
        H, E, P, K = (8, 8, 128, 2)
        SCALE = 1.0 / np.sqrt(P)

        def _get_sel_gate(x, w, route_scale):
            logits = jnp.einsum('bsd,ed->bse', x, w).astype(jnp.float32)
            raw = logits.reshape(x.shape[0], x.shape[1], H, E)
            probs = jax.nn.sigmoid(raw)
            vals, idx = jax.lax.top_k(probs, K)
            vals = vals / jnp.clip(vals.sum(-1, keepdims=True), 1e-09)
            vals = vals * route_scale
            gate = (jax.nn.one_hot(idx, E, dtype=vals.dtype) * vals[..., None]).sum(-2)
            return gate
        rs = route_scale[0]
        gate_v = _get_sel_gate(x, sel_v_w, rs)
        gate_o = _get_sel_gate(x, sel_o_w, rs)
        q = jnp.einsum('bsd,hpd->bhsp', x, q_w.reshape(H, P, D))
        k = jnp.einsum('bsd,hpd->bhsp', x, k_w.reshape(H, P, D))
        xv = jnp.einsum('bsd,hedp->bshep', x, v_w.reshape(H, E, D, P))
        v = jnp.einsum('bshep,bshe->bhsp', xv, gate_v)
        att = jax.nn.softmax(jnp.einsum('bhqp,bhkp->bhqk', q, k) * SCALE, axis=-1)
        ctx = jnp.einsum('bhqk,bhkp->bqhp', att, v)
        weighted = ctx[:, :, :, None, :] * gate_o[..., None]
        out = jnp.einsum('bshep,hepd->bsd', weighted, o_w.reshape(H, E, P, D))
        return out

    def _L2_xattn_ref(x, context, Wg, bg, W1, b1, W2, b2):
        import jax, jax.numpy as jnp
        import numpy as np
        D_MODEL = 256
        FFN = 1024
        E = 8
        K = 2
        B, S = (4, 128)
        logits = jnp.einsum('bsd,de->bse', context, Wg) + bg
        scores_topk, idx_topk = jax.lax.top_k(logits, K)
        weights = jax.nn.softmax(scores_topk, axis=-1)
        combine = jnp.sum(jax.nn.one_hot(idx_topk, E, dtype=weights.dtype) * weights[..., None], axis=-2)
        h = jax.nn.relu(jnp.einsum('bsd,edf->bsef', x, W1) + b1)
        y = jnp.einsum('bsef,efd->bsed', h, W2) + b2
        out = jnp.einsum('bsed,bse->bsd', y, combine)
        return out

    def _L2_ffn_ref(x, proj, C1, Win1, Wout1, C2, Win2, Wout2):
        import jax, jax.numpy as jnp
        import numpy as np
        LN_EPS = 1e-05

        def entmax15(z):
            z = z / 2.0
            z = z - jnp.max(z, axis=-1, keepdims=True)
            zs = -jnp.sort(-z, axis=-1)
            k = jnp.arange(1, z.shape[-1] + 1, dtype=z.dtype)
            mean = jnp.cumsum(zs, axis=-1) / k
            meansq = jnp.cumsum(zs * zs, axis=-1) / k
            ss = k * (meansq - jnp.square(mean))
            delta = (1.0 - ss) / k
            tau = mean - jnp.sqrt(jnp.clip(delta, 0.0))
            support = jnp.sum((tau <= zs).astype(jnp.int32), axis=-1, keepdims=True)
            tau_star = jnp.take_along_axis(tau, support - 1, axis=-1)
            return jnp.square(jnp.clip(z - tau_star, 0.0))

        def layernorm_noaffine(v):
            m = jnp.mean(v, axis=-1, keepdims=True)
            var = jnp.mean(jnp.square(v - m), axis=-1, keepdims=True)
            return (v - m) / jnp.sqrt(var + LN_EPS)

        def cp_mumoe(x, gate, Win, Wout):
            ones = jnp.ones(x.shape[:-1] + (1,), x.dtype)
            xb = jnp.concatenate([x, ones], axis=-1)
            z = jnp.einsum('btd,dr->btr', xb, Win) * gate
            return jnp.einsum('btr,or->bto', z, Wout)
        a = entmax15(layernorm_noaffine(jnp.einsum('btd,de->bte', x, proj)))
        g1 = jnp.einsum('bte,er->btr', a, C1)
        h = cp_mumoe(x, g1, Win1, Wout1)
        h = jax.nn.gelu(h, approximate=False)
        g2 = jnp.einsum('bte,er->btr', a, C2)
        return cp_mumoe(h, g2, Win2, Wout2)

    def _L3_xattn_ref(hidden_states, cached_key, cached_value, Wq, bq, Wk, bk, Wv, bv):
        import jax, jax.numpy as jnp
        import numpy as np
        HEAD_DIM = 64
        D_MODEL = 256
        q = jnp.einsum('bsd,ed->bse', hidden_states, Wq) + bq
        new_k = jnp.einsum('bsd,ed->bse', hidden_states, Wk) + bk
        new_v = jnp.einsum('bsd,ed->bse', hidden_states, Wv) + bv
        k = jnp.concatenate([cached_key, new_k], axis=1)
        v = jnp.concatenate([cached_value, new_v], axis=1)
        scale = 1.0 / jnp.sqrt(jnp.asarray(HEAD_DIM, dtype=q.dtype))
        scores = jnp.einsum('bqd,bkd->bqk', q, k) * scale
        probs = jax.nn.softmax(scores, axis=-1)
        out = jnp.einsum('bqk,bkd->bqd', probs, v)
        return out

    def _L3_ffn_ref(x, gate_w, gate_b, sh_w1, sh_b1, sh_w2, sh_b2, ew1, eb1, ew2, eb2):
        import jax, jax.numpy as jnp
        import numpy as np
        TOP_K = 2

        def _mlp(x, w1, b1, w2, b2):
            h = jax.nn.gelu(jnp.einsum('bsd,di->bsi', x, w1) + b1)
            return jnp.einsum('bsi,id->bsd', h, w2) + b2
        E = ew1.shape[0]
        router_probs = jax.nn.softmax(jnp.einsum('bsd,de->bse', x, gate_w) + gate_b, axis=-1)
        expert_values, expert_indices = jax.lax.top_k(router_probs, k=TOP_K)
        expert_values = expert_values / (jnp.sum(expert_values, axis=-1, keepdims=True) + 1e-09)
        h = jax.nn.gelu(jnp.einsum('bsd,edi->bsei', x, ew1) + eb1)
        all_outputs = jnp.einsum('bsei,eid->bsed', h, ew2) + eb2
        one_hot = jax.nn.one_hot(expert_indices, E, dtype=x.dtype)
        weights_E = (one_hot * expert_values[..., None]).sum(axis=2)
        moe_out = jnp.einsum('bse,bsed->bsd', weights_E, all_outputs)
        return x + _mlp(x, sh_w1, sh_b1, sh_w2, sh_b2) + moe_out
    x = x + _L0_xattn_ref(_layernorm(x, axis=-1), ctx_1024, ctx_1024, L0_xattn_igate_w, L0_xattn_igate_b, L0_xattn_fgate_w, L0_xattn_fgate_b, L0_xattn_out_w)
    x = x + _L0_ffn_ref(_layernorm(x, axis=-1), L0_ffn_router_w, L0_ffn_fc1_w, L0_ffn_fc2_w)
    x = x + _L1_xattn_ref(_layernorm(x, axis=-1), ctx_1024, mask_BxS2_bk0, L1_xattn_rms_scale, L1_xattn_q_w, L1_xattn_kv_w, L1_xattn_out_w)
    x = x + _L1_ffn_ref(_layernorm(x, axis=-1), L1_ffn_q_w, L1_ffn_k_w, L1_ffn_v_w, L1_ffn_o_w, L1_ffn_sel_v_w, L1_ffn_sel_o_w, L1_ffn_route_scale)
    x = x + _L2_xattn_ref(_layernorm(x, axis=-1), ctx_1024, L2_xattn_Wg, L2_xattn_bg, L2_xattn_W1, L2_xattn_b1, L2_xattn_W2, L2_xattn_b2)
    x = x + _L2_ffn_ref(_layernorm(x, axis=-1), L2_ffn_proj, L2_ffn_C1, L2_ffn_Win1, L2_ffn_Wout1, L2_ffn_C2, L2_ffn_Win2, L2_ffn_Wout2)
    x = x + _L3_xattn_ref(_layernorm(x, axis=-1), ctx_1024, ctx_1024, L3_xattn_Wq, L3_xattn_bq, L3_xattn_Wk, L3_xattn_bk, L3_xattn_Wv, L3_xattn_bv)
    x = x + _L3_ffn_ref(_layernorm(x, axis=-1), L3_ffn_gate_w, L3_ffn_gate_b, L3_ffn_sh_w1, L3_ffn_sh_b1, L3_ffn_sh_w2, L3_ffn_sh_b2, L3_ffn_ew1, L3_ffn_eb1, L3_ffn_ew2, L3_ffn_eb2)
    return x

_drawn_inputs = setup_inputs


def setup_inputs(seed=0):
    import zlib

    import numpy as np

    out = dict(_drawn_inputs(seed))
    spreads = {'L0_xattn_out_w': (0.0, 0.1),
     'L2_xattn_bg': (0.0, 0.1),
     'L2_xattn_b1': (0.0, 0.1),
     'L2_xattn_b2': (0.0, 0.1),
     'L3_xattn_bq': (0.0, 0.8),
     'L3_xattn_bk': (0.0, 2.0),
     'L3_xattn_bv': (0.0, 2.0),
     'L3_ffn_gate_b': (0.0, 0.8),
     'L3_ffn_sh_b1': (0.0, 2.0),
     'L3_ffn_sh_b2': (0.0, 2.0),
     'L3_ffn_eb1': (0.0, 2.0),
     'L3_ffn_eb2': (0.0, 2.0)}
    factors = {'L0_xattn_igate_b': 64.0,
     'L1_xattn_rms_scale': 3.619,
     'L2_ffn_proj': 4.488,
     'L2_ffn_C1': 4.352,
     'L2_ffn_Win1': 4.88,
     'L2_ffn_Wout1': 4.023,
     'L2_ffn_C2': 3.943,
     'L2_ffn_Win2': 4.369,
     'L2_ffn_Wout2': 4.404,
     'L3_xattn_Wq': 8.0,
     'L3_xattn_Wk': 8.0,
     'L3_xattn_Wv': 8.0,
     'L3_ffn_gate_w': 8.0,
     'L3_ffn_sh_w1': 8.0,
     'L3_ffn_sh_w2': 8.0,
     'L3_ffn_ew1': 8.0,
     'L3_ffn_ew2': 8.0}
    for name, (base, spread) in spreads.items():
        noise = np.random.default_rng([zlib.crc32(name.encode()), seed]).standard_normal(out[name].shape)
        drawn = base * np.exp(spread * noise) if base else spread * noise
        out[name] = jnp.asarray(drawn.astype(out[name].dtype))
    for name, factor in factors.items():
        out[name] = (out[name] * factor).astype(out[name].dtype)
    return out
```

```python
from contextlib import ExitStack

import concourse.bass as bass
from concourse import mybir

F32 = mybir.dt.float32
U8 = mybir.dt.uint8
ALU = mybir.AluOpType
ACT = mybir.ActivationFunctionType
AX = mybir.AxisListType

P = 128
T = 16
D = 256
DC = D // P
G = 4
NG = T // G
GT = G * P
BANK = 512
LN_EPS = 1e-5
RMS_EPS = 1e-6
LOWEST = -3.0e38
MASK_FILL = -2.3819763e38


class Counter:

    def __init__(self, sem, step=1):
        self.sem, self.step, self.value = sem, step, 0

    def after(self, instruction):
        instruction.then_inc(self.sem, self.step)
        self.value += self.step
        return (self, self.value)


class Ring:

    def __init__(self, n):
        self.n, self.turn, self.freed = n, 0, [()] * n

    def take(self):
        slot = self.turn % self.n
        self.turn += 1
        marks, self.freed[slot] = self.freed[slot], None
        assert marks is not None, "the buffer is still held"
        return slot, marks


class Machine:

    def __init__(self, nc, ctx):
        self.nc, self.ctx = nc, ctx
        self.pe, self.dve, self.act, self.pool, self.sp = nc.tensor, nc.vector, nc.scalar, nc.gpsimd, nc.sync
        self.seen = {}

    def sb(self, name, shape, dt=F32, ctx=None):
        return (ctx or self.ctx).enter_context(self.nc.sbuf_tensor(name, shape, dt))

    def counter(self, name, step=1):
        return Counter(self.ctx.enter_context(self.nc.semaphore(name)), step)

    def wait(self, engine, *marks):
        for counter, value in marks:
            key = (engine.engine, counter.sem.name)
            if self.seen.get(key, 0) < value:
                engine.wait_ge(counter.sem, value)
                self.seen[key] = value

    def layer(self, name):
        self.S_pe = self.counter(name + "_pe")
        self.S_dve = self.counter(name + "_dve")
        self.S_act = self.counter(name + "_act")
        self.S_pool = self.counter(name + "_pool")

    def V(self, instruction):
        return self.S_dve.after(instruction)

    def A(self, instruction):
        return self.S_act.after(instruction)

    def M(self, instruction):
        return self.S_pe.after(instruction)

    def Q(self, instruction):
        return self.S_pool.after(instruction)

    def VV(self, instruction):
        mark = self.V(instruction)
        self.wait(self.dve, mark)
        return mark


def bcast(ap, *shape):
    return ap.broadcast_to(list(shape))



def constants(m, ins):
    m.layer("const")
    pool, dve, sp = m.pool, m.dve, m.sp
    m.ident = m.sb("ident", [P, P])
    m.tri_incl = m.sb("tri_incl", [P, P])
    m.tri_excl = m.sb("tri_excl", [P, P])
    m.ones = m.sb("ones", [P, 1])
    m.minus_half = m.sb("minus_half", [P, T * 4])
    m.rank8 = m.sb("rank8", [P, 8])
    m.count16 = m.sb("count16", [P, 16])
    zero = dve.memset(m.ident[:, :], 0.0)
    dve.memset(m.tri_incl[:, :], 1.0)
    dve.memset(m.tri_excl[:, :], 1.0)
    dve.memset(m.ones[:, :], 1.0)
    for j in range(8):
        dve.memset(m.rank8[:, j:j + 1], float(8 - j))
    for j in range(16):
        dve.memset(m.count16[:, j:j + 1], float(j + 1))
    filled = m.V(dve.memset(m.minus_half[:, :], -0.5))
    m.wait(pool, filled)
    pool.affine_select(out=m.ident[:, :], in_=m.ident[:, :], compare_op=ALU.not_equal, fill=1.0,
                       base=0, pattern=[[-1, P]], channel_multiplier=1)
    pool.affine_select(out=m.tri_incl[:, :], in_=m.tri_incl[:, :], compare_op=ALU.is_ge, fill=0.0,
                       base=0, pattern=[[1, P]], channel_multiplier=-1)
    m.const_ready = m.Q(pool.affine_select(out=m.tri_excl[:, :], in_=m.tri_excl[:, :], compare_op=ALU.is_gt,
                                           fill=0.0, base=0, pattern=[[1, P]], channel_multiplier=-1))
    m.filled = filled
    S_in = m.counter("load_x", 16)
    S_ctx = m.counter("load_ctx", 16)
    S_small = m.counter("load_small", 16)
    m.X = m.sb("X", [P, T, D])
    m.CTX = m.sb("CTX", [P, T, D])
    m.x_ready = [S_in.after(sp.dma_start(m.X[:, :, :], ins["x"]))] * T
    m.ctx_ready = S_ctx.after(sp.dma_start(m.CTX[:, :, :], ins["ctx"]))
    m.small = {}
    for name, shape in SMALL:
        t = m.sb("w_" + name, [P] + list(shape))
        src = ins[name]
        if src.shape[0] == 1:
            src = src.partition_broadcast(P) if len(src.shape) == 1 else src[0].partition_broadcast(P)
        np_ = src.shape[0]
        m.small_ready = S_small.after(sp.dma_start(t[0:np_], src))
        m.small[name] = t


SMALL = [
    ("gate_w0", (6, 8)), ("gate_b0", (8,)), ("head_scale0", (D,)),
    ("router_w0", (DC, 8)),
    ("rms_scale", (D,)), ("q_w1", (DC, D)), ("kv_w1", (DC, P)), ("out_w1", (DC, D)),
    ("cos", (2, 32)), ("sin", (2, 32)),
    ("sel_w1", (DC, P)), ("route_scale", (1,)),
    ("router_w2", (DC, 8)), ("router_b2", (8,)), ("b1_2", (8, 8)), ("b2_2", (D,)),
    ("proj2", (DC, 16)), ("C1", (P,)), ("C2", (P,)), ("Win1", (DC, P)), ("win1_b", (1,)),
    ("Wout1", (8, P)), ("Win2", (8, P)), ("win2_b", (1,)), ("Wout2", (D,)),
    ("q_w3", (DC, D)), ("k_w3", (DC, D)), ("v_w3", (DC, D)), ("q_b3", (DC,)), ("k_b3", (DC,)), ("v_b3", (D,)),
    ("router_w3", (DC, 8)), ("router_b3", (8,)), ("b1_3", (9, 8)), ("b2_3", (D,)), ("sh_b2_3", (D,)),
]



def rsqrt(m, out, in_, eps, ready):
    n = out.shape[-1]
    e = m.VV(m.dve.tensor_scalar(out, in_, eps, None, ALU.add))
    m.wait(m.pool, e, m.filled)
    done = m.Q(m.pool.tensor_tensor(out, out, m.minus_half[:, 0:n], ALU.pow))
    m.wait(m.dve, done)
    return done


def transposed(m, dst, tiles, ready):
    last = None
    marks = []
    for c in range(DC):
        bank, free = m.banks.take()
        m.wait(m.pe, ready, m.const_ready, *free)
        for j in range(G):
            last = m.pe.transpose(m.psum[:, bank, j * P:(j + 1) * P], tiles[:, j, c * P:(c + 1) * P], m.ident[:, :])
        full = m.M(last)
        m.wait(m.act, full)
        last = m.A(m.act.activation(dst[:, c, :], m.psum[:, bank, :], ACT.Copy))
        m.banks.freed[bank] = (last,)
        marks.append(last)
    return marks[-1]


def layernorm(m, xt_free, add_back=False):
    dve = m.dve
    ready = []
    for g in range(NG):
        tiles = slice(g * G, (g + 1) * G)
        m.wait(dve, *m.x_ready[tiles])
        for j in range(G):
            st = dve.bn_stats(m.ln_stats[:, j, :], m.X[:, g * G + j, :])
        m.VV(st)
        for j in range(G):
            ag = dve.bn_aggr(m.ln_mv[:, j, :], m.ln_stats[:, j, :])
        m.VV(ag)
        rsqrt(m, m.ln_rstd[:, :], m.ln_mv[:, :, 1], LN_EPS, None)
        slot, free = m.ln_ring.take()
        m.wait(dve, *free)
        for j in range(G):
            done = m.V(dve.tensor_scalar(m.LN[:, slot, j, :], m.X[:, g * G + j, :], m.ln_mv[:, j, 0:1],
                                         m.ln_rstd[:, j:j + 1], ALU.subtract, ALU.mult))
        if add_back:
            m.wait(dve, done)
            added = m.V(dve.tensor_tensor(m.X[:, tiles, :], m.X[:, tiles, :], m.LN[:, slot], ALU.add))
            m.x_ready[g * G:(g + 1) * G] = [added] * G
        m.wait(m.act, *xt_free)
        end = transposed(m, m.XT[:, :, g * GT:(g + 1) * GT], m.LN[:, slot], done)
        m.ln_ring.freed[slot] = (end,)
        ready.append(end)
    return ready


def top2(m, probs, ready):
    dve = m.dve
    n = probs.shape[1]
    shape = [P, n, 8]
    m.wait(dve, ready, m.filled)
    rank = bcast(m.rank8[:, :].unsqueeze(1), *shape)
    key = m.top_key[:, 0:n, :]
    best = m.top_best[:, 0:n]
    for k in range(2):
        val, hot = m.top_v[:, k, 0:n], m.top_h[:, k, 0:n, :]
        m.VV(dve.tensor_reduce(val, probs, AX.X, ALU.max))
        m.VV(dve.tensor_tensor(key, probs, bcast(val.unsqueeze(2), *shape), ALU.is_equal))
        m.VV(dve.tensor_tensor(key, key, rank, ALU.mult))
        m.VV(dve.tensor_reduce(best, key, AX.X, ALU.max))
        m.VV(dve.tensor_tensor(hot, key, bcast(best.unsqueeze(2), *shape), ALU.is_equal))
        if k == 0:
            m.VV(dve.scalar_tensor_tensor(out=probs, in0=hot, scalar=LOWEST, in1=probs, op0=ALU.mult, op1=ALU.add))


def combine(m, out, n):
    dve = m.dve
    shape = [P, n, 8]
    m.VV(dve.tensor_tensor(m.top_key[:, 0:n, :], m.top_h[:, 0, 0:n, :], bcast(m.top_v[:, 0, 0:n].unsqueeze(2), *shape), ALU.mult))
    m.VV(dve.tensor_tensor(out, m.top_h[:, 1, 0:n, :], bcast(m.top_v[:, 1, 0:n].unsqueeze(2), *shape), ALU.mult))
    return m.VV(dve.tensor_tensor(out, out, m.top_key[:, 0:n, :], ALU.add))


def router_logits(m, act_fm, ready, w, n):
    bank, free = m.banks.take()
    m.wait(m.pe, m.small_ready, *free)
    for t in range(T):
        m.wait(m.pe, ready[t // G])
        for c in range(DC):
            mm = m.pe.matmul(m.psum[:, bank, t * n:(t + 1) * n], act_fm[:, c, t * P:(t + 1) * P], w[:, c, 0:n],
                             start=(c == 0), stop=(c == DC - 1))
    return bank, m.M(mm)


def softmax8(m, logits):
    dve = m.dve
    shape = [P, T, 8]
    m.VV(dve.tensor_reduce(m.top_best[:, 0:T], logits, AX.X, ALU.max))
    sub = m.V(dve.tensor_tensor(logits, logits, bcast(m.top_best[:, 0:T].unsqueeze(2), *shape), ALU.subtract))
    m.wait(m.act, sub)
    ex = m.A(m.act.activation(logits, logits, ACT.Exp))
    m.wait(dve, ex)
    m.VV(dve.tensor_reduce(m.top_best[:, 0:T], logits, AX.X, ALU.add))
    m.VV(dve.reciprocal(m.top_best[:, 0:T], m.top_best[:, 0:T]))
    return m.VV(dve.tensor_tensor(logits, logits, bcast(m.top_best[:, 0:T].unsqueeze(2), *shape), ALU.mult))


class Weights:

    def __init__(self, m, slots, size):
        self.m, self.size = m, size
        self.buf = m.sb("weights", [P, slots, size])
        self.ring = Ring(slots)
        self.counters = [m.counter(f"load_w{i}", 16) for i in range(slots)]

    def load(self, *sources):
        slot, free = self.ring.take()
        self.m.wait(self.m.sp, *free)
        at, views = 0, []
        for src in sources:
            n = src.shape[1]
            view = self.buf[:, slot, at:at + n]
            mark = self.counters[slot].after(self.m.sp.dma_start(view, src))
            views.append(view)
            at += n
        assert at <= self.size
        return slot, views, mark



def experts(m, xt_ready, F, sources, gates, gates_ready, hidden):
    FC = F // P
    steps = [(e, g) for e in range(len(sources)) for g in range(NG)]
    loaded = {}

    def up(e, g):
        if g == 0:
            slot, (w1, w2), mark = m.W.load(*sources[e])
            loaded[e] = (slot, w1.rearrange("p (c f) -> p c f", c=DC), w2.rearrange("p (c d) -> p c d", c=FC), mark)
        slot, w1, w2, mark = loaded[e]
        h_slot, h_free = m.h_ring.take()
        m.wait(m.pe, mark, xt_ready[g])
        m.wait(m.act, *h_free)
        marks = []
        for f in range(FC):
            bank, free = m.banks.take()
            m.wait(m.pe, *free)
            for c in range(DC):
                mm = m.pe.matmul(m.psum[:, bank, :], w1[:, c, f * P:(f + 1) * P], m.XT[:, c, g * GT:(g + 1) * GT],
                                 start=(c == 0), stop=(c == DC - 1))
            m.wait(m.act, m.M(mm))
            freed, done = hidden(m.psum[:, bank, :], m.H[:, h_slot, f, :], e, f)
            m.banks.freed[bank] = (freed,)
            marks.append(done)
        return h_slot, marks

    def down(e, g, h_slot, h_marks):
        slot, w1, w2, mark = loaded[e]
        for half in range(G // 2):
            bank, free = m.banks.take()
            m.wait(m.pe, *free)
            for j in range(2):
                t = g * G + half * 2 + j
                for f in range(FC):
                    m.wait(m.pe, h_marks[f])
                    tok = slice((half * 2 + j) * P, (half * 2 + j + 1) * P)
                    mm = m.pe.matmul(m.psum[:, bank, j * D:(j + 1) * D], m.H[:, h_slot, f, tok], w2[:, f, :],
                                     start=(f == 0), stop=(f == FC - 1))
            full = m.M(mm)
            m.wait(m.dve, full, gates_ready)
            for j in range(2):
                t = g * G + half * 2 + j
                m.wait(m.dve, m.x_ready[t])
                gate = gates(t, e)
                src = m.psum[:, bank, j * D:(j + 1) * D]
                if gate is None:
                    added = m.V(m.dve.tensor_tensor(m.X[:, t, :], src, m.X[:, t, :], ALU.add))
                else:
                    added = m.V(m.dve.scalar_tensor_tensor(out=m.X[:, t, :], in0=src, scalar=gate, in1=m.X[:, t, :],
                                                           op0=ALU.mult, op1=ALU.add))
                m.x_ready[t] = added
            m.banks.freed[bank] = (added,)
        m.h_ring.freed[h_slot] = (full,)
        if g == NG - 1:
            m.W.ring.freed[slot] = (full,)
        return full

    pending = None
    for e, g in steps:
        now = (e, g) + up(e, g)
        if pending:
            down(*pending)
        pending = now
    return down(*pending)


def layer0_ffn(m, ins):
    m.layer("ffn0")
    xt = layernorm(m, m.xt_free)
    bank, logits = router_logits(m, m.XT, xt, m.small["router_w0"], 8)
    m.wait(m.dve, logits)
    probs = m.route[:, :, :]
    copied = m.VV(m.dve.tensor_copy(probs, m.psum[:, bank, 0:T * 8].rearrange("p (t e) -> p t e", t=T)))
    m.banks.freed[bank] = (copied,)
    top2(m, probs, softmax8(m, probs))
    v = m.top_v
    m.VV(m.dve.tensor_tensor(m.top_best[:, 0:T], v[:, 0, 0:T], v[:, 1, 0:T], ALU.add))
    m.VV(m.dve.reciprocal(m.top_best[:, 0:T], m.top_best[:, 0:T]))
    m.VV(m.dve.tensor_tensor(v[:, :, 0:T], v[:, :, 0:T], bcast(m.top_best[:, 0:T].unsqueeze(1), P, 2, T), ALU.mult))
    gates_ready = combine(m, m.gates[:, :, :], T)

    def hidden(src, out, e, f):
        relu = m.A(m.act.activation(out, src, ACT.Relu))
        m.wait(m.pool, relu)
        return relu, m.Q(m.pool.tensor_tensor(out, out, out, ALU.mult))

    end = experts(m, xt, 512, [(ins["ffn0_w1"][e], ins["ffn0_w2"][e]) for e in range(8)],
                  lambda t, e: m.gates[:, t, e:e + 1], gates_ready, hidden)
    m.xt_free = (end,)


def gate_bias(m, b2, ready):
    for t in range(0, T, 2):
        bank, free = m.banks.take()
        m.wait(m.pe, ready, m.const_ready, *free)
        for j in range(2):
            mm = m.pe.transpose(m.psum[0:8, bank, j * P:(j + 1) * P], m.gates[:, t + j, :], m.ident[:, :])
        m.wait(m.dve, m.M(mm))
        gt = m.V(m.dve.tensor_copy(m.gates_fm[:, t * P:(t + 2) * P], m.psum[0:8, bank, 0:2 * P]))
        m.banks.freed[bank] = (gt,)
        bank, free = m.banks.take()
        m.wait(m.pe, gt, m.small_ready, *free)
        for j in range(2):
            mm = m.pe.matmul(m.psum[:, bank, j * D:(j + 1) * D], m.gates_fm[:, (t + j) * P:(t + j + 1) * P], b2[0:8, :],
                             start=True, stop=True)
        m.wait(m.dve, m.M(mm), m.x_ready[t], m.x_ready[t + 1])
        added = m.V(m.dve.tensor_tensor(m.X[:, t:t + 2, :], m.X[:, t:t + 2, :],
                                        m.psum[:, bank, :].rearrange("p (j d) -> p j d", j=2), ALU.add))
        m.banks.freed[bank] = (added,)
        m.x_ready[t:t + 2] = [added] * 2


def layer2_mix(m, ins):
    m.layer("mix2")
    bank, logits = router_logits(m, m.CTXT, m.ctxt_ready, m.small["router_w2"], 8)
    m.wait(m.dve, logits)
    lg = m.route[:, :, :]
    added = m.VV(m.dve.tensor_tensor(lg, m.psum[:, bank, 0:T * 8].rearrange("p (t e) -> p t e", t=T),
                                     bcast(m.small["router_b2"][:, :].unsqueeze(1), P, T, 8), ALU.add))
    m.banks.freed[bank] = (added,)
    xt = layernorm(m, m.xt_free)
    top2(m, lg, added)
    v = m.top_v
    m.VV(m.dve.tensor_tensor(v[:, 1, 0:T], v[:, 1, 0:T], v[:, 0, 0:T], ALU.subtract))
    m.wait(m.act, m.VV(m.dve.tensor_tensor(v[:, 0, 0:T], v[:, 0, 0:T], v[:, 0, 0:T], ALU.subtract)))
    m.wait(m.dve, m.A(m.act.activation(v[:, :, 0:T], v[:, :, 0:T], ACT.Exp)))
    m.VV(m.dve.tensor_tensor(m.top_best[:, 0:T], v[:, 0, 0:T], v[:, 1, 0:T], ALU.add))
    m.VV(m.dve.reciprocal(m.top_best[:, 0:T], m.top_best[:, 0:T]))
    m.VV(m.dve.tensor_tensor(v[:, :, 0:T], v[:, :, 0:T], bcast(m.top_best[:, 0:T].unsqueeze(1), P, 2, T), ALU.mult))
    gates_ready = combine(m, m.gates[:, :, :], T)
    gate_bias(m, m.small["b2_2"], gates_ready)

    def hidden(src, out, e, f):
        done = m.A(m.act.activation(out, src, ACT.Relu, bias=m.small["b1_2"][:, e, f:f + 1]))
        return done, done

    end = experts(m, xt, 1024, [(ins["mix2_w1"][e], ins["mix2_w2"][e]) for e in range(8)],
                  lambda t, e: m.gates[:, t, e:e + 1], gates_ready, hidden)
    m.xt_free = (end,)


def layer3_ffn(m, ins):
    m.layer("ffn3")
    xt = layernorm(m, m.xt_free, add_back=True)
    bank, logits = router_logits(m, m.XT, xt, m.small["router_w3"], 8)
    m.wait(m.dve, logits)
    probs = m.route[:, :, :]
    added = m.VV(m.dve.tensor_tensor(probs, m.psum[:, bank, 0:T * 8].rearrange("p (t e) -> p t e", t=T),
                                     bcast(m.small["router_b3"][:, :].unsqueeze(1), P, T, 8), ALU.add))
    m.banks.freed[bank] = (added,)
    top2(m, probs, softmax8(m, probs))
    v = m.top_v
    m.VV(m.dve.tensor_tensor(m.top_best[:, 0:T], v[:, 0, 0:T], v[:, 1, 0:T], ALU.add))
    m.VV(m.dve.tensor_scalar(m.top_best[:, 0:T], m.top_best[:, 0:T], 1e-9, None, ALU.add))
    m.VV(m.dve.reciprocal(m.top_best[:, 0:T], m.top_best[:, 0:T]))
    m.VV(m.dve.tensor_tensor(v[:, :, 0:T], v[:, :, 0:T], bcast(m.top_best[:, 0:T].unsqueeze(1), P, 2, T), ALU.mult))
    gates_ready = combine(m, m.gates[:, :, :], T)
    gate_bias(m, m.small["b2_3"], gates_ready)
    for t in range(T):
        m.wait(m.dve, m.x_ready[t])
        m.x_ready[t] = m.V(m.dve.tensor_tensor(m.X[:, t, :], m.X[:, t, :], m.small["sh_b2_3"][:, :], ALU.add))

    def hidden(src, out, e, f):
        done = m.A(m.act.activation(out, src, ACT.Gelu_apprx_tanh, bias=m.small["b1_3"][:, e, f:f + 1]))
        return done, done

    end = experts(m, xt, 1024, [(ins["ffn3_w1"][e], ins["ffn3_w2"][e]) for e in range(9)],
                  lambda t, e: None if e == 0 else m.gates[:, t, e - 1:e], gates_ready, hidden)
    m.xt_free = (end,)



def layer0_mix(m, ins):
    NH, DH, HB = 4, 64, T * 4
    m.layer("mix0")
    pe, dve, act, pool = m.pe, m.dve, m.act, m.pool
    with ExitStack() as scratch:
        def sb(name, shape):
            return m.sb(name, shape, F32, scratch)
        gf = sb("gate_pre", [P, T, 8])
        fneg, fexp, lf, a, cs = (sb(n, [P, T, NH]) for n in ("f_neg", "f_exp", "log_f", "a_col", "cs_col"))
        floor = sb("norm_floor", [P, T, NH])
        PAD = 64
        scan = [sb(f"scan{i}", [HB, PAD + P]) for i in range(2)]
        dist = sb("dist", [P, 2, NH, P])
        E = sb("decay", [P, 2, NH, P])
        C = sb("weights_t", [P, 2, NH, P])
        sums, nrm = sb("c_sum", [P, 2, NH]), sb("normaliser", [P, 2, NH])
        h = sb("h_tile", [P, 2, NH, DH])
        hst, hmv, hr = sb("h_stats", [P, 2, NH, 6]), sb("h_mv", [P, 2, NH, 2]), sb("h_rstd", [P, 2, NH])
        scale1 = sb("out_scale", [P, D])

        m.ctxt_ready = []
        for g in range(NG):
            m.ctxt_ready.append(transposed(m, m.CTXT[:, :, g * GT:(g + 1) * GT], m.CTX[:, g * G:(g + 1) * G, :], m.ctx_ready))
        xt = layernorm(m, m.xt_free)

        bank, free = m.banks.take()
        m.wait(pe, m.small_ready, *free)
        for t in range(T):
            m.wait(pe, xt[t // G], m.ctxt_ready[t // G])
            for c in range(6):
                src = m.XT if c < 2 else m.CTXT
                mm = pe.matmul(m.psum[:, bank, t * 8:(t + 1) * 8], src[:, c % 2, t * P:(t + 1) * P],
                               m.small["gate_w0"][:, c, :], start=(c == 0), stop=(c == 5))
        m.wait(dve, m.M(mm), m.small_ready)
        m.VV(dve.tensor_scalar(scale1[:, :], m.small["head_scale0"][:, :], 1.0, None, ALU.add))
        added = m.VV(dve.tensor_tensor(gf[:, :, :], m.psum[:, bank, 0:T * 8].rearrange("p (t e) -> p t e", t=T),
                                       bcast(m.small["gate_b0"][:, :].unsqueeze(1), P, T, 8), ALU.add))
        m.banks.freed[bank] = (added,)
        f = gf[:, :, NH:2 * NH]
        neg = m.V(dve.scalar_tensor_tensor(out=fneg[:, :, :], in0=f, scalar=-1.0, in1=f, op0=ALU.mult, op1=ALU.min))
        m.wait(act, neg)
        m.wait(act, m.A(act.activation(fexp[:, :, :], fneg[:, :, :], ACT.Exp)))
        log = m.A(act.activation(fexp[:, :, :], fexp[:, :, :], ACT.Ln, bias=1.0))
        m.wait(dve, log)
        lfr = m.V(dve.scalar_tensor_tensor(out=lf[:, :, :], in0=f, scalar=0.0, in1=fexp[:, :, :], op0=ALU.min, op1=ALU.subtract))
        bank, free = m.banks.take()
        m.wait(pe, lfr, m.const_ready, *free)
        flat = lf[:, :, :].rearrange("p t h -> p (t h)")
        pe.matmul(m.psum[:, bank, 0:HB], m.tri_incl[:, :], flat, start=True, stop=True)
        m.wait(dve, m.M(pe.matmul(m.psum[:, bank, HB:2 * HB], m.tri_excl[:, :], flat, start=True, stop=True)))
        dve.tensor_copy(cs[:, :, :], m.psum[:, bank, 0:HB].rearrange("p (t h) -> p t h", t=T))
        ar = m.VV(dve.tensor_tensor(a[:, :, :], gf[:, :, 0:NH],
                                    m.psum[:, bank, HB:2 * HB].rearrange("p (t h) -> p t h", t=T), ALU.subtract))
        m.banks.freed[bank] = (ar,)
        bank, free = m.banks.take()
        m.wait(pe, ar, *free)
        tr = m.M(pe.transpose(m.psum[0:HB, bank, 0:P], a[:, :, :].rearrange("p t h -> p (t h)"), m.ident[:, :]))
        dve.memset(scan[0][:, 0:PAD], LOWEST)
        dve.memset(scan[1][:, 0:PAD], LOWEST)
        m.wait(dve, tr)
        got = m.VV(dve.tensor_copy(scan[0][:, PAD:], m.psum[0:HB, bank, 0:P]))
        m.banks.freed[bank] = (got,)
        for k in range(7):
            x, y, s = scan[k % 2], scan[1 - k % 2], 1 << k
            got = m.VV(dve.tensor_tensor(y[:, PAD:], x[:, PAD:], x[:, PAD - s:PAD - s + P], ALU.max))
        top = scan[7 % 2][:, PAD:]
        bank, free = m.banks.take()
        m.wait(pe, got, *free)
        tr = m.M(pe.transpose(m.psum[:, bank, 0:HB], top, m.ident[0:HB, 0:HB]))
        m.wait(dve, tr)
        fl = m.V(dve.tensor_tensor(floor[:, :, :], cs[:, :, :], m.psum[:, bank, 0:HB].rearrange("p (t h) -> p t h", t=T), ALU.add))
        m.banks.freed[bank] = (fl,)
        m.wait(act, fl)
        floor_ready = m.A(act.activation(floor[:, :, :], floor[:, :, :], ACT.Exp, scale=-1.0))

        tail = ((), ())
        for b in range(T):
            i = b % 2
            tok = slice(b * P, (b + 1) * P)
            bm, free = m.banks.take()
            m.wait(pe, got, *free)
            for hd in range(NH):
                r = b * NH + hd
                mm = pe.matmul(m.psum[:, bm, hd * P:(hd + 1) * P], bcast(m.ident[0:HB, r:r + 1], HB, P), top, start=True, stop=True)
            max_full = m.M(mm)
            qk = []
            for lo in range(2):
                bq, free = m.banks.take()
                m.wait(pe, *free)
                for c in range(DC):
                    part = slice(lo * DH, (lo + 1) * DH)
                    mm = pe.matmul(m.psum[:, bq, c * P:(c + 1) * P], m.CTXT[part, c, tok], m.XT[part, c, tok], start=True, stop=True)
                qk.append((bq, m.M(mm)))
            m.wait(dve, max_full)
            for hd in range(NH):
                far = m.V(dve.tensor_scalar(dist[:, i, hd, :], m.psum[:, bm, hd * P:(hd + 1) * P], a[:, b, hd:hd + 1], 0.0,
                                            ALU.subtract, ALU.max))
            m.banks.freed[bm] = (far,)
            m.wait(act, far, *tail[i])
            ex = m.A(act.activation(E[:, i], dist[:, i], ACT.Exp, scale=-1.0))
            m.wait(pool, ex)
            cut = m.Q(pool.affine_select(out=E[:, i], in_=E[:, i], compare_op=ALU.is_ge, fill=0.0,
                                         base=0, pattern=[[0, NH], [1, P]], channel_multiplier=-1))
            m.wait(dve, cut)
            for lo, (bq, full) in enumerate(qk):
                m.wait(dve, full)
                c_ready = m.V(dve.scalar_tensor_tensor(
                    out=C[:, i, lo::2, :], in0=m.psum[:, bq, 0:2 * P].rearrange("p (c s) -> p c s", c=DC),
                    scalar=DH ** -0.5, in1=E[:, i, lo::2, :], op0=ALU.mult, op1=ALU.mult))
                m.banks.freed[bq] = (c_ready,)
            bo, free = m.banks.take()
            m.wait(pe, c_ready, *free)
            for hd in range(NH):
                pe.matmul(m.psum[:, bo, hd * DH:(hd + 1) * DH], C[:, i, hd, :], m.CTX[:, b, hd * DH:(hd + 1) * DH], start=True, stop=True)
                mm = pe.matmul(m.psum[:, bo, D + hd:D + hd + 1], C[:, i, hd, :], m.ones[:, :], start=True, stop=True)
            c_used = m.M(mm)
            tail = (tail[0], (c_used,)) if i else ((c_used,), tail[1])
            m.wait(dve, c_used, floor_ready)
            m.VV(dve.tensor_copy(sums[:, i], m.psum[:, bo, D:D + NH]))
            m.VV(dve.scalar_tensor_tensor(out=nrm[:, i], in0=sums[:, i], scalar=-1.0, in1=sums[:, i], op0=ALU.mult, op1=ALU.max))
            m.VV(dve.tensor_tensor(nrm[:, i], nrm[:, i], floor[:, b, :], ALU.max))
            m.VV(dve.tensor_scalar(nrm[:, i], nrm[:, i], 1e-8, None, ALU.add))
            m.VV(dve.reciprocal(nrm[:, i], nrm[:, i]))
            hv = m.VV(dve.tensor_tensor(h[:, i], m.psum[:, bo, 0:D].rearrange("p (h d) -> p h d", h=NH),
                                        bcast(nrm[:, i].unsqueeze(2), P, NH, DH), ALU.mult))
            m.banks.freed[bo] = (hv,)
            for hd in range(NH):
                st = dve.bn_stats(hst[:, i, hd, :], h[:, i, hd, :])
            m.VV(st)
            for hd in range(NH):
                ag = dve.bn_aggr(hmv[:, i, hd, :], hst[:, i, hd, :])
            m.VV(ag)
            rsqrt(m, hr[:, i, :], hmv[:, i, :, 1], LN_EPS, None)
            for hd in range(NH):
                nm = dve.tensor_scalar(h[:, i, hd, :], h[:, i, hd, :], hmv[:, i, hd, 0:1], hr[:, i, hd:hd + 1], ALU.subtract, ALU.mult)
            m.VV(nm)
            hf = h[:, i].rearrange("p h d -> p (h d)")
            m.VV(dve.tensor_tensor(hf, hf, scale1[:, :], ALU.mult))
            m.x_ready[b] = m.V(dve.tensor_tensor(m.X[:, b, :], m.X[:, b, :], hf, ALU.add))
        m.xt_free = (c_used,)
        m.barrier()



def layer1_mix(m, ins):
    NH, DH = 4, 64
    HALF = DH // 2
    m.layer("mix1")
    pe, dve, act, pool = m.pe, m.dve, m.act, m.pool
    with ExitStack() as scratch:
        def sb(name, shape, dt=F32):
            return m.sb(name, shape, dt, scratch)
        S_mask = m.counter("load_mask", 16)
        mask8 = sb("mask8", [P, T * P], U8)
        keep = sb("keep", [P, T * P])
        fill = sb("fill", [P, T * P])
        scale1 = sb("rms_scale1", [P, D])
        sq = sb("sq", [P, D])
        ms = sb("mean_sq", [P, 2, T])
        rx = sb("rms_r", [P, 2, T])
        xn = sb("xn", [P, 2, 2, D])
        xnT = sb("xnT", [P, 2, 2, DC, P])
        q = sb("q_tok", [P, 2, NH + 2, DH])
        qr = sb("q_rot", [P, 2, NH + 2, DH])
        rot = sb("rot", [P, 2, NH + 2, HALF])
        v = sb("v_tok", [P, 2, DH])
        qT = sb("q_t", [P, 2, 3, P])
        L = sb("logits", [P, 2, NH, P])
        mx, sm = sb("row_max", [P, 2, NH]), sb("row_sum", [P, 2, NH])
        pT = sb("probs_t", [P, 2, NH, P])
        enc = sb("enc", [P, 2, D])
        encT = sb("enc_t", [P, 2, DC, P])

        mask_ready = S_mask.after(m.sp.dma_start(mask8[:, :], ins["mask"][0].partition_broadcast(P)))
        m.wait(dve, mask_ready)
        m.VV(dve.tensor_copy(keep[:, :], mask8[:, :]))
        m.VV(dve.tensor_scalar(fill[:, :], keep[:, :], -1.0, -MASK_FILL, ALU.add, ALU.mult))
        m.wait(dve, m.small_ready)
        m.VV(dve.tensor_scalar(scale1[:, :], m.small["rms_scale"][:, :], 1.0, None, ALU.add))
        st, mv, rs = sb("l_st", [P, T, 6]), sb("l_mv", [P, T, 2]), sb("l_rs", [P, T])
        for t in range(T):
            m.wait(dve, m.x_ready[t])
            s_ = dve.bn_stats(st[:, t, :], m.X[:, t, :])
        m.VV(s_)
        for t in range(T):
            ag = dve.bn_aggr(mv[:, t, :], st[:, t, :])
        m.VV(ag)
        rsqrt(m, rs[:, :], mv[:, :, 1], LN_EPS, None)
        free_q, free_sq = [(), ()], ()
        for b in range(T):
            i = b % 2
            m.wait(dve, m.ctx_ready, *free_q[i])
            m.VV(dve.tensor_scalar(xn[:, i, 0, :], m.X[:, b, :], mv[:, b, 0:1], rs[:, b:b + 1], ALU.subtract, ALU.mult))
            for k, src in enumerate((xn[:, i, 0, :], m.CTX[:, b, :])):
                m.VV(dve.tensor_tensor(sq[:, :], src, src, ALU.mult))
                m.VV(dve.tensor_reduce(ms[:, k, b:b + 1], sq[:, :], AX.X, ALU.add))
                m.VV(dve.tensor_scalar(ms[:, k, b:b + 1], ms[:, k, b:b + 1], 1.0 / D, RMS_EPS, ALU.mult, ALU.add))
            pw = m.S_dve.value
            m.wait(pool, (m.S_dve, pw), m.filled)
            m.wait(dve, m.Q(pool.tensor_tensor(rx[:, :, b], ms[:, :, b], m.minus_half[:, 0:2], ALU.pow)))
            for k, src in enumerate((xn[:, i, 0, :], m.CTX[:, b, :])):
                nx = m.VV(dve.scalar_tensor_tensor(out=xn[:, i, k, :], in0=src, scalar=rx[:, k, b:b + 1], in1=scale1[:, :],
                                                   op0=ALU.mult, op1=ALU.mult))
            bank, free = m.banks.take()
            m.wait(pe, nx, m.const_ready, *free)
            for k in range(2):
                for c in range(DC):
                    mm = pe.transpose(m.psum[:, bank, (k * DC + c) * P:(k * DC + c + 1) * P], xn[:, i, k, c * P:(c + 1) * P], m.ident[:, :])
            m.wait(act, m.M(mm))
            xt = m.A(act.activation(xnT[:, i].rearrange("p k c s -> p (k c s)"), m.psum[:, bank, :], ACT.Copy))
            m.banks.freed[bank] = (xt,)
            bank, free = m.banks.take()
            m.wait(pe, xt, m.small_ready, *free)
            for c in range(DC):
                pe.matmul(m.psum[:, bank, 0:D], xnT[:, i, 0, c, :], m.small["q_w1"][:, c, :], start=(c == 0), stop=(c == DC - 1))
            for c in range(DC):
                mm = pe.matmul(m.psum[:, bank, D:D + P], xnT[:, i, 1, c, :], m.small["kv_w1"][:, c, :], start=(c == 0), stop=(c == DC - 1))
            m.wait(dve, m.M(mm))
            dve.tensor_scalar(q[:, i, 0:NH, :], m.psum[:, bank, 0:D].rearrange("p (h d) -> p h d", h=NH), DH ** -0.5, None, ALU.mult)
            dve.tensor_copy(q[:, i, NH:NH + 2, :], bcast(m.psum[:, bank, D:D + DH].unsqueeze(1), P, 2, DH))
            vr = m.VV(dve.tensor_copy(v[:, i, :], m.psum[:, bank, D + DH:D + P]))
            m.banks.freed[bank] = (vr,)
            for hs, pos in ((slice(0, NH), 1), (slice(NH, NH + 2), 0)):
                n = hs.stop - hs.start
                cosb = bcast(m.small["cos"][:, pos, :].unsqueeze(1), P, n, HALF)
                sinb = bcast(m.small["sin"][:, pos, :].unsqueeze(1), P, n, HALF)
                x1, x2 = q[:, i, hs, 0:HALF], q[:, i, hs, HALF:DH]
                o1, o2, r = qr[:, i, hs, 0:HALF], qr[:, i, hs, HALF:DH], rot[:, i, hs, :]
                dve.tensor_tensor(o1, x1, cosb, ALU.mult)
                m.VV(dve.tensor_tensor(r, x2, sinb, ALU.mult))
                m.VV(dve.tensor_tensor(o1, o1, r, ALU.subtract))
                dve.tensor_tensor(o2, x2, cosb, ALU.mult)
                m.VV(dve.tensor_tensor(r, x1, sinb, ALU.mult))
                qr_ready = m.VV(dve.tensor_tensor(o2, o2, r, ALU.add))
            bank, free = m.banks.take()
            m.wait(pe, qr_ready, *free)
            flat = qr[:, i].rearrange("p h d -> p (h d)")
            for c in range(3):
                mm = pe.transpose(m.psum[:, bank, c * P:(c + 1) * P], flat[:, c * P:(c + 1) * P], m.ident[:, :])
            m.wait(act, m.M(mm))
            qt = m.A(act.activation(qT[:, i].rearrange("p c s -> p (c s)"), m.psum[:, bank, 0:3 * P], ACT.Copy))
            m.banks.freed[bank] = (qt,)
            tok = slice(b * P, (b + 1) * P)
            for lo in range(2):
                bank, free = m.banks.take()
                m.wait(pe, qt, *free)
                part = slice(lo * DH, (lo + 1) * DH)
                for c in range(DC):
                    mm = pe.matmul(m.psum[:, bank, c * P:(c + 1) * P], qT[part, i, c, :], qT[part, i, 2, :], start=True, stop=True)
                m.wait(dve, m.M(mm))
                lg = m.VV(dve.tensor_tensor(L[:, i, lo::2, :], m.psum[:, bank, 0:2 * P].rearrange("p (c s) -> p c s", c=DC),
                                            bcast(keep[:, tok].unsqueeze(1), P, 2, P), ALU.mult))
                m.banks.freed[bank] = (lg,)
            m.VV(dve.tensor_tensor(L[:, i], L[:, i], bcast(fill[:, tok].unsqueeze(1), P, NH, P), ALU.add))
            m.VV(dve.tensor_reduce(mx[:, i], L[:, i], AX.X, ALU.max))
            sub = m.V(dve.tensor_tensor(L[:, i], L[:, i], bcast(mx[:, i].unsqueeze(2), P, NH, P), ALU.subtract))
            m.wait(act, sub)
            m.wait(dve, m.A(act.activation(L[:, i], L[:, i], ACT.Exp)))
            m.VV(dve.tensor_reduce(sm[:, i], L[:, i], AX.X, ALU.add))
            m.VV(dve.reciprocal(sm[:, i], sm[:, i]))
            bank, free = m.banks.take()
            m.wait(pe, (m.S_act, m.S_act.value), *free)
            for hd in range(NH):
                mm = pe.transpose(m.psum[:, bank, hd * P:(hd + 1) * P], L[:, i, hd, :], m.ident[:, :])
            m.wait(act, m.M(mm))
            pt = m.A(act.activation(pT[:, i].rearrange("p h s -> p (h s)"), m.psum[:, bank, :], ACT.Copy))
            m.banks.freed[bank] = (pt,)
            bank, free = m.banks.take()
            m.wait(pe, pt, vr, *free)
            for hd in range(NH):
                mm = pe.matmul(m.psum[:, bank, hd * DH:(hd + 1) * DH], pT[:, i, hd, :], v[:, i, :], start=True, stop=True)
            m.wait(dve, m.M(mm))
            en = m.V(dve.tensor_tensor(enc[:, i, :].rearrange("p (h d) -> p h d", h=NH),
                                       m.psum[:, bank, 0:D].rearrange("p (h d) -> p h d", h=NH),
                                       bcast(sm[:, i].unsqueeze(2), P, NH, DH), ALU.mult))
            m.banks.freed[bank] = (en,)
            bank, free = m.banks.take()
            m.wait(pe, en, *free)
            for c in range(DC):
                mm = pe.transpose(m.psum[:, bank, c * P:(c + 1) * P], enc[:, i, c * P:(c + 1) * P], m.ident[:, :])
            m.wait(act, m.M(mm))
            et = m.A(act.activation(encT[:, i].rearrange("p c s -> p (c s)"), m.psum[:, bank, 0:D], ACT.Copy))
            m.banks.freed[bank] = (et,)
            bank, free = m.banks.take()
            m.wait(pe, et, *free)
            for c in range(DC):
                mm = pe.matmul(m.psum[:, bank, 0:D], encT[:, i, c, :], m.small["out_w1"][:, c, :], start=(c == 0), stop=(c == DC - 1))
            out = m.M(mm)
            m.wait(dve, out)
            m.x_ready[b] = m.V(dve.tensor_tensor(m.X[:, b, :], m.X[:, b, :], m.psum[:, bank, 0:D], ALU.add))
            m.banks.freed[bank] = (m.x_ready[b],)
            free_q[i] = (out,)
        m.barrier()



def layer1_ffn(m, ins):
    NH, NE, DP = 8, 8, 128
    SCALE = 1.0 / float(DP) ** 0.5
    m.layer("ffn1")
    pe, dve, act, pool = m.pe, m.dve, m.act, m.pool
    xt = layernorm(m, m.xt_free)
    with ExitStack() as scratch:
        def sb(name, shape):
            return m.sb(name, shape, F32, scratch)
        gates = sb("gates1", [P, T, 2 * NH, NE])
        den = sb("den1", [P, T * 2 * NH])
        qT, kT = sb("qT1", [P, T * P]), sb("kT1", [P, T * P])
        v = sb("v1", [P, T, DP])
        cT = sb("cT1", [P, T * P])
        S = sb("scores1", [P, 2, G, P])
        sm = sb("sum1", [P, 2, G])
        mx = sb("max1", [P, 2, G])
        sT = sb("scoresT1", [P, 2, G * P])
        n = T * 2 * NH
        flat = gates[:, :, :, :].rearrange("p t h e -> p (t h) e")
        for g in range(NG):
            bank, free = m.banks.take()
            m.wait(pe, m.small_ready, xt[g], *free)
            for j in range(G):
                t = g * G + j
                for c in range(DC):
                    mm = pe.matmul(m.psum[:, bank, j * P:(j + 1) * P], m.XT[:, c, t * P:(t + 1) * P], m.small["sel_w1"][:, c, :],
                                   start=(c == 0), stop=(c == DC - 1))
            m.wait(act, m.M(mm))
            sg = m.A(act.activation(gates[:, g * G:(g + 1) * G].rearrange("p t h e -> p (t h e)"), m.psum[:, bank, :], ACT.Sigmoid))
            m.banks.freed[bank] = (sg,)
        CH = 64
        for k in range(n // CH):
            part = slice(k * CH, (k + 1) * CH)
            top2(m, flat[:, part, :], sg)
            v2 = m.top_v
            m.VV(dve.tensor_tensor(den[:, part], v2[:, 0, 0:CH], v2[:, 1, 0:CH], ALU.add))
            m.VV(dve.tensor_scalar(den[:, part], den[:, part], 1e-9, None, ALU.max))
            m.VV(dve.reciprocal(den[:, part], den[:, part]))
            m.wait(dve, m.small_ready)
            m.VV(dve.tensor_scalar(den[:, part], den[:, part], m.small["route_scale"][:, 0:1], None, ALU.mult))
            m.VV(dve.tensor_tensor(v2[:, :, 0:CH], v2[:, :, 0:CH], bcast(den[:, part].unsqueeze(1), P, 2, CH), ALU.mult))
            gates_ready = combine(m, flat[:, part, :], CH)

        qk_free, ct_free = (), ()
        for hd in range(NH):
            slot, (wq, wk, wv, wo), w_ready = m.W.load(ins["ffn1_q"][hd], ins["ffn1_k"][hd], ins["ffn1_v"][hd], ins["ffn1_o"][hd])
            wv = wv.rearrange("p (c e) -> p c e", c=DC)
            m.wait(pe, w_ready)
            qk_ready = []
            for g in range(NG):
                tok = slice(g * GT, (g + 1) * GT)
                for w, dst in ((wq, qT), (wk, kT)):
                    w = w.rearrange("p (c f) -> p c f", c=DC)
                    bank, free = m.banks.take()
                    m.wait(pe, *free)
                    for c in range(DC):
                        mm = pe.matmul(m.psum[:, bank, :], w[:, c, :], m.XT[:, c, tok], start=(c == 0), stop=(c == DC - 1))
                    m.wait(act, m.M(mm), *qk_free)
                    qk = m.A(act.activation(dst[:, tok], m.psum[:, bank, :], ACT.Copy))
                    m.banks.freed[bank] = (qk,)
                qk_ready.append(qk)
            v_ready = []
            for t in range(T):
                for half in range(2):
                    bank, free = m.banks.take()
                    m.wait(pe, *free)
                    for c in range(DC):
                        mm = pe.matmul(m.psum[:, bank, :], m.XT[:, c, t * P:(t + 1) * P], wv[:, c, half * BANK:(half + 1) * BANK],
                                       start=(c == 0), stop=(c == DC - 1))
                    m.wait(dve, m.M(mm), gates_ready)
                    for j in range(4):
                        e = half * 4 + j
                        src, gate = m.psum[:, bank, j * DP:(j + 1) * DP], gates[:, t, hd, e:e + 1]
                        if e == 0:
                            m.wait(dve, *qk_free)
                            vr = m.VV(dve.tensor_scalar(v[:, t, :], src, gate, None, ALU.mult))
                        else:
                            vr = m.VV(dve.scalar_tensor_tensor(out=v[:, t, :], in0=src, scalar=gate, in1=v[:, t, :], op0=ALU.mult, op1=ALU.add))
                    m.banks.freed[bank] = (vr,)
                v_ready.append(vr)
            for g in range(NG):
                i = g % 2
                bank, free = m.banks.take()
                m.wait(pe, qk_ready[g], *free)
                for j in range(G):
                    tok = slice((g * G + j) * P, (g * G + j + 1) * P)
                    mm = pe.matmul(m.psum[:, bank, j * P:(j + 1) * P], qT[:, tok], kT[:, tok], start=True, stop=True)
                m.wait(dve, m.M(mm))
                src = m.psum[:, bank, :].rearrange("p (j s) -> p j s", j=G)
                m.VV(dve.tensor_reduce(mx[:, i], src, AX.X, ALU.max))
                sub = m.V(dve.tensor_tensor(S[:, i], src, bcast(mx[:, i].unsqueeze(2), P, G, P), ALU.subtract))
                m.banks.freed[bank] = (sub,)
                m.wait(act, sub)
                m.wait(dve, m.A(act.activation(S[:, i], S[:, i], ACT.Exp, scale=SCALE)))
                m.VV(dve.tensor_reduce(sm[:, i], S[:, i], AX.X, ALU.add))
                m.VV(dve.reciprocal(sm[:, i], sm[:, i]))
                pr = m.V(dve.tensor_tensor(S[:, i], S[:, i], bcast(sm[:, i].unsqueeze(2), P, G, P), ALU.mult))
                bank, free = m.banks.take()
                m.wait(pe, pr, *free)
                for j in range(G):
                    mm = pe.transpose(m.psum[:, bank, j * P:(j + 1) * P], S[:, i, j, :], m.ident[:, :])
                m.wait(act, m.M(mm))
                st = m.A(act.activation(sT[:, i, :], m.psum[:, bank, :], ACT.Copy))
                m.banks.freed[bank] = (st,)
                bank, free = m.banks.take()
                m.wait(pe, st, v_ready[g * G + G - 1], *free)
                for j in range(G):
                    mm = pe.matmul(m.psum[:, bank, j * P:(j + 1) * P], v[:, g * G + j, :], sT[:, i, j * P:(j + 1) * P], start=True, stop=True)
                used = m.M(mm)
                m.wait(act, used, *ct_free)
                ct = m.A(act.activation(cT[:, g * GT:(g + 1) * GT], m.psum[:, bank, :], ACT.Copy))
                m.banks.freed[bank] = (ct,)
            qk_free = (used,)
            m.wait(pe, ct)
            for t in range(T):
                for k in range(4):
                    bank, free = m.banks.take()
                    m.wait(pe, *free)
                    mm = pe.matmul(m.psum[:, bank, :], cT[:, t * P:(t + 1) * P], wo[:, k * BANK:(k + 1) * BANK], start=True, stop=True)
                    used = m.M(mm)
                    m.wait(dve, used, m.x_ready[t])
                    for j in range(2):
                        e = k * 2 + j
                        added = m.VV(dve.scalar_tensor_tensor(out=m.X[:, t, :], in0=m.psum[:, bank, j * D:(j + 1) * D],
                                                              scalar=gates[:, t, NH + hd, e:e + 1], in1=m.X[:, t, :],
                                                              op0=ALU.mult, op1=ALU.add))
                    m.banks.freed[bank] = (added,)
                m.x_ready[t] = added
            ct_free = (used,)
            m.W.ring.freed[slot] = (used,)
        m.xt_free = (used,)
        m.barrier()



def layer2_ffn(m, ins):
    NE = 16
    m.layer("ffn2")
    pe, dve, act, pool = m.pe, m.dve, m.act, m.pool
    xt = layernorm(m, m.xt_free)
    with ExitStack() as scratch:
        def sb(name, shape):
            return m.sb(name, shape, F32, scratch)
        z = sb("z", [P, T, NE])
        zs = sb("z_sorted", [P, T, NE])
        zr = sb("z_rest", [P, T, NE])
        st, mv, rs = sb("z_st", [P, T, 6]), sb("z_mv", [P, T, 2]), sb("z_rs", [P, T])
        c1 = [sb(f"cum{i}", [P, T, NE]) for i in range(2)]
        c2 = [sb(f"cumsq{i}", [P, T, NE]) for i in range(2)]
        ik = sb("inv_count", [P, NE])
        mean, tau, hit = sb("mean", [P, T, NE]), sb("tau", [P, T, NE]), sb("hit", [P, T, NE])
        zt, sup = sb("z_top", [P, T]), sb("support", [P, T])
        aT = sb("a_t", [NE, T * P])
        g1, g2, z1 = sb("g1", [P, 2, GT]), sb("g2", [P, 2, GT]), sb("z1", [P, 2, GT])
        z2 = sb("z2", [P, 2, GT])
        shape = [P, T, NE]
        bank, logits = router_logits(m, m.XT, xt, m.small["proj2"], NE)
        m.wait(dve, logits)
        cp = m.VV(dve.tensor_copy(z[:, :, :], m.psum[:, bank, 0:T * NE].rearrange("p (t e) -> p t e", t=T)))
        m.banks.freed[bank] = (cp,)
        for t in range(T):
            s_ = dve.bn_stats(st[:, t, :], z[:, t, :])
        m.VV(s_)
        for t in range(T):
            s_ = dve.bn_aggr(mv[:, t, :], st[:, t, :])
        m.VV(s_)
        rsqrt(m, rs[:, :], mv[:, :, 1], LN_EPS, None)
        m.VV(dve.tensor_tensor(z[:, :, :], z[:, :, :], bcast(mv[:, :, 0:1], *shape), ALU.subtract))
        m.VV(dve.tensor_tensor(z[:, :, :], z[:, :, :], bcast(rs[:, :].unsqueeze(2), *shape), ALU.mult))
        m.VV(dve.tensor_scalar(z[:, :, :], z[:, :, :], 0.5, None, ALU.mult))
        m.VV(dve.tensor_reduce(zt[:, :], z[:, :, :], AX.X, ALU.max))
        m.VV(dve.tensor_tensor(z[:, :, :], z[:, :, :], bcast(zt[:, :].unsqueeze(2), *shape), ALU.subtract))
        for t in range(T):
            s_ = dve.max(zs[:, t, 0:8], z[:, t, :])
        m.VV(s_)
        for t in range(T):
            s_ = dve.match_replace(zr[:, t, :], zs[:, t, 0:8], z[:, t, :], LOWEST)
        m.VV(s_)
        for t in range(T):
            s_ = dve.max(zs[:, t, 8:16], zr[:, t, :])
        m.VV(s_)
        m.VV(dve.reciprocal(ik[:, :], m.count16[:, :]))
        m.VV(dve.tensor_copy(c1[0][:, :, :], zs[:, :, :]))
        m.VV(dve.tensor_tensor(c2[0][:, :, :], zs[:, :, :], zs[:, :, :], ALU.mult))
        for k in range(4):
            s = 1 << k
            for c in (c1, c2):
                x, y = c[k % 2], c[1 - k % 2]
                dve.tensor_copy(y[:, :, 0:s], x[:, :, 0:s])
                m.VV(dve.tensor_tensor(y[:, :, s:], x[:, :, s:], x[:, :, 0:NE - s], ALU.add))
        kb = bcast(m.count16[:, :].unsqueeze(1), *shape)
        ikb = bcast(ik[:, :].unsqueeze(1), *shape)
        m.VV(dve.tensor_tensor(mean[:, :, :], c1[0][:, :, :], ikb, ALU.mult))
        m.VV(dve.tensor_tensor(c2[0][:, :, :], c2[0][:, :, :], ikb, ALU.mult))
        m.VV(dve.tensor_tensor(c1[1][:, :, :], mean[:, :, :], mean[:, :, :], ALU.mult))
        m.VV(dve.tensor_tensor(c2[0][:, :, :], c2[0][:, :, :], c1[1][:, :, :], ALU.subtract))
        m.VV(dve.tensor_tensor(c2[0][:, :, :], c2[0][:, :, :], kb, ALU.mult))
        m.VV(dve.tensor_scalar(c2[0][:, :, :], c2[0][:, :, :], -1.0, 1.0, ALU.mult, ALU.add))
        m.VV(dve.tensor_tensor(c2[0][:, :, :], c2[0][:, :, :], ikb, ALU.mult))
        dl = m.V(dve.tensor_scalar(c2[0][:, :, :], c2[0][:, :, :], 0.0, None, ALU.max))
        m.wait(act, dl)
        m.wait(dve, m.A(act.activation(c2[1][:, :, :], c2[0][:, :, :], ACT.Sqrt)))
        m.VV(dve.tensor_tensor(tau[:, :, :], mean[:, :, :], c2[1][:, :, :], ALU.subtract))
        m.VV(dve.tensor_tensor(hit[:, :, :], tau[:, :, :], zs[:, :, :], ALU.is_le))
        m.VV(dve.tensor_reduce(sup[:, :], hit[:, :, :], AX.X, ALU.add))
        m.VV(dve.tensor_tensor(hit[:, :, :], kb, bcast(sup[:, :].unsqueeze(2), *shape), ALU.is_equal))
        m.VV(dve.tensor_tensor(hit[:, :, :], hit[:, :, :], tau[:, :, :], ALU.mult))
        m.VV(dve.tensor_reduce(zt[:, :], hit[:, :, :], AX.X, ALU.add))
        m.VV(dve.tensor_tensor(z[:, :, :], z[:, :, :], bcast(zt[:, :].unsqueeze(2), *shape), ALU.subtract))
        m.VV(dve.tensor_scalar(z[:, :, :], z[:, :, :], 0.0, None, ALU.max))
        ar = m.VV(dve.tensor_tensor(z[:, :, :], z[:, :, :], z[:, :, :], ALU.mult))
        for g in range(NG):
            bank, free = m.banks.take()
            m.wait(pe, ar, m.const_ready, *free)
            for j in range(G):
                mm = pe.transpose(m.psum[0:NE, bank, j * P:(j + 1) * P], z[:, g * G + j, :], m.ident[:, :])
            m.wait(act, m.M(mm))
            at = m.A(act.activation(aT[:, g * GT:(g + 1) * GT], m.psum[0:NE, bank, :], ACT.Copy))
            m.banks.freed[bank] = (at,)
        z2_free = [(), ()]
        for g in range(NG):
            i = g % 2
            tok = slice(g * GT, (g + 1) * GT)
            for w, dst in ((m.small["C1"], g1), (m.small["C2"], g2)):
                bank, free = m.banks.take()
                m.wait(pe, at, m.small_ready, *free)
                mm = pe.matmul(m.psum[:, bank, :], w[0:NE, :], aT[:, tok], start=True, stop=True)
                m.wait(act, m.M(mm), *z2_free[i])
                gr = m.A(act.activation(dst[:, i, :], m.psum[:, bank, :], ACT.Copy))
                m.banks.freed[bank] = (gr,)
            bank, free = m.banks.take()
            m.wait(pe, *free)
            for c in range(DC):
                mm = pe.matmul(m.psum[:, bank, :], m.small["Win1"][:, c, :], m.XT[:, c, tok], start=(c == 0), stop=(c == DC - 1))
            xt_used = m.M(mm)
            m.wait(dve, xt_used, gr, *z2_free[i])
            z1r = m.V(dve.scalar_tensor_tensor(out=z1[:, i, :], in0=m.psum[:, bank, :], scalar=m.small["win1_b"][:, 0:1],
                                               in1=g1[:, i, :], op0=ALU.add, op1=ALU.mult))
            m.banks.freed[bank] = (z1r,)
            h_slot, h_free = m.h_ring.take()
            m.wait(act, *h_free)
            hm = []
            for f in range(8):
                bank, free = m.banks.take()
                m.wait(pe, z1r, *free)
                mm = pe.matmul(m.psum[:, bank, :], m.small["Wout1"][:, f, :], z1[:, i, :], start=True, stop=True)
                m.wait(act, m.M(mm))
                hr = m.A(act.activation(m.H[:, h_slot, f, :], m.psum[:, bank, :], ACT.Gelu))
                m.banks.freed[bank] = (hr,)
                hm.append(hr)
            bank, free = m.banks.take()
            m.wait(pe, *free)
            for f in range(8):
                m.wait(pe, hm[f])
                mm = pe.matmul(m.psum[:, bank, :], m.small["Win2"][:, f, :], m.H[:, h_slot, f, :], start=(f == 0), stop=(f == 7))
            h_used = m.M(mm)
            m.h_ring.freed[h_slot] = (h_used,)
            m.wait(dve, h_used)
            z2r = m.V(dve.scalar_tensor_tensor(out=z2[:, i, :], in0=m.psum[:, bank, :], scalar=m.small["win2_b"][:, 0:1],
                                               in1=g2[:, i, :], op0=ALU.add, op1=ALU.mult))
            m.banks.freed[bank] = (z2r,)
            for half in range(2):
                bank, free = m.banks.take()
                m.wait(pe, z2r, *free)
                for j in range(2):
                    k = half * 2 + j
                    mm = pe.matmul(m.psum[:, bank, j * D:(j + 1) * D], z2[:, i, k * P:(k + 1) * P], m.small["Wout2"][:, :], start=True, stop=True)
                out = m.M(mm)
                t = g * G + half * 2
                m.wait(dve, out, m.x_ready[t], m.x_ready[t + 1])
                added = m.V(dve.tensor_tensor(m.X[:, t:t + 2, :], m.X[:, t:t + 2, :],
                                              m.psum[:, bank, :].rearrange("p (j d) -> p j d", j=2), ALU.add))
                m.banks.freed[bank] = (added,)
                m.x_ready[t:t + 2] = [added] * 2
            z2_free[i] = (out, added)
        m.xt_free = (xt_used,)
        m.barrier()



def layer3_mix(m, ins):
    SCALE = 64 ** -0.5
    KEYS = 2 * P
    m.layer("mix3")
    pe, dve, act, pool = m.pe, m.dve, m.act, m.pool
    xt = layernorm(m, m.xt_free)
    with ExitStack() as scratch:
        def sb(name, shape):
            return m.sb(name, shape, F32, scratch)
        qT, kT = sb("qT3", [P, 2, DC, GT]), sb("kT3", [P, 2, DC, GT])
        v = sb("v3", [P, 2, G, D])
        S = sb("scores3", [P, 2, 2, KEYS])
        mx, sm = sb("max3", [P, 2, 2]), sb("sum3", [P, 2, 2])
        sT = sb("scoresT3", [P, 2, 2, KEYS])
        free_g = [(), ()]
        n = 0
        s_free = [(), ()]
        for g in range(NG):
            i = g % 2
            tok = slice(g * GT, (g + 1) * GT)
            m.wait(pe, xt[g], m.small_ready)
            for w, bias, dst in (("q_w3", "q_b3", qT), ("k_w3", "k_b3", kT)):
                for o in range(DC):
                    bank, free = m.banks.take()
                    m.wait(pe, *free)
                    for c in range(DC):
                        mm = pe.matmul(m.psum[:, bank, :], m.small[w][:, c, o * P:(o + 1) * P], m.XT[:, c, tok], start=(c == 0), stop=(c == DC - 1))
                    m.wait(act, m.M(mm), m.small_ready, *free_g[i])
                    qk = m.A(act.activation(dst[:, i, o, :], m.psum[:, bank, :], ACT.Identity, bias=m.small[bias][:, o:o + 1]))
                    m.banks.freed[bank] = (qk,)
            for half in range(2):
                bank, free = m.banks.take()
                m.wait(pe, *free)
                for j in range(2):
                    t = g * G + half * 2 + j
                    for c in range(DC):
                        mm = pe.matmul(m.psum[:, bank, j * D:(j + 1) * D], m.XT[:, c, t * P:(t + 1) * P], m.small["v_w3"][:, c, :],
                                       start=(c == 0), stop=(c == DC - 1))
                xt_used = m.M(mm)
                m.wait(dve, xt_used, *free_g[i])
                vr = m.V(dve.tensor_tensor(v[:, i, half * 2:half * 2 + 2, :], m.psum[:, bank, :].rearrange("p (j d) -> p j d", j=2),
                                           bcast(m.small["v_b3"][:, :].unsqueeze(1), P, 2, D), ALU.add))
                m.banks.freed[bank] = (vr,)
            for half in range(2):
                s = n % 2
                n += 1
                bank, free = m.banks.take()
                m.wait(pe, qk, *free)
                for j in range(2):
                    k = half * 2 + j
                    loc = slice(k * P, (k + 1) * P)
                    glob = slice((g * G + k) * P, (g * G + k + 1) * P)
                    for part, keys in ((0, lambda c: m.CTXT[:, c, glob]), (1, lambda c: kT[:, i, c, loc])):
                        col = j * KEYS + part * P
                        for c in range(DC):
                            mm = pe.matmul(m.psum[:, bank, col:col + P], qT[:, i, c, loc], keys(c), start=(c == 0), stop=(c == DC - 1))
                m.wait(dve, m.M(mm))
                src = m.psum[:, bank, :].rearrange("p (j s) -> p j s", j=2)
                m.VV(dve.tensor_reduce(mx[:, s], src, AX.X, ALU.max))
                sub = m.V(dve.tensor_tensor(S[:, s], src, bcast(mx[:, s].unsqueeze(2), P, 2, KEYS), ALU.subtract))
                m.banks.freed[bank] = (sub,)
                m.wait(act, sub)
                ex = m.A(act.activation(S[:, s], S[:, s], ACT.Exp, scale=SCALE))
                m.wait(dve, ex)
                m.VV(dve.tensor_reduce(sm[:, s], S[:, s], AX.X, ALU.add))
                m.VV(dve.reciprocal(sm[:, s], sm[:, s]))
                bank, free = m.banks.take()
                m.wait(pe, ex, *free)
                for j in range(2):
                    for part in range(2):
                        col = j * KEYS + part * P
                        mm = pe.transpose(m.psum[:, bank, col:col + P], S[:, s, j, part * P:(part + 1) * P], m.ident[:, :])
                m.wait(act, m.M(mm))
                st = m.A(act.activation(sT[:, s].rearrange("p j s -> p (j s)"), m.psum[:, bank, :], ACT.Copy))
                m.banks.freed[bank] = (st,)
                bank, free = m.banks.take()
                m.wait(pe, st, vr, *free)
                for j in range(2):
                    k = half * 2 + j
                    t = g * G + k
                    pe.matmul(m.psum[:, bank, j * D:(j + 1) * D], sT[:, s, j, 0:P], m.CTX[:, t, :], start=True, stop=False)
                    mm = pe.matmul(m.psum[:, bank, j * D:(j + 1) * D], sT[:, s, j, P:KEYS], v[:, i, k, :], start=False, stop=True)
                out = m.M(mm)
                m.wait(dve, out)
                for j in range(2):
                    t = g * G + half * 2 + j
                    m.wait(dve, m.x_ready[t])
                    m.x_ready[t] = m.V(dve.scalar_tensor_tensor(out=m.X[:, t, :], in0=m.psum[:, bank, j * D:(j + 1) * D],
                                                                scalar=sm[:, s, j:j + 1], in1=m.X[:, t, :], op0=ALU.mult, op1=ALU.add))
                m.banks.freed[bank] = (m.x_ready[t],)
            free_g[i] = (out,)
        m.xt_free = (xt_used,)
        m.barrier()


LAYERS = [layer0_mix, layer0_ffn, layer1_mix, layer1_ffn, layer2_mix, layer2_ffn, layer3_mix, layer3_ffn]
NLAYERS = 8


def build(nc, ins, out):
    with ExitStack() as ctx:
        m = Machine(nc, ctx)
        m.psum = ctx.enter_context(nc.psum_tensor("psum", [P, 8, BANK], F32))
        m.banks = Ring(8)
        constants(m, ins)
        m.XT = m.sb("XT", [P, DC, T * P])
        m.CTXT = m.sb("CTXT", [P, DC, T * P])
        m.xt_free = ()
        m.LN = m.sb("LN", [P, 1, G, D])
        m.ln_ring = Ring(1)
        m.ln_stats, m.ln_mv, m.ln_rstd = m.sb("ln_stats", [P, G, 6]), m.sb("ln_mv", [P, G, 2]), m.sb("ln_rstd", [P, G])
        NR = 64
        m.top_key, m.top_best = m.sb("top_key", [P, NR, 8]), m.sb("top_best", [P, NR])
        m.top_v, m.top_h = m.sb("top_v", [P, 2, NR]), m.sb("top_h", [P, 2, NR, 8])
        m.route, m.gates = m.sb("route", [P, T, 8]), m.sb("gates", [P, T, 8])
        def barrier():
            ends = tuple((s, s.value) for s in (m.S_pe, m.S_dve, m.S_act, m.S_pool) if s.value)
            for eng in (m.pe, m.dve, m.act, m.pool, m.sp):
                m.wait(eng, *ends)
        m.barrier = barrier
        m.W = Weights(m, 2, 4608)
        for n, layer in enumerate(LAYERS[:NLAYERS]):
            with ExitStack() as part:
                if layer in (layer0_ffn, layer2_mix, layer3_ffn):
                    m.H = m.sb(f"H{n}", [P, 2, 8, GT], F32, part)
                    m.gates_fm = m.sb(f"gates_fm{n}", [8, T * P], F32, part)
                    m.h_ring = Ring(2)
                elif layer is layer2_ffn:
                    m.H = m.sb(f"H{n}", [P, 1, 8, GT], F32, part)
                    m.h_ring = Ring(1)
                layer(m, ins)
                m.barrier()
        S_out = m.counter("store", 16)
        m.wait(m.sp, *m.x_ready)
        stored = S_out.after(m.sp.dma_start(out, m.X[:, :, :]))
        m.wait(m.sp, stored)


def chunks(w):
    n = w.shape[0] // P
    return w.reshape(n, P, w.shape[1]).transpose(1, 0, 2)


def kernel(**a):
    import numpy as np
    import concourse.bacc as bacc
    from concourse.bass_utils import run_bass_kernel_spmd

    a = {k: np.asarray(v) for k, v in a.items()}

    def tiles(x):
        return x.transpose(1, 0, 2)

    def ffn(w1, w2):
        E = w1.shape[0]
        w1 = np.stack([chunks(w1[e]).reshape(P, -1) for e in range(E)])
        w2 = np.stack([chunks(w2[e]).reshape(P, -1) for e in range(E)])
        return w1, w2

    h = {"x": tiles(a["x"]), "ctx": tiles(a["ctx_1024"]), "mask": a["mask_BxS2_bk0"].reshape(1, -1)}
    h["gate_w0"] = chunks(np.concatenate([a["L0_xattn_igate_w"], a["L0_xattn_fgate_w"]]).T)
    h["gate_b0"] = np.concatenate([a["L0_xattn_igate_b"], a["L0_xattn_fgate_b"]])[None]
    h["head_scale0"] = a["L0_xattn_out_w"][None]
    h["router_w0"] = chunks(a["L0_ffn_router_w"].T)
    h["ffn0_w1"], h["ffn0_w2"] = ffn(a["L0_ffn_fc1_w"].transpose(0, 2, 1), a["L0_ffn_fc2_w"].transpose(0, 2, 1))
    h["rms_scale"] = a["L1_xattn_rms_scale"][None]
    h["q_w1"] = chunks(a["L1_xattn_q_w"].transpose(1, 0, 2).reshape(D, D))
    h["kv_w1"] = chunks(a["L1_xattn_kv_w"][:, 0].transpose(1, 0, 2).reshape(D, P))
    h["out_w1"] = chunks(a["L1_xattn_out_w"].reshape(D, D))
    freq = np.float32(10000.0) ** (np.float32(2.0 / 64) * np.arange(32, dtype=np.float32))
    pos = np.arange(2 * P, dtype=np.float32).reshape(2, P, 1) / freq
    h["cos"], h["sin"] = (np.ascontiguousarray(f(pos).astype(np.float32).transpose(1, 0, 2)) for f in (np.cos, np.sin))
    h["sel_w1"] = chunks(np.concatenate([a["L1_ffn_sel_v_w"], a["L1_ffn_sel_o_w"]]).T)
    h["route_scale"] = a["L1_ffn_route_scale"][None]
    for k in "qk":
        w = a[f"L1_ffn_{k}_w"].reshape(8, P, D).transpose(0, 2, 1)
        h["ffn1_" + k] = np.stack([chunks(w[i]).reshape(P, -1) for i in range(8)])
    w = a["L1_ffn_v_w"].reshape(8, 8, D, P).transpose(0, 2, 1, 3).reshape(8, D, 8 * P)
    h["ffn1_v"] = np.stack([chunks(w[i]).reshape(P, -1) for i in range(8)])
    h["ffn1_o"] = a["L1_ffn_o_w"].reshape(8, 8, P, D).transpose(0, 2, 1, 3).reshape(8, P, 8 * D)
    h["router_w2"] = chunks(a["L2_xattn_Wg"])
    h["router_b2"] = a["L2_xattn_bg"][None]
    h["mix2_w1"], h["mix2_w2"] = ffn(a["L2_xattn_W1"], a["L2_xattn_W2"])
    h["b1_2"] = a["L2_xattn_b1"].reshape(8, 8, P).transpose(2, 0, 1)
    h["b2_2"] = a["L2_xattn_b2"]
    h["proj2"] = chunks(a["L2_ffn_proj"])
    h["C1"], h["C2"] = a["L2_ffn_C1"], a["L2_ffn_C2"]
    h["Win1"], h["win1_b"] = chunks(a["L2_ffn_Win1"][:D]), a["L2_ffn_Win1"][D][:, None]
    h["Wout1"] = a["L2_ffn_Wout1"].T.reshape(P, 8, P)
    h["Win2"], h["win2_b"] = chunks(a["L2_ffn_Win2"][:1024]), a["L2_ffn_Win2"][1024][:, None]
    h["Wout2"] = a["L2_ffn_Wout2"].T
    for k in "qkv":
        h[k + "_w3"] = chunks(a[f"L3_xattn_W{k}"].T)
    for k in "qk":
        h[k + "_b3"] = a[f"L3_xattn_b{k}"].reshape(DC, P).T
    h["v_b3"] = a["L3_xattn_bv"][None]
    h["router_w3"] = chunks(a["L3_ffn_gate_w"])
    h["router_b3"] = a["L3_ffn_gate_b"][None]
    w1 = np.concatenate([a["L3_ffn_sh_w1"][None], a["L3_ffn_ew1"]])
    w2 = np.concatenate([a["L3_ffn_sh_w2"][None], a["L3_ffn_ew2"]])
    h["ffn3_w1"], h["ffn3_w2"] = ffn(w1, w2)
    h["b1_3"] = np.concatenate([a["L3_ffn_sh_b1"][None], a["L3_ffn_eb1"]]).reshape(9, 8, P).transpose(2, 0, 1)
    h["b2_3"] = a["L3_ffn_eb2"]
    h["sh_b2_3"] = a["L3_ffn_sh_b2"][None]

    nc = bacc.Bacc("TRN2", target_bir_lowering=False, num_devices=1)
    arrays, ins = {}, {}
    for name, v in h.items():
        v = np.ascontiguousarray(v)
        arrays["in_" + name] = v
        ins[name] = nc.dram_tensor("in_" + name, v.shape, mybir.dt.from_np(v.dtype), kind="ExternalInput").ap()
    out = nc.dram_tensor("out", (P, T, D), F32, kind="ExternalOutput").ap()
    build(nc, ins, out)
    r = run_bass_kernel_spmd(nc, [arrays], core_ids=[0])
    return np.ascontiguousarray(r.results[0]["out"].transpose(1, 0, 2))
```

```python
from contextlib import ExitStack

import concourse.bass as bass
from concourse import mybir

F32 = mybir.dt.float32
F32R = mybir.dt.float32r
U8 = mybir.dt.uint8
I32 = mybir.dt.int32
ALU = mybir.AluOpType
ACT = mybir.ActivationFunctionType
AX = mybir.AxisListType

P = 128
T = 16
D = 256
DC = D // P
G = 4
NG = T // G
GT = G * P
BANK = 512
LN_EPS = 1e-5
RMS_EPS = 1e-6
LOWEST = -3.0e38
MASK_FILL = -2.3819763e38


class Counter:

    def __init__(self, sem, step=1):
        self.sem, self.step, self.value = sem, step, 0

    def after(self, instruction):
        instruction.then_inc(self.sem, self.step)
        self.value += self.step
        return (self, self.value)


class Ring:

    def __init__(self, n):
        self.n, self.turn, self.freed = n, 0, [()] * n

    def take(self):
        for k in range(self.n):
            slot = (self.turn + k) % self.n
            if self.freed[slot] is not None:
                self.turn = slot + 1
                marks, self.freed[slot] = self.freed[slot], None
                return slot, marks
        raise AssertionError("every buffer is held")


def interleave(jobs, depth):
    jobs, live = list(jobs), []
    while jobs or live:
        if jobs and len(live) < depth:
            live.append(jobs.pop(0))
        for job in list(live):
            for _ in job:
                break
            else:
                live.remove(job)


class Machine:

    def __init__(self, nc, ctx):
        self.nc, self.ctx = nc, ctx
        self.pe, self.dve, self.act, self.pool, self.sp = nc.tensor, nc.vector, nc.scalar, nc.gpsimd, nc.sync
        self.seen = {}

    def sb(self, name, shape, dt=F32, ctx=None):
        return (ctx or self.ctx).enter_context(self.nc.sbuf_tensor(name, shape, dt))

    def counter(self, name, step=1):
        return Counter(self.ctx.enter_context(self.nc.semaphore(name)), step)

    def wait(self, engine, *marks):
        for counter, value in marks:
            key = (engine.engine, counter.sem.name)
            if self.seen.get(key, 0) < value:
                engine.wait_ge(counter.sem, value)
                self.seen[key] = value

    def layer(self, name):
        self.S_pe = self.counter(name + "_pe")
        self.S_dve = self.counter(name + "_dve")
        self.S_act = self.counter(name + "_act")
        self.S_pool = self.counter(name + "_pool")

    def V(self, instruction):
        return self.S_dve.after(instruction)

    def A(self, instruction):
        return self.S_act.after(instruction)

    def M(self, instruction):
        return self.S_pe.after(instruction)

    def Q(self, instruction):
        return self.S_pool.after(instruction)

    def VV(self, instruction):
        mark = self.V(instruction)
        self.wait(self.dve, mark)
        return mark


def bcast(ap, *shape):
    return ap.broadcast_to(list(shape))



def constants(m, ins):
    m.layer("const")
    pool, dve, sp = m.pool, m.dve, m.sp
    m.ident = m.sb("ident", [P, P])
    m.tri_incl = m.sb("tri_incl", [P, P])
    m.tri_excl = m.sb("tri_excl", [P, P])
    m.ones = m.sb("ones", [P, 1])
    m.minus_half = m.sb("minus_half", [P, T * 4])
    m.rank8 = m.sb("rank8", [P, 8])
    m.count16 = m.sb("count16", [P, 16])
    zero = dve.memset(m.ident[:, :], 0.0)
    dve.memset(m.tri_incl[:, :], 1.0)
    dve.memset(m.tri_excl[:, :], 1.0)
    dve.memset(m.ones[:, :], 1.0)
    for j in range(8):
        dve.memset(m.rank8[:, j:j + 1], float(8 - j))
    m.expert_row = m.sb("expert_row", [P, 8])
    for j in range(8):
        dve.memset(m.expert_row[:, j:j + 1], float(j * T * P))
    for j in range(16):
        dve.memset(m.count16[:, j:j + 1], float(j + 1))
    filled = m.V(dve.memset(m.minus_half[:, :], -0.5))
    m.wait(pool, filled)
    pool.affine_select(out=m.ident[:, :], in_=m.ident[:, :], compare_op=ALU.not_equal, fill=1.0,
                       base=0, pattern=[[-1, P]], channel_multiplier=1)
    pool.affine_select(out=m.tri_incl[:, :], in_=m.tri_incl[:, :], compare_op=ALU.is_ge, fill=0.0,
                       base=0, pattern=[[1, P]], channel_multiplier=-1)
    m.const_ready = m.Q(pool.affine_select(out=m.tri_excl[:, :], in_=m.tri_excl[:, :], compare_op=ALU.is_gt,
                                           fill=0.0, base=0, pattern=[[1, P]], channel_multiplier=-1))
    m.filled = filled
    S_in = m.counter("load_x", 16)
    m.S_ctx = m.counter("load_ctx", 16)
    S_small = m.counter("load_small", 16)
    m.X = m.sb("X", [P, T, D])
    m.x_ready = [S_in.after(sp.dma_start(m.X[:, :, :], ins["x"]))] * T
    S_first = m.counter("load_first", 16)
    m.small = {}
    for name, shape in SMALL:
        t = m.sb("w_" + name, [P] + list(shape))
        src = ins[name]
        if src.shape[0] == 1:
            src = src.partition_broadcast(P) if len(src.shape) == 1 else src[0].partition_broadcast(P)
        np_ = src.shape[0]
        mark = (S_first if name in FIRST else S_small).after(sp.dma_start(t[0:np_], src))
        if name in FIRST:
            m.first_ready = mark
        else:
            m.small_ready = mark
        m.small[name] = t


FIRST = ("gate_w0", "gate_b0", "head_scale0")
SMALL = [
    ("gate_w0", (6, 8)), ("gate_b0", (8,)), ("head_scale0", (D,)),
    ("router_w0", (DC, 8)),
    ("rms_scale", (D,)), ("q_w1", (DC, D)), ("kv_w1", (DC, 3 * 64)), ("out_w1", (DC, D)),
    ("cos", (6, 32)), ("sin", (6, 2, 32)),
    ("sel_w1", (DC, P)), ("route_scale", (1,)),
    ("router_w2", (DC, 8)), ("router_b2", (8,)), ("b1_2", (8, 8)), ("b2_2", (D,)),
    ("proj2", (DC, 16)), ("C1", (P,)), ("C2", (P,)), ("Win1", (DC, P)), ("win1_b", (1,)),
    ("Wout1", (8, P)), ("Win2", (8, P)), ("win2_b", (1,)), ("Wout2", (D,)),
    ("q_w3", (DC, D)), ("k_w3", (DC, D)), ("v_w3", (DC, D)), ("q_b3", (DC,)), ("k_b3", (DC,)), ("v_b3", (D,)),
    ("router_w3", (DC, 8)), ("router_b3", (8,)), ("b1_3", (9, 8)), ("b2_3", (D,)), ("sh_b2_3", (D,)),
]



def rsqrt(m, out, in_, eps, ready):
    n = out.shape[-1]
    e = m.VV(m.dve.tensor_scalar(out, in_, eps, None, ALU.add))
    m.wait(m.pool, e, m.filled)
    done = m.Q(m.pool.tensor_tensor(out, out, m.minus_half[:, 0:n], ALU.pow))
    m.wait(m.dve, done)
    return done


def transposed(m, dst, tiles, ready):
    last = None
    marks = []
    for c in range(DC):
        bank, free = m.banks.take()
        m.wait(m.pe, ready, m.const_ready, *free)
        for j in range(G):
            last = m.pe.transpose(m.psum[:, bank, j * P:(j + 1) * P], tiles[:, j, c * P:(c + 1) * P], m.ident[:, :])
        full = m.M(last)
        m.wait(m.act, full)
        last = m.A(m.act.activation(dst[:, c, :], m.psum[:, bank, :], ACT.Copy))
        m.banks.freed[bank] = (last,)
        marks.append(last)
    return marks[-1]


def layernorm(m, xt_free, keep=None, fm=True, add_back=False, to=None):
    dve = m.dve
    ready, m.ln_ready = [], []
    for g in range(NG):
        tiles = slice(g * G, (g + 1) * G)
        if m.arriving:
            m.arriving.need(g)
        m.wait(dve, *m.x_ready[tiles])
        for j in range(G):
            st = dve.bn_stats(m.ln_stats[:, j, :], m.X[:, g * G + j, :])
        m.VV(st)
        for j in range(G):
            ag = dve.bn_aggr(m.ln_mv[:, j, :], m.ln_stats[:, j, :])
        m.VV(ag)
        rsqrt(m, m.ln_rstd[:, :], m.ln_mv[:, :, 1], LN_EPS, None)
        if keep is None:
            slot, free = m.ln_ring.take()
            m.wait(dve, *free)
            dst = m.LN[:, slot]
        else:
            dst = keep[:, tiles, :]
        for j in range(G):
            done = m.V(dve.tensor_scalar(dst[:, j, :], m.X[:, g * G + j, :], m.ln_mv[:, j, 0:1],
                                         m.ln_rstd[:, j:j + 1], ALU.subtract, ALU.mult))
        m.ln_ready.append(done)
        if add_back:
            m.wait(dve, done)
            added = m.V(dve.tensor_tensor(m.X[:, tiles, :], m.X[:, tiles, :], dst, ALU.add))
            m.x_ready[g * G:(g + 1) * G] = [added] * G
        if fm:
            m.wait(m.act, *xt_free)
            ready.append(to(g, dst, done) if to else transposed(m, m.XT[:, :, g * GT:(g + 1) * GT], dst, done))
        if keep is None:
            m.ln_ring.freed[slot] = (ready[-1],)
    return ready


def top2(m, probs, ready):
    dve = m.dve
    n = probs.shape[1]
    shape = [P, n, 8]
    m.wait(dve, ready, m.filled)
    rank = bcast(m.rank8[:, :].unsqueeze(1), *shape)
    key = m.top_key[:, 0:n, :]
    best = m.top_best[:, 0:n]
    for k in range(2):
        val, hot = m.top_v[:, k, 0:n], m.top_h[:, k, 0:n, :]
        m.VV(dve.tensor_reduce(val, probs, AX.X, ALU.max))
        m.VV(dve.tensor_tensor(key, probs, bcast(val.unsqueeze(2), *shape), ALU.is_equal))
        m.VV(dve.tensor_tensor(key, key, rank, ALU.mult))
        m.VV(dve.tensor_reduce(best, key, AX.X, ALU.max))
        m.VV(dve.tensor_tensor(hot, key, bcast(best.unsqueeze(2), *shape), ALU.is_equal))
        if k == 0:
            m.VV(dve.scalar_tensor_tensor(out=probs, in0=hot, scalar=LOWEST, in1=probs, op0=ALU.mult, op1=ALU.add))


def combine(m, out, n):
    dve = m.dve
    shape = [P, n, 8]
    m.VV(dve.tensor_tensor(m.top_key[:, 0:n, :], m.top_h[:, 0, 0:n, :], bcast(m.top_v[:, 0, 0:n].unsqueeze(2), *shape), ALU.mult))
    m.VV(dve.tensor_tensor(out, m.top_h[:, 1, 0:n, :], bcast(m.top_v[:, 1, 0:n].unsqueeze(2), *shape), ALU.mult))
    return m.VV(dve.tensor_tensor(out, out, m.top_key[:, 0:n, :], ALU.add))


def router_logits(m, act_fm, ready, w, n):
    bank, free = m.banks.take()
    m.wait(m.pe, m.small_ready, *free)
    for t in range(T):
        m.wait(m.pe, ready[t // G])
        for c in range(DC):
            mm = m.pe.matmul(m.psum[:, bank, t * n:(t + 1) * n], act_fm[:, c, t * P:(t + 1) * P], w[:, c, 0:n],
                             start=(c == 0), stop=(c == DC - 1))
    return bank, m.M(mm)


def softmax8(m, logits):
    dve = m.dve
    shape = [P, T, 8]
    m.VV(dve.tensor_reduce(m.top_best[:, 0:T], logits, AX.X, ALU.max))
    sub = m.V(dve.tensor_tensor(logits, logits, bcast(m.top_best[:, 0:T].unsqueeze(2), *shape), ALU.subtract))
    m.wait(m.act, sub)
    ex = m.A(m.act.activation(logits, logits, ACT.Exp))
    m.wait(dve, ex)
    m.VV(dve.tensor_reduce(m.top_best[:, 0:T], logits, AX.X, ALU.add))
    m.VV(dve.reciprocal(m.top_best[:, 0:T], m.top_best[:, 0:T]))
    return m.VV(dve.tensor_tensor(logits, logits, bcast(m.top_best[:, 0:T].unsqueeze(2), *shape), ALU.mult))


class Weights:

    def __init__(self, m, name, ctx, slots, size):
        self.m, self.size = m, size
        self.buf = m.sb("weights" + name, [P, slots, size], F32, ctx)
        self.ring = Ring(slots)
        self.counters = [m.counter(f"load_w{name}{i}", 16) for i in range(slots)]

    def load(self, *sources):
        slot, free = self.ring.take()
        self.m.wait(self.m.sp, *free)
        at, views = 0, []
        for src in sources:
            n = src.shape[1]
            view = self.buf[:, slot, at:at + n]
            mark = self.counters[slot].after(self.m.sp.dma_start(view, src))
            views.append(view)
            at += n
        assert at <= self.size
        return slot, views, mark



def experts(m, xt_ready, F, sources, gates, gates_ready, hidden):
    FC = F // P
    PAIR, WIDE = 2, 2 * P
    last = T // PAIR - 1
    steps = [(e, g) for e in range(len(sources)) for g in range(T // PAIR)]
    loaded = {}

    def up(e, g):
        if g == 0:
            slot, (w1, w2), mark = m.W.load(*sources[e])
            loaded[e] = (slot, w1.rearrange("p (c f) -> p c f", c=DC), w2.rearrange("p (c d) -> p c d", c=FC), mark)
        slot, w1, w2, mark = loaded[e]
        h_slot, h_free = m.h_ring.take()
        m.wait(m.pe, mark, xt_ready[g * PAIR // G])
        m.wait(m.act, *h_free)
        marks = []
        for f in range(FC):
            bank, free = m.banks.take()
            m.wait(m.pe, *free)
            for c in range(DC):
                mm = m.pe.matmul(m.psum[:, bank, 0:WIDE], w1[:, c, f * P:(f + 1) * P], m.XT[:, c, g * WIDE:(g + 1) * WIDE],
                                 start=(c == 0), stop=(c == DC - 1))
            m.wait(m.act, m.M(mm))
            freed, done = hidden(m.psum[:, bank, 0:WIDE], m.H[:, h_slot, f, :], e, f)
            m.banks.freed[bank] = (freed,)
            marks.append(done)
        return h_slot, marks

    def down(e, g, h_slot, h_marks):
        slot, w1, w2, mark = loaded[e]
        bank, free = m.banks.take()
        m.wait(m.pe, *free)
        for j in range(PAIR):
            for f in range(FC):
                m.wait(m.pe, h_marks[f])
                mm = m.pe.matmul(m.psum[:, bank, j * D:(j + 1) * D], m.H[:, h_slot, f, j * P:(j + 1) * P], w2[:, f, :],
                                 start=(f == 0), stop=(f == FC - 1))
        full = m.M(mm)
        m.wait(m.dve, full, gates_ready)
        for j in range(PAIR):
            t = g * PAIR + j
            m.wait(m.dve, m.x_ready[t])
            gate = gates(t, e)
            src = m.psum[:, bank, j * D:(j + 1) * D]
            if gate is None:
                added = m.V(m.dve.tensor_tensor(m.X[:, t, :], src, m.X[:, t, :], ALU.add))
            else:
                added = m.V(m.dve.scalar_tensor_tensor(out=m.X[:, t, :], in0=src, scalar=gate, in1=m.X[:, t, :],
                                                       op0=ALU.mult, op1=ALU.add))
            m.x_ready[t] = added
        m.banks.freed[bank] = (added,)
        m.h_ring.freed[h_slot] = (full,)
        if g == last:
            m.W.ring.freed[slot] = (full,)
        return full

    pending = None
    for e, g in steps:
        now = (e, g) + up(e, g)
        if pending:
            down(*pending)
        pending = now
    down(*pending)



STEP = 2 * P
NSTEP = T * P // STEP
ALWAYS = 2 * T * P // 8 // STEP


def skip(m, engine, counter, before):
    if before:
        engine.wait_ge(counter.sem, before)
    engine.sem_inc(counter.sem, counter.value - before)


class Sparse:

    def __init__(self, m, name, ctx, FC):
        def sb(n, shape, dt=F32):
            return m.sb(name + n, shape, dt, ctx)
        self.FC = FC
        self.LN = sb("_ln", [P, T, D])
        self.H = sb("_h", [P, 2, FC, STEP])
        self.h_ring = Ring(2)
        self.XS = sb("_xs", [P, 3, 2, D])
        self.xs_ring = Ring(3)
        self.XST = sb("_xst", [P, 3, DC, STEP])
        self.xst_ring = Ring(3)
        self.YS = sb("_ys", [P, 2, 2, D])
        self.ys_ring = Ring(2)
        self.posf = sb("_posf", [P, 2, T])
        self.count = sb("_count", [P, 8], I32)
        self.S_xs = [m.counter(f"{name}_load_x{i}", 16) for i in range(3)]
        self.S_ys = [m.counter(f"{name}_store_y{i}", 16) for i in range(2)]
        self.S_scatter = m.counter(name + "_scatter", 16)


def places(m, s):
    pe, dve = m.pe, m.dve
    hot = m.top_h[:, :, 0:T, :]
    mask = m.top_key[:, 0:T, :]
    flat = mask.rearrange("p t e -> p (t e)")
    picked = m.VV(dve.tensor_tensor(mask, hot[:, 0], hot[:, 1], ALU.add))
    bank, free = m.banks.take()
    m.wait(pe, picked, m.const_ready, *free)
    pe.matmul(m.psum[:, bank, 0:P], m.tri_excl[:, :], flat, start=True, stop=True)
    both = m.M(pe.matmul(m.psum[:, bank, P:2 * P], bcast(m.ones[:, :], P, P), flat, start=True, stop=True))
    m.wait(dve, both)
    total = m.psum[:, bank, P:2 * P].rearrange("p (t e) -> p t e", t=T)
    m.wait(dve, m.zeroed)
    cum = m.cum
    m.VV(dve.tensor_copy(cum[:, 0], total))
    for k in range(4):
        x, y, d = cum[:, k % 2], cum[:, 1 - k % 2], 1 << k
        dve.tensor_copy(y[:, 0:d, :], x[:, 0:d, :])
        m.VV(dve.tensor_tensor(y[:, d:, :], x[:, d:, :], x[:, 0:T - d, :], ALU.add))
    counted = m.VV(dve.tensor_copy(s.count[:, :], cum[:, 0, T - 1, :]))
    m.VV(dve.tensor_tensor(cum[:, 1], cum[:, 0], total, ALU.subtract))
    got = m.VV(dve.tensor_tensor(cum[:, 1], cum[:, 1], m.psum[:, bank, 0:P].rearrange("p (t e) -> p t e", t=T), ALU.add))
    m.banks.freed[bank] = (got,)
    m.VV(dve.tensor_tensor(cum[:, 1], cum[:, 1], bcast(m.expert_row[:, :].unsqueeze(1), P, T, 8), ALU.add))
    for k in range(2):
        m.VV(dve.tensor_tensor(cum[:, 0], cum[:, 1], hot[:, k], ALU.mult))
        m.VV(dve.tensor_reduce(s.posf[:, k, :], cum[:, 0], AX.X, ALU.add))
    return counted, m.VV(dve.tensor_copy(m.pos[:, :, :], s.posf[:, :, :]))


def scatter(m, s, pos_ready):
    m.wait(m.pool, m.zeroed, pos_ready)
    for t in range(T):
        m.wait(m.pool, m.ln_ready[t // G])
        for k in range(2):
            done = s.S_scatter.after(m.pool.indirect_dma_start(
                m.x_table, bass.IndirectOffsetOnAxis(m.pos[:, k, t:t + 1], 0), s.LN[:, t, :], None))
    return done


def sparse_experts(m, s, scattered, counted, sources, hidden):
    pe, act, dve, sp, FC = m.pe, m.act, m.dve, m.sp, s.FC
    x_rows = m.x_table.rearrange("(n a p) d -> n p a d", a=2, p=P)
    y_rows = m.y_table.rearrange("(n a p) d -> n p a d", a=2, p=P)
    engines = (pe, act, sp, m.pool, m.dve)
    m.wait(sp, m.zeroed)
    for eng in engines:
        m.wait(eng, counted)
    counts = [m.nc.values_load(s.count[0:1, e:e + 1], engines=[eng.engine for eng in engines], min_val=0, max_val=T * P)
              for e in range(8)]
    banks, ybank = Ring(6), Ring(1)
    banks.freed = [m.banks.freed[b] for b in range(6)]
    ybank.freed = [tuple(m.banks.freed[6]) + tuple(m.banks.freed[7])]
    LAG = 2

    def load_rows(e, j):
        i, x_free = s.xs_ring.take()
        m.wait(sp, scattered, *x_free)
        return i, s.S_xs[i].after(sp.dma_start(s.XS[:, i], x_rows[e * NSTEP + j]))

    def turn_rows(i, loaded):
        o, xst_free = s.xst_ring.take()
        bank, free = banks.take()
        m.wait(pe, loaded, m.const_ready, *free)
        for c in range(DC):
            for a in range(2):
                mm = pe.transpose(m.psum[:, bank, (c * 2 + a) * P:(c * 2 + a + 1) * P],
                                  s.XS[:, i, a, c * P:(c + 1) * P], m.ident[:, :])
        turned = m.M(mm)
        s.xs_ring.freed[i] = (turned,)
        m.wait(act, turned, *xst_free)
        ready = m.A(act.activation(s.XST[:, o].rearrange("p c k -> p (c k)"), m.psum[:, bank, :], ACT.Copy))
        banks.freed[bank] = (ready,)
        return o, ready

    weights = [m.W.load(*sources[0])]
    first = [turn_rows(*load_rows(0, 0))]
    second = [load_rows(0, 1)]
    for e in range(8):
        if e < 7:
            weights.append(m.W.load(*sources[e + 1]))
        w_slot, (w1, w2), w_ready = weights[e]
        w1 = w1.rearrange("p (c f) -> p c f", c=DC)
        w2 = w2.rearrange("p (c d) -> p c d", c=FC)
        m.wait(pe, w_ready)
        def body(j, x):
            o, x_ready = x
            y, ys_free = s.ys_ring.take()
            h, h_free = s.h_ring.take()
            yb, yb_free = ybank.take()
            rows_first = None
            if j == 0:
                rows = second[e]
                if e < 7:
                    rows_first = load_rows(e + 1, 0)
                    second.append(load_rows(e + 1, 1))
            else:
                rows = load_rows(e, j + 1) if j + 1 < NSTEP else None
            m.wait(act, *h_free)
            m.wait(pe, x_ready)
            h_marks = []

            def down(f):
                m.wait(pe, h_marks[f])
                for a in range(2):
                    mm = pe.matmul(m.psum[:, 6 + a, 0:D], s.H[:, h, f, a * P:(a + 1) * P], w2[:, f, :],
                                   start=(f == 0), stop=(f == FC - 1))
                return mm

            for f in range(FC):
                bank, free = banks.take()
                m.wait(pe, *free)
                for c in range(DC):
                    mm = pe.matmul(m.psum[:, bank, 0:STEP], w1[:, c, f * P:(f + 1) * P], s.XST[:, o, c, :],
                                   start=(c == 0), stop=(c == DC - 1))
                up_done = m.M(mm)
                m.wait(act, up_done)
                freed, done = hidden(m.psum[:, bank, 0:STEP], s.H[:, h, f, 0:STEP], e, f)
                banks.freed[bank] = (freed,)
                h_marks.append(done)
                if f >= LAG:
                    if f == LAG:
                        m.wait(pe, *yb_free)
                    down(f - LAG)
            s.xst_ring.freed[o] = (up_done,)
            coming = turn_rows(*rows) if rows else None
            if rows_first:
                first.append(turn_rows(*rows_first))
            for f in range(FC - LAG, FC):
                mm = down(f)
            y_full = m.M(mm)
            s.h_ring.freed[h] = (y_full,)
            m.wait(dve, y_full, *ys_free)
            y_out = m.V(dve.tensor_copy(s.YS[:, y], m.psum[:, 6:8, 0:D]))
            ybank.freed[yb] = (y_out,)
            m.wait(sp, y_out)
            s.ys_ring.freed[y] = (s.S_ys[y].after(sp.dma_start(y_rows[e * NSTEP + j], s.YS[:, y])),)
            return coming, y_full

        def branch(j, x):
            counting = [(pe, m.S_pe), (act, m.S_act), (dve, m.S_dve)] + [(sp, c) for c in s.S_xs] + [(sp, c) for c in s.S_ys]
            before = [c.value for _, c in counting]
            with m.nc.If(counts[e] > j * STEP):
                x, y_full = body(j, x)
                if j + 1 < NSTEP:
                    y_full = branch(j + 1, x)
            with m.nc.Else():
                for (engine, counter), value in zip(counting, before):
                    if counter.value > value:
                        skip(m, engine, counter, value)
            return y_full

        x = first[e]
        for j in range(ALWAYS):
            x, y_full = body(j, x)
        seen = dict(m.seen)
        y_full = branch(ALWAYS, x)
        m.seen = seen
        m.W.ring.freed[w_slot] = (y_full,)
    m.banks.freed = banks.freed + [ybank.freed[0]] * 2
    return y_full, (s.ys_ring.freed[0] + s.ys_ring.freed[1])


class Gather:

    SLOTS = 4 * G

    def __init__(self, m, name, stores):
        self.m, self.name, self.stores, self.asked, self.added = m, name, stores, 0, 0

    def open(self):
        m = self.m
        ctx = self.stack = ExitStack()
        self.rows = m.sb(self.name + "_rows", [P, self.SLOTS, D], F32, ctx)
        self.counters = [m.counter(f"{self.name}_gather{i}", 16) for i in range(self.SLOTS)]
        self.freed = [()] * self.SLOTS
        m.wait(m.pool, *self.stores)
        self.ask(0)

    def close(self):
        self.m.barrier()
        self.stack.close()
        self.m.arriving = None

    def slot(self, t, k):
        return (2 * t + k) % self.SLOTS

    def ask(self, g):
        m = self.m
        for t in range(g * G, min((g + 1) * G, T)):
            for k in range(2):
                i = self.slot(t, k)
                m.wait(m.pool, *self.freed[i])
                self.freed[i] = (self.counters[i].after(m.pool.indirect_dma_start(
                    self.rows[:, i, :], None, m.y_table, bass.IndirectOffsetOnAxis(m.pos[:, k, t:t + 1], 0))),)

    def need(self, g):
        m = self.m
        for n in range(self.added, g + 1):
            self.ask(n + 1)
            for k in range(2):
                for t in range(n * G, (n + 1) * G):
                    i = self.slot(t, k)
                    m.wait(m.dve, *self.freed[i], m.x_ready[t])
                    m.x_ready[t] = m.V(m.dve.scalar_tensor_tensor(out=m.X[:, t, :], in0=self.rows[:, i, :], scalar=m.top_v[:, k, t:t + 1],
                                                                  in1=m.X[:, t, :], op0=ALU.mult, op1=ALU.add))
                    self.freed[i] = (m.x_ready[t],)
            self.added = n + 1


def layer0_ffn(m, ins, scratch):
    m.layer("ffn0")
    s = Sparse(m, "ffn0", scratch, 4)
    xt = layernorm(m, m.xt_free, keep=s.LN)
    bank, logits = router_logits(m, m.XT, xt, m.small["router_w0"], 8)
    m.wait(m.dve, logits)
    probs = m.route[:, :, :]
    copied = m.VV(m.dve.tensor_copy(probs, m.psum[:, bank, 0:T * 8].rearrange("p (t e) -> p t e", t=T)))
    m.banks.freed[bank] = (copied,)
    top2(m, probs, softmax8(m, probs))
    counted, pos_ready = places(m, s)
    scattered = scatter(m, s, pos_ready)
    v = m.top_v
    m.VV(m.dve.tensor_tensor(m.top_best[:, 0:T], v[:, 0, 0:T], v[:, 1, 0:T], ALU.add))
    m.VV(m.dve.reciprocal(m.top_best[:, 0:T], m.top_best[:, 0:T]))
    m.VV(m.dve.tensor_tensor(v[:, :, 0:T], v[:, :, 0:T], bcast(m.top_best[:, 0:T].unsqueeze(1), P, 2, T), ALU.mult))

    def hidden(src, out, e, f):
        relu = m.A(m.act.activation(out, src, ACT.Relu))
        m.wait(m.act, relu)
        return relu, m.A(m.act.activation(out, out, ACT.Square))

    end, stores = sparse_experts(m, s, scattered, counted, [(ins["ffn0_w1"][e], ins["ffn0_w2"][e]) for e in range(8)], hidden)
    m.arriving = Gather(m, "ffn0", stores)
    m.xt_free = (end,)


def gate_bias(m, b2, ready):
    pair = Ring(1)
    for t in range(0, T, 2):
        i, pair_free = pair.take()
        bank, free = m.banks.take()
        m.wait(m.pe, ready, m.const_ready, *free)
        for j in range(2):
            mm = m.pe.transpose(m.psum[0:8, bank, j * P:(j + 1) * P], m.gates[:, t + j, :], m.ident[:, :])
        m.wait(m.dve, m.M(mm), *pair_free)
        gt = m.V(m.dve.tensor_copy(m.gates_fm[:, i, :], m.psum[0:8, bank, 0:2 * P]))
        m.banks.freed[bank] = (gt,)
        bank, free = m.banks.take()
        m.wait(m.pe, gt, m.small_ready, *free)
        for j in range(2):
            mm = m.pe.matmul(m.psum[:, bank, j * D:(j + 1) * D], m.gates_fm[:, i, j * P:(j + 1) * P], b2[0:8, :],
                             start=True, stop=True)
        used = m.M(mm)
        pair.freed[i] = (used,)
        m.wait(m.dve, used, m.x_ready[t], m.x_ready[t + 1])
        added = m.V(m.dve.tensor_tensor(m.X[:, t:t + 2, :], m.X[:, t:t + 2, :],
                                        m.psum[:, bank, :].rearrange("p (j d) -> p j d", j=2), ALU.add))
        m.banks.freed[bank] = (added,)
        m.x_ready[t:t + 2] = [added] * 2


def layer2_mix(m, ins, scratch):
    m.layer("mix2")
    s = Sparse(m, "mix2", scratch, 8)
    bank, logits = router_logits(m, m.CTXT, m.ctxt_ready, m.small["router_w2"], 8)
    m.wait(m.dve, logits)
    lg = m.route[:, :, :]
    added = m.VV(m.dve.tensor_tensor(lg, m.psum[:, bank, 0:T * 8].rearrange("p (t e) -> p t e", t=T),
                                     bcast(m.small["router_b2"][:, :].unsqueeze(1), P, T, 8), ALU.add))
    m.banks.freed[bank] = (added,)
    top2(m, lg, added)
    counted, pos_ready = places(m, s)
    layernorm(m, (), keep=s.LN, fm=False)
    scattered = scatter(m, s, pos_ready)
    v = m.top_v
    m.VV(m.dve.tensor_tensor(v[:, 1, 0:T], v[:, 1, 0:T], v[:, 0, 0:T], ALU.subtract))
    m.wait(m.act, m.VV(m.dve.tensor_tensor(v[:, 0, 0:T], v[:, 0, 0:T], v[:, 0, 0:T], ALU.subtract)))
    m.wait(m.dve, m.A(m.act.activation(v[:, :, 0:T], v[:, :, 0:T], ACT.Exp)))
    m.VV(m.dve.tensor_tensor(m.top_best[:, 0:T], v[:, 0, 0:T], v[:, 1, 0:T], ALU.add))
    m.VV(m.dve.reciprocal(m.top_best[:, 0:T], m.top_best[:, 0:T]))
    m.VV(m.dve.tensor_tensor(v[:, :, 0:T], v[:, :, 0:T], bcast(m.top_best[:, 0:T].unsqueeze(1), P, 2, T), ALU.mult))
    gates_ready = combine(m, m.gates[:, :, :], T)
    gate_bias(m, m.small["b2_2"], gates_ready)

    def hidden(src, out, e, f):
        done = m.A(m.act.activation(out, src, ACT.Relu, bias=m.small["b1_2"][:, e, f:f + 1]))
        return done, done

    end, stores = sparse_experts(m, s, scattered, counted, [(ins["mix2_w1"][e], ins["mix2_w2"][e]) for e in range(8)], hidden)
    m.arriving = Gather(m, "mix2", stores)


def layer3_ffn(m, ins, scratch):
    m.layer("ffn3")
    s = Sparse(m, "ffn3", scratch, 8)
    xt = layernorm(m, m.xt_free, keep=s.LN, add_back=True)
    bank, logits = router_logits(m, m.XT, xt, m.small["router_w3"], 8)
    m.wait(m.dve, logits)
    probs = m.route[:, :, :]
    added = m.VV(m.dve.tensor_tensor(probs, m.psum[:, bank, 0:T * 8].rearrange("p (t e) -> p t e", t=T),
                                     bcast(m.small["router_b3"][:, :].unsqueeze(1), P, T, 8), ALU.add))
    m.banks.freed[bank] = (added,)
    top2(m, probs, softmax8(m, probs))
    counted, pos_ready = places(m, s)
    scattered = scatter(m, s, pos_ready)
    v = m.top_v
    m.VV(m.dve.tensor_tensor(m.top_best[:, 0:T], v[:, 0, 0:T], v[:, 1, 0:T], ALU.add))
    m.VV(m.dve.tensor_scalar(m.top_best[:, 0:T], m.top_best[:, 0:T], 1e-9, None, ALU.add))
    m.VV(m.dve.reciprocal(m.top_best[:, 0:T], m.top_best[:, 0:T]))
    m.VV(m.dve.tensor_tensor(v[:, :, 0:T], v[:, :, 0:T], bcast(m.top_best[:, 0:T].unsqueeze(1), P, 2, T), ALU.mult))
    gates_ready = combine(m, m.gates[:, :, :], T)
    gate_bias(m, m.small["b2_3"], gates_ready)
    for t in range(T):
        m.wait(m.dve, m.x_ready[t])
        m.x_ready[t] = m.V(m.dve.tensor_tensor(m.X[:, t, :], m.X[:, t, :], m.small["sh_b2_3"][:, :], ALU.add))

    def hidden(src, out, e, f):
        done = m.A(m.act.activation(out, src, ACT.Gelu_apprx_tanh, bias=m.small["b1_3"][:, e, f:f + 1]))
        return done, done

    m.H, m.h_ring = s.H, s.h_ring
    experts(m, xt, 1024, [(ins["ffn3_w1"][0], ins["ffn3_w2"][0])], lambda t, e: None, gates_ready, hidden)
    end, stores = sparse_experts(m, s, scattered, counted, [(ins["ffn3_w1"][e], ins["ffn3_w2"][e]) for e in range(1, 9)],
                                 lambda src, out, e, f: hidden(src, out, e + 1, f))
    m.arriving = Gather(m, "ffn3", stores)
    m.xt_free = (end,)



def layer0_mix(m, ins, scratch):
    NH, DH, HB = 4, 64, T * 4
    DEPTH = 3
    m.layer("mix0")
    pe, dve, act, pool = m.pe, m.dve, m.act, m.pool
    with ExitStack() as scratch:
        def sb(name, shape):
            return m.sb(name, shape, F32, scratch)
        gf = sb("gate_pre", [P, T, 8])
        fneg, fexp, lf, a, cs = (sb(n, [P, T, NH]) for n in ("f_neg", "f_exp", "log_f", "a_col", "cs_col"))
        floor = sb("norm_floor", [P, T, NH])
        PAD = 64
        scan = [sb(f"scan{i}", [HB, PAD + P]) for i in range(2)]
        dist = sb("dist", [P, DEPTH, NH, P])
        E = sb("decay", [P, DEPTH, NH, P])
        C = sb("weights_t", [P, DEPTH, NH, P])
        sums, nrm = sb("c_sum", [P, DEPTH, NH]), sb("normaliser", [P, DEPTH, NH])
        h = sb("h_tile", [P, DEPTH, NH, DH])
        hst, hmv, hr = sb("h_stats", [P, DEPTH, NH, 6]), sb("h_mv", [P, DEPTH, NH, 2]), sb("h_rstd", [P, DEPTH, NH])
        scale1 = sb("out_scale", [P, D])

        m.ctxt_ready = []
        for g in range(NG):
            m.ctxt_ready.append(transposed(m, m.CTXT[:, :, g * GT:(g + 1) * GT], m.CTX[:, g * G:(g + 1) * G, :], m.ctx_ready))
        xt = layernorm(m, m.xt_free)

        bank, free = m.banks.take()
        m.wait(pe, m.first_ready, *free)
        for t in range(T):
            m.wait(pe, xt[t // G], m.ctxt_ready[t // G])
            for c in range(6):
                src = m.XT if c < 2 else m.CTXT
                mm = pe.matmul(m.psum[:, bank, t * 8:(t + 1) * 8], src[:, c % 2, t * P:(t + 1) * P],
                               m.small["gate_w0"][:, c, :], start=(c == 0), stop=(c == 5))
        m.wait(dve, m.M(mm), m.first_ready)
        m.VV(dve.tensor_scalar(scale1[:, :], m.small["head_scale0"][:, :], 1.0, None, ALU.add))
        added = m.VV(dve.tensor_tensor(gf[:, :, :], m.psum[:, bank, 0:T * 8].rearrange("p (t e) -> p t e", t=T),
                                       bcast(m.small["gate_b0"][:, :].unsqueeze(1), P, T, 8), ALU.add))
        m.banks.freed[bank] = (added,)
        f = gf[:, :, NH:2 * NH]
        neg = m.V(dve.scalar_tensor_tensor(out=fneg[:, :, :], in0=f, scalar=-1.0, in1=f, op0=ALU.mult, op1=ALU.min))
        m.wait(act, neg)
        m.wait(act, m.A(act.activation(fexp[:, :, :], fneg[:, :, :], ACT.Exp)))
        log = m.A(act.activation(fexp[:, :, :], fexp[:, :, :], ACT.Ln, bias=1.0))
        m.wait(dve, log)
        lfr = m.V(dve.scalar_tensor_tensor(out=lf[:, :, :], in0=f, scalar=0.0, in1=fexp[:, :, :], op0=ALU.min, op1=ALU.subtract))
        bank, free = m.banks.take()
        m.wait(pe, lfr, m.const_ready, *free)
        flat = lf[:, :, :].rearrange("p t h -> p (t h)")
        pe.matmul(m.psum[:, bank, 0:HB], m.tri_incl[:, :], flat, start=True, stop=True)
        m.wait(dve, m.M(pe.matmul(m.psum[:, bank, HB:2 * HB], m.tri_excl[:, :], flat, start=True, stop=True)))
        dve.tensor_copy(cs[:, :, :], m.psum[:, bank, 0:HB].rearrange("p (t h) -> p t h", t=T))
        ar = m.VV(dve.tensor_tensor(a[:, :, :], gf[:, :, 0:NH],
                                    m.psum[:, bank, HB:2 * HB].rearrange("p (t h) -> p t h", t=T), ALU.subtract))
        m.banks.freed[bank] = (ar,)
        bank, free = m.banks.take()
        m.wait(pe, ar, *free)
        tr = m.M(pe.transpose(m.psum[0:HB, bank, 0:P], a[:, :, :].rearrange("p t h -> p (t h)"), m.ident[:, :]))
        dve.memset(scan[0][:, 0:PAD], LOWEST)
        dve.memset(scan[1][:, 0:PAD], LOWEST)
        m.wait(dve, tr)
        got = m.VV(dve.tensor_copy(scan[0][:, PAD:], m.psum[0:HB, bank, 0:P]))
        m.banks.freed[bank] = (got,)
        for k in range(7):
            x, y, s = scan[k % 2], scan[1 - k % 2], 1 << k
            got = m.VV(dve.tensor_tensor(y[:, PAD:], x[:, PAD:], x[:, PAD - s:PAD - s + P], ALU.max))
        top = scan[7 % 2][:, PAD:]
        bank, free = m.banks.take()
        m.wait(pe, got, *free)
        tr = m.M(pe.transpose(m.psum[:, bank, 0:HB], top, m.ident[0:HB, 0:HB]))
        m.wait(dve, tr)
        fl = m.V(dve.tensor_tensor(floor[:, :, :], cs[:, :, :], m.psum[:, bank, 0:HB].rearrange("p (t h) -> p t h", t=T), ALU.add))
        m.banks.freed[bank] = (fl,)
        m.wait(act, fl)
        floor_ready = m.A(act.activation(floor[:, :, :], floor[:, :, :], ACT.Exp, scale=-1.0))

        tail = [()] * DEPTH

        def batch(b):
            i = b % DEPTH
            tok = slice(b * P, (b + 1) * P)
            bm, free = m.banks.take()
            m.wait(pe, got, *free)
            for hd in range(NH):
                r = b * NH + hd
                mm = pe.matmul(m.psum[:, bm, hd * P:(hd + 1) * P], bcast(m.ident[0:HB, r:r + 1], HB, P), top, start=True, stop=True)
            max_full = m.M(mm)
            yield
            m.wait(dve, max_full)
            for hd in range(NH):
                far = m.V(dve.tensor_scalar(dist[:, i, hd, :], m.psum[:, bm, hd * P:(hd + 1) * P], a[:, b, hd:hd + 1], 0.0,
                                            ALU.subtract, ALU.max))
            m.banks.freed[bm] = (far,)
            m.wait(act, far, *tail[i])
            ex = m.A(act.activation(E[:, i], dist[:, i], ACT.Exp, scale=-1.0))
            m.wait(pool, ex)
            cut = m.Q(pool.affine_select(out=E[:, i], in_=E[:, i], compare_op=ALU.is_ge, fill=0.0,
                                         base=0, pattern=[[0, NH], [1, P]], channel_multiplier=-1))
            qk = []
            for lo in range(2):
                bq, free = m.banks.take()
                m.wait(pe, *free)
                for c in range(DC):
                    part = slice(lo * DH, (lo + 1) * DH)
                    mm = pe.matmul(m.psum[:, bq, c * P:(c + 1) * P], m.CTXT[part, c, tok], m.XT[part, c, tok], start=True, stop=True)
                qk.append((bq, m.M(mm)))
            yield
            m.wait(dve, cut)
            for lo, (bq, full) in enumerate(qk):
                m.wait(dve, full)
                c_ready = m.V(dve.scalar_tensor_tensor(
                    out=C[:, i, lo::2, :], in0=m.psum[:, bq, 0:2 * P].rearrange("p (c s) -> p c s", c=DC),
                    scalar=DH ** -0.5, in1=E[:, i, lo::2, :], op0=ALU.mult, op1=ALU.mult))
                m.banks.freed[bq] = (c_ready,)
            bo, free = m.banks.take()
            m.wait(pe, c_ready, *free)
            for hd in range(NH):
                pe.matmul(m.psum[:, bo, hd * DH:(hd + 1) * DH], C[:, i, hd, :], m.CTX[:, b, hd * DH:(hd + 1) * DH], start=True, stop=True)
                mm = pe.matmul(m.psum[:, bo, D + hd:D + hd + 1], C[:, i, hd, :], m.ones[:, :], start=True, stop=True)
            c_used = m.M(mm)
            tail[i] = (c_used,)
            yield
            m.wait(dve, c_used, floor_ready)
            m.VV(dve.tensor_copy(sums[:, i], m.psum[:, bo, D:D + NH]))
            m.VV(dve.scalar_tensor_tensor(out=nrm[:, i], in0=sums[:, i], scalar=-1.0, in1=sums[:, i], op0=ALU.mult, op1=ALU.max))
            m.VV(dve.tensor_tensor(nrm[:, i], nrm[:, i], floor[:, b, :], ALU.max))
            m.VV(dve.tensor_scalar(nrm[:, i], nrm[:, i], 1e-8, None, ALU.add))
            m.VV(dve.reciprocal(nrm[:, i], nrm[:, i]))
            hv = m.VV(dve.tensor_tensor(h[:, i], m.psum[:, bo, 0:D].rearrange("p (h d) -> p h d", h=NH),
                                        bcast(nrm[:, i].unsqueeze(2), P, NH, DH), ALU.mult))
            m.banks.freed[bo] = (hv,)
            for hd in range(NH):
                st = dve.bn_stats(hst[:, i, hd, :], h[:, i, hd, :])
            m.VV(st)
            for hd in range(NH):
                ag = dve.bn_aggr(hmv[:, i, hd, :], hst[:, i, hd, :])
            m.VV(ag)
            e = m.V(dve.tensor_scalar(hr[:, i, :], hmv[:, i, :, 1], LN_EPS, None, ALU.add))
            m.wait(pool, e, m.filled)
            powered = m.Q(pool.tensor_tensor(hr[:, i, :], hr[:, i, :], m.minus_half[:, 0:NH], ALU.pow))
            yield
            m.wait(dve, powered)
            for hd in range(NH):
                nm = dve.tensor_scalar(h[:, i, hd, :], h[:, i, hd, :], hmv[:, i, hd, 0:1], hr[:, i, hd:hd + 1], ALU.subtract, ALU.mult)
            m.wait(pool, m.V(nm))
            hf = h[:, i].rearrange("p h d -> p (h d)")
            scaled = m.Q(pool.tensor_tensor(hf, hf, scale1[:, :], ALU.mult))
            yield
            m.wait(dve, scaled)
            m.x_ready[b] = m.V(dve.tensor_tensor(m.X[:, b, :], m.X[:, b, :], hf, ALU.add))

        interleave([batch(b) for b in range(T)], DEPTH)
        c_used = tail[(T - 1) % DEPTH][0]
        m.xt_free = (c_used,)
        m.barrier()



def layer1_mix(m, ins, scratch):
    NH, DH = 4, 64
    HALF = DH // 2
    HK = NH + 2
    DEPTH = 3
    m.layer("mix1")
    pe, dve, act, pool = m.pe, m.dve, m.act, m.pool

    def sb(name, shape, dt=F32):
        return m.sb(name, shape, dt, scratch)
    S_mask = m.counter("load_mask", 16)
    mask8 = sb("mask8", [P, T * P], U8)
    fill = sb("fill", [P, DEPTH, P])
    scale1 = sb("rms_scale1", [P, D])
    ms = sb("mean_sq", [P, T, 2])
    xn = sb("xn", [P, DEPTH, 2, D])
    xnT = sb("xnT", [P, DEPTH, 2, DC, P])
    qr = sb("q_rot", [P, DEPTH, HK, 2, HALF])
    rot = sb("rot", [P, DEPTH, HK, 2, HALF])
    v = sb("v_tok", [P, DEPTH, DH])
    qT = sb("q_t", [P, DEPTH, 3, P])
    L = sb("logits", [P, DEPTH, NH, P])
    mx, sm = sb("row_max", [P, DEPTH, NH]), sb("row_sum", [P, DEPTH, NH])
    pT = sb("probs_t", [P, DEPTH, NH, P])
    st, mv, rs = sb("l_st", [P, T, 6]), sb("l_mv", [P, T, 2]), sb("l_rs", [P, T])

    mask_ready = S_mask.after(m.sp.dma_start(mask8[:, :], ins["mask"][0].partition_broadcast(P)))
    m.wait(dve, m.small_ready)
    m.VV(dve.tensor_scalar(scale1[:, :], m.small["rms_scale"][:, :], 1.0, None, ALU.add))
    rstd_ready = []

    def prepare(g):
        tiles = slice(g * G, (g + 1) * G)
        if m.arriving:
            m.arriving.need(g)
        m.wait(dve, *m.x_ready[tiles])
        for t in range(g * G, (g + 1) * G):
            s_ = dve.bn_stats(st[:, t, :], m.X[:, t, :])
        m.VV(s_)
        for t in range(g * G, (g + 1) * G):
            s_ = dve.bn_aggr(mv[:, t, :], st[:, t, :])
        m.VV(s_)
        m.wait(pool, m.V(dve.tensor_scalar(rs[:, tiles], mv[:, tiles, 1], LN_EPS, None, ALU.add)), m.filled)
        rstd_ready.append(m.Q(pool.tensor_tensor(rs[:, tiles], rs[:, tiles], m.minus_half[:, 0:G], ALU.pow)))

    prepare(0)
    m.wait(act, m.ctx_ready)

    def batch(b):
        i = b % DEPTH
        tok = slice(b * P, (b + 1) * P)
        if b % G == 1 and b // G + 1 < NG:
            prepare(b // G + 1)
        m.wait(dve, m.ctx_ready, rstd_ready[b // G])
        xl = m.V(dve.tensor_scalar(xn[:, i, 0, :], m.X[:, b, :], mv[:, b, 0:1], rs[:, b:b + 1], ALU.subtract, ALU.mult))
        act.activation(L[:, i, 2:4, :].rearrange("p h s -> p (h s)"), m.CTX[:, b, :], ACT.Square, accum_out=ms[:, b, 1:2])
        m.wait(act, xl)
        squared = m.A(act.activation(L[:, i, 0:2, :].rearrange("p h s -> p (h s)"), xn[:, i, 0, :], ACT.Square, accum_out=ms[:, b, 0:1]))
        yield
        m.wait(dve, squared)
        m.wait(pool, m.V(dve.tensor_scalar(ms[:, b, :], ms[:, b, :], 1.0 / D, RMS_EPS, ALU.mult, ALU.add)))
        powered = m.Q(pool.tensor_tensor(ms[:, b, :], ms[:, b, :], m.minus_half[:, 0:2], ALU.pow))
        yield
        m.wait(dve, powered)
        for k, src in enumerate((xn[:, i, 0, :], m.CTX[:, b, :])):
            nx = m.V(dve.scalar_tensor_tensor(out=xn[:, i, k, :], in0=src, scalar=ms[:, b, k:k + 1], in1=scale1[:, :],
                                              op0=ALU.mult, op1=ALU.mult))
        bank, free = m.banks.take()
        m.wait(pe, nx, m.const_ready, *free)
        for k in range(2):
            for c in range(DC):
                mm = pe.transpose(m.psum[:, bank, (k * DC + c) * P:(k * DC + c + 1) * P], xn[:, i, k, c * P:(c + 1) * P], m.ident[:, :])
        xn_used = m.M(mm)
        yield
        m.wait(act, xn_used)
        xt = m.A(act.activation(xnT[:, i].rearrange("p k c s -> p (k c s)"), m.psum[:, bank, :], ACT.Copy))
        m.banks.freed[bank] = (xt,)
        bank, free = m.banks.take()
        m.wait(pe, xt, m.small_ready, *free)
        for c in range(DC):
            pe.matmul(m.psum[:, bank, 0:D], xnT[:, i, 0, c, :], m.small["q_w1"][:, c, :], start=(c == 0), stop=(c == DC - 1))
        for c in range(DC):
            mm = pe.matmul(m.psum[:, bank, D:D + 3 * DH], xnT[:, i, 1, c, :], m.small["kv_w1"][:, c, :], start=(c == 0), stop=(c == DC - 1))
        qkv = m.M(mm)
        yield
        m.wait(dve, qkv)
        x = m.psum[:, bank, 0:HK * DH].rearrange("p (h t d) -> p h t d", h=HK, t=2)
        cos = bcast(m.small["cos"][:, :, :].unsqueeze(2), P, HK, 2, HALF)
        m.V(dve.tensor_tensor(qr[:, i], x, cos, ALU.mult))
        for half in range(2):
            m.V(dve.tensor_tensor(rot[:, i, :, half, :], x[:, :, 1 - half, :], m.small["sin"][:, :, half, :], ALU.mult))
        vr = m.VV(dve.tensor_copy(v[:, i, :], m.psum[:, bank, HK * DH:(HK + 1) * DH]))
        m.banks.freed[bank] = (vr,)
        qr_ready = m.V(dve.tensor_tensor(qr[:, i], qr[:, i], rot[:, i], ALU.add))
        bank, free = m.banks.take()
        m.wait(pe, qr_ready, *free)
        flat = qr[:, i].rearrange("p h t d -> p (h t d)")
        for c in range(3):
            mm = pe.transpose(m.psum[:, bank, c * P:(c + 1) * P], flat[:, c * P:(c + 1) * P], m.ident[:, :])
        turned = m.M(mm)
        yield
        m.wait(act, turned)
        qt = m.A(act.activation(qT[:, i].rearrange("p c s -> p (c s)"), m.psum[:, bank, 0:3 * P], ACT.Copy))
        m.banks.freed[bank] = (qt,)
        full = []
        for lo in range(2):
            bank, free = m.banks.take()
            m.wait(pe, qt, *free)
            part = slice(lo * DH, (lo + 1) * DH)
            for c in range(DC):
                mm = pe.matmul(m.psum[:, bank, c * P:(c + 1) * P], qT[part, i, c, :], qT[part, i, 2, :], start=True, stop=True)
            full.append((bank, m.M(mm)))
        m.wait(pool, mask_ready, squared)
        filled = m.Q(pool.tensor_scalar(fill[:, i, :], mask8[:, tok], -1.0, -MASK_FILL, ALU.add, ALU.mult))
        yield
        m.wait(dve, squared, mask_ready, filled)
        for lo, (bank, mark) in enumerate(full):
            m.wait(dve, mark)
            lg = m.V(dve.scalar_tensor_tensor(out=L[:, i, lo::2, :], in0=m.psum[:, bank, 0:2 * P].rearrange("p (c s) -> p c s", c=DC),
                                              scalar=DH ** -0.5, in1=bcast(mask8[:, tok].unsqueeze(1), P, 2, P),
                                              op0=ALU.mult, op1=ALU.mult))
            m.banks.freed[bank] = (lg,)
        m.wait(dve, lg)
        m.VV(dve.tensor_tensor(L[:, i], L[:, i], bcast(fill[:, i, :].unsqueeze(1), P, NH, P), ALU.add))
        top = m.V(dve.tensor_reduce(mx[:, i], L[:, i], AX.X, ALU.max, negate=True))
        m.wait(act, top)
        for hd in range(NH):
            ex = m.A(act.activation(L[:, i, hd, :], L[:, i, hd, :], ACT.Exp, bias=mx[:, i, hd:hd + 1], accum_out=sm[:, i, hd:hd + 1]))
        bank, free = m.banks.take()
        m.wait(pe, ex, *free)
        for hd in range(NH):
            mm = pe.transpose(m.psum[:, bank, hd * P:(hd + 1) * P], L[:, i, hd, :], m.ident[:, :])
        turned = m.M(mm)
        yield
        m.wait(dve, ex)
        m.V(dve.reciprocal(sm[:, i], sm[:, i]))
        m.wait(act, turned)
        pt = m.A(act.activation(pT[:, i].rearrange("p h s -> p (h s)"), m.psum[:, bank, :], ACT.Copy))
        m.banks.freed[bank] = (pt,)
        bank, free = m.banks.take()
        m.wait(pe, pt, vr, *free)
        for hd in range(NH):
            mm = pe.matmul(m.psum[:, bank, hd * DH:(hd + 1) * DH], pT[:, i, hd, :], v[:, i, :], start=True, stop=True)
        heads = m.M(mm)
        yield
        enc, encT = xn[:, i, 0, :], xnT[:, i, 0]
        m.wait(dve, heads, (m.S_dve, m.S_dve.value))
        en = m.V(dve.tensor_tensor(enc.rearrange("p (h d) -> p h d", h=NH), m.psum[:, bank, 0:D].rearrange("p (h d) -> p h d", h=NH),
                                   bcast(sm[:, i].unsqueeze(2), P, NH, DH), ALU.mult))
        m.banks.freed[bank] = (en,)
        bank, free = m.banks.take()
        m.wait(pe, en, *free)
        for c in range(DC):
            mm = pe.transpose(m.psum[:, bank, c * P:(c + 1) * P], enc[:, c * P:(c + 1) * P], m.ident[:, :])
        turned = m.M(mm)
        yield
        m.wait(act, turned)
        et = m.A(act.activation(encT.rearrange("p c s -> p (c s)"), m.psum[:, bank, 0:D], ACT.Copy))
        m.banks.freed[bank] = (et,)
        bank, free = m.banks.take()
        m.wait(pe, et, *free)
        for c in range(DC):
            mm = pe.matmul(m.psum[:, bank, 0:D], encT[:, c, :], m.small["out_w1"][:, c, :], start=(c == 0), stop=(c == DC - 1))
        out = m.M(mm)
        yield
        m.wait(dve, out)
        m.x_ready[b] = m.V(dve.tensor_tensor(m.X[:, b, :], m.X[:, b, :], m.psum[:, bank, 0:D], ALU.add))
        m.banks.freed[bank] = (m.x_ready[b],)
        m.wait(act, out)

    interleave([batch(b) for b in range(T)], DEPTH)
    m.barrier()



def split(m, hi, lo, raw, ready, free, lo_engine):
    m.wait(m.act, ready, *free)
    high = m.A(m.act.activation(hi, raw, ACT.Copy))
    m.wait(lo_engine, high)
    rest = lo_engine.tensor_tensor(lo, raw, hi.bitcast(F32), ALU.subtract)
    return m.V(rest) if lo_engine is m.dve else m.Q(rest)


def product(m, out, left, right, start, stop):
    m.pe.matmul(out, left[1], right[0], start=start, stop=False)
    m.pe.matmul(out, left[0], right[0], start=False, stop=False)
    return m.pe.matmul(out, left[0], right[1], start=False, stop=stop)


def layer1_ffn(m, ins, scratch):
    NH, NE, DP = 8, 8, 128
    SCALE = 1.0 / float(DP) ** 0.5
    NQ, NV = 2 * DC * DP, DC * NE * DP
    CH = 512
    m.layer("ffn1")
    pe, dve, act, pool = m.pe, m.dve, m.act, m.pool

    m.wide.close()

    def sb(name, shape, dt=F32):
        return m.sb(name, shape, dt, scratch)
    xt_hi, xt_lo = sb("xt_hi", [P, DC, T * P], F32R), sb("xt_lo", [P, DC, T * P], F32R)
    xt_raw = sb("xt_raw", [P, DC, GT])
    m.LN, m.ln_ring = sb("LN_ffn1", [P, 1, G, D]), Ring(1)
    qk_hi, qk_lo = sb("qk_hi", [P, 2, NQ], F32R), sb("qk_lo", [P, 2, NQ], F32R)
    w_hi, w_lo = sb("w_hi", [P, 2 * NV], F32R), sb("w_lo", [P, 2 * NV], F32R)
    RAW = 6
    raw = sb("w_raw", [P, RAW, CH])
    raw_ring = Ring(RAW)
    S_raw = [m.counter(f"load_raw{k}", 16) for k in range(RAW)]
    gates = sb("gates1", [P, T, 2 * NH, NE])
    den = sb("den1", [P, G * 2 * NH])
    qT, kT = sb("qT1", [P, GT]), sb("kT1", [P, GT])
    v = sb("v1", [P, G, DP])
    cT_hi, cT_lo = sb("cT_hi", [P, GT], F32R), sb("cT_lo", [P, GT], F32R)
    S = sb("scores1", [P, G, P])
    sT = sb("scoresT1", [P, G * P])
    mx, sm = sb("max1", [P, 2, G]), sb("sum1", [P, 2, G])
    out_gate = sb("out_gate", [P, 2, G, NE])
    part_out = sb("part_out", [P, 2, 2, D])
    part_v = sb("part_v", [P, 1, 4, DP])

    gate_pre, raw_free = [], [()]

    def to_parts(g, tiles, ready):
        m.wait(act, *raw_free[-1])
        xt = transposed(m, xt_raw[:, :, :], tiles, ready)
        bank, free = m.banks.take()
        m.wait(pe, m.small_ready, xt, *free)
        for j in range(G):
            for c in range(DC):
                mm = pe.matmul(m.psum[:, bank, j * P:(j + 1) * P], xt_raw[:, c, j * P:(j + 1) * P], m.small["sel_w1"][:, c, :],
                               start=(c == 0), stop=(c == DC - 1))
        read = m.M(mm)
        tok = slice(g * GT, (g + 1) * GT)
        parts = split(m, xt_hi[:, :, tok], xt_lo[:, :, tok], xt_raw[:, :, :], xt, (), pool)
        m.wait(act, read)
        sg = m.A(act.activation(gates[:, g * G:(g + 1) * G].rearrange("p t h e -> p (t h e)"), m.psum[:, bank, :], ACT.Sigmoid))
        m.banks.freed[bank] = (sg,)
        gate_pre.append(sg)
        raw_free.append((read, parts))
        return parts

    def route(g):
        n = G * 2 * NH
        part = gates[:, g * G:(g + 1) * G].rearrange("p t h e -> p (t h) e")
        top2(m, part, gate_pre[g])
        v2 = m.top_v
        m.VV(dve.tensor_tensor(den[:, :], v2[:, 0, 0:n], v2[:, 1, 0:n], ALU.add))
        m.VV(dve.tensor_scalar(den[:, :], den[:, :], 1e-9, None, ALU.max))
        m.VV(dve.reciprocal(den[:, :], den[:, :]))
        m.wait(dve, m.small_ready)
        m.VV(dve.tensor_scalar(den[:, :], den[:, :], m.small["route_scale"][:, 0:1], None, ALU.mult))
        m.VV(dve.tensor_tensor(v2[:, :, 0:n], v2[:, :, 0:n], bcast(den[:, :].unsqueeze(1), P, 2, n), ALU.mult))
        return combine(m, part, n)

    qk_w, v_w, o_w = {}, {}, {}
    used = dict(qk=[(), ()], v=(), o=[()] * (NV // CH))

    pieces = []
    for hd in range(NH):
        pieces.append((ins["ffn1_q"][hd], ins["ffn1_k"][hd]))
        for src in (ins["ffn1_v"][hd], ins["ffn1_o"][hd]):
            pieces += [(src[:, at:at + CH],) for at in range(0, NV, CH)]
    on_way = []

    def fetch():
        if pieces:
            k, free = raw_ring.take()
            m.wait(m.sp, *free)
            at = 0
            for src in pieces.pop(0):
                mark = S_raw[k].after(m.sp.dma_start(raw[:, k, at:at + src.shape[1]], src))
                at += src.shape[1]
            on_way.append((k, mark))

    def split_piece(hi, lo, free, lo_engine):
        k, loaded = on_way.pop(0)
        done = split(m, hi, lo, raw[:, k, :], loaded, free, lo_engine)
        raw_ring.freed[k] = (done,)
        fetch()
        return done

    def split_qk(hd):
        qk_w[hd] = split_piece(qk_hi[:, hd % 2, :], qk_lo[:, hd % 2, :], used["qk"][hd % 2], pool)

    def split_v(hd):
        v_w[hd] = [split_piece(w_hi[:, at:at + CH], w_lo[:, at:at + CH], used["v"], dve if at // CH % 2 else pool)
                   for at in range(0, NV, CH)]

    def split_o(hd):
        o_w[hd] = [split_piece(w_hi[:, NV + k * CH:NV + (k + 1) * CH], w_lo[:, NV + k * CH:NV + (k + 1) * CH],
                               used["o"][k], dve if k % 2 else pool) for k in range(NV // CH)]

    for _ in range(RAW):
        fetch()
    x_split = layernorm(m, (), to=to_parts)

    last = dict(scores=(), av=(), cT=())
    parts, v_parts = Ring(2), Ring(1)

    def queries_keys(hd, g):
        tok = slice(g * GT, (g + 1) * GT)
        m.wait(pe, x_split[g], qk_w[hd])
        for at, dst in ((0, qT), (DC * DP, kT)):
            bank, free = m.banks.take()
            m.wait(pe, *free)
            for c in range(DC):
                col = slice(at + c * DP, at + (c + 1) * DP)
                mm = product(m, m.psum[:, bank, :], (qk_hi[:, hd % 2, col], qk_lo[:, hd % 2, col]),
                             (xt_hi[:, c, tok], xt_lo[:, c, tok]), c == 0, c == DC - 1)
            full = m.M(mm)
            m.wait(act, full, *last["scores"])
            qk = m.A(act.activation(dst[:, :], m.psum[:, bank, :], ACT.Copy))
            m.banks.freed[bank] = (qk,)
        used["qk"][hd % 2] = (full,)
        return qk

    def scores(hd, g, i, qk):
        bank, free = m.banks.take()
        m.wait(pe, qk, *free)
        for j in range(G):
            tok = slice(j * P, (j + 1) * P)
            mm = pe.matmul(m.psum[:, bank, tok], qT[:, tok], kT[:, tok], start=True, stop=True)
        full = m.M(mm)
        last["scores"] = (full,)
        m.wait(dve, full)
        m.VV(dve.tensor_reduce(mx[:, i], m.psum[:, bank, :].rearrange("p (j s) -> p j s", j=G), AX.X, ALU.max, negate=True))
        top = m.V(dve.tensor_scalar(mx[:, i], mx[:, i], SCALE, None, ALU.mult))
        m.wait(act, top, *last["S"])
        for j in range(G):
            ex = m.A(act.activation(S[:, j, :], m.psum[:, bank, j * P:(j + 1) * P], ACT.Exp, bias=mx[:, i, j:j + 1],
                                    scale=SCALE, accum_out=sm[:, i, j:j + 1]))
        m.banks.freed[bank] = (ex,)
        return ex

    def out_gates(hd, g, i, ex):
        m.wait(dve, ex)
        m.VV(dve.reciprocal(sm[:, i], sm[:, i]))
        return m.V(dve.tensor_tensor(out_gate[:, i], gates[:, g * G:(g + 1) * G, NH + hd, :],
                                     bcast(sm[:, i].unsqueeze(2), P, G, NE), ALU.mult))

    def values(hd, g, j):
        t = g * G + j
        for half in range(2):
            bank, free = m.banks.take()
            m.wait(pe, *free)
            for c in range(DC):
                at = (c * 2 + half) * CH
                m.wait(pe, v_w[hd][c * 2 + half])
                tok = slice(t * P, (t + 1) * P)
                mm = product(m, m.psum[:, bank, :], (xt_hi[:, c, tok], xt_lo[:, c, tok]),
                             (w_hi[:, at:at + CH], w_lo[:, at:at + CH]), c == 0, c == DC - 1)
            full = m.M(mm)
            src = [m.psum[:, bank, q * DP:(q + 1) * DP] for q in range(4)]
            gate = [gates[:, t, hd, e:e + 1] for e in range(half * 4, half * 4 + 4)]
            if half == 0:
                m.wait(dve, full, gates_ready[g], *last["av"])
                vr = m.VV(dve.tensor_scalar(v[:, j, :], src[0], gate[0], None, ALU.mult))
                for q in range(1, 4):
                    vr = m.VV(dve.scalar_tensor_tensor(out=v[:, j, :], in0=src[q], scalar=gate[q], in1=v[:, j, :],
                                                       op0=ALU.mult, op1=ALU.add))
                m.banks.freed[bank] = (vr,)
            else:
                b, part_free = v_parts.take()
                m.wait(act, full, gates_ready[g], *part_free)
                for q in range(4):
                    scaled = m.A(act.activation(part_v[:, b, q, :], src[q], ACT.Copy, scale=gate[q]))
                m.banks.freed[bank] = (scaled,)
                m.wait(pool, scaled)
                m.wait(pool, m.Q(pool.tensor_tensor(part_v[:, b, 0:2, :], part_v[:, b, 0:2, :], part_v[:, b, 2:4, :], ALU.add)))
                m.wait(pool, m.Q(pool.tensor_tensor(part_v[:, b, 0, :], part_v[:, b, 0, :], part_v[:, b, 1, :], ALU.add)), vr)
                vr = m.Q(pool.tensor_tensor(v[:, j, :], v[:, j, :], part_v[:, b, 0, :], ALU.add))
                v_parts.freed[b] = (vr,)
        used["v"] = (full,)
        return vr

    def turn(ex):
        bank, free = m.banks.take()
        m.wait(pe, ex, *free)
        for j in range(G):
            mm = pe.transpose(m.psum[:, bank, j * P:(j + 1) * P], S[:, j, :], m.ident[:, :])
        full = m.M(mm)
        last["S"] = (full,)
        m.wait(act, full, *last["av"])
        st = m.A(act.activation(sT[:, :], m.psum[:, bank, :], ACT.Copy))
        m.banks.freed[bank] = (st,)
        return st

    def attend(st, vr):
        bank, free = m.banks.take()
        m.wait(pe, st, vr, *free)
        for j in range(G):
            mm = pe.matmul(m.psum[:, bank, j * P:(j + 1) * P], v[:, j, :], sT[:, j * P:(j + 1) * P], start=True, stop=True)
        full = m.M(mm)
        last["av"] = (full,)
        m.wait(act, full, *last["cT"])
        high = m.A(act.activation(cT_hi[:, :], m.psum[:, bank, :], ACT.Copy))
        m.wait(dve, high)
        low = m.V(dve.tensor_tensor(cT_lo[:, :], m.psum[:, bank, :], cT_hi[:, :].bitcast(F32), ALU.subtract))
        m.banks.freed[bank] = (low,)
        return low

    def outputs(hd, g, i, j, ct, og):
        t = g * G + j
        tok = slice(j * P, (j + 1) * P)
        m.wait(pe, ct)
        for k in range(4):
            bank, free = m.banks.take()
            m.wait(pe, o_w[hd][k], *free)
            at = NV + k * CH
            mm = product(m, m.psum[:, bank, :], (cT_hi[:, tok], cT_lo[:, tok]),
                         (w_hi[:, at:at + CH], w_lo[:, at:at + CH]), True, True)
            full = m.M(mm)
            used["o"][k] = (full,)
            gate = [out_gate[:, i, j, e:e + 1] for e in (2 * k, 2 * k + 1)]
            src = [m.psum[:, bank, q * D:(q + 1) * D] for q in range(2)]
            if k < 3:
                m.wait(dve, full, og, m.x_ready[t])
                for q in range(2):
                    added = m.VV(dve.scalar_tensor_tensor(out=m.X[:, t, :], in0=src[q], scalar=gate[q], in1=m.X[:, t, :],
                                                          op0=ALU.mult, op1=ALU.add))
                m.banks.freed[bank] = (added,)
            else:
                b, part_free = parts.take()
                m.wait(act, full, og, *part_free)
                for q in range(2):
                    scaled = m.A(act.activation(part_out[:, b, q, :], src[q], ACT.Copy, scale=gate[q]))
                m.banks.freed[bank] = (scaled,)
                m.wait(pool, scaled)
                summed = m.Q(pool.tensor_tensor(part_out[:, b, 0, :], part_out[:, b, 0, :], part_out[:, b, 1, :], ALU.add))
                m.wait(pool, summed, added)
                m.x_ready[t] = m.Q(pool.tensor_tensor(m.X[:, t, :], m.X[:, t, :], part_out[:, b, 0, :], ALU.add))
                parts.freed[b] = (m.x_ready[t],)
        last["cT"] = (full,)
        return full

    last["S"] = ()
    split_qk(0)
    split_v(0)
    split_o(0)
    gates_ready = [route(0)]
    before = None
    for n in range(NH * NG):
        hd, g, i = n // NG, n % NG, n % 2

        def out(j):
            return outputs(*before[:3], j, *before[3:]) if before else None

        qk = queries_keys(hd, g)
        out(0)
        ex = scores(hd, g, i, qk)
        values(hd, g, 0)
        out(1)
        og = out_gates(hd, g, i, ex)
        values(hd, g, 1)
        st = turn(ex)
        values(hd, g, 2)
        out(2)
        vr = values(hd, g, 3)
        if g == NG - 1 and hd + 1 < NH:
            split_v(hd + 1)
        done = out(3)
        if g == 0:
            if hd:
                split_o(hd)
        if g == 2 and hd + 1 < NH:
            split_qk(hd + 1)
        if len(gates_ready) < NG:
            gates_ready.append(route(len(gates_ready)))
        before = (hd, g, i, attend(st, vr), og)
    for j in range(G):
        done = out(j)
    m.xt_free = ()
    m.barrier()



def layer2_ffn(m, ins, scratch):
    NE = 16
    m.layer("ffn2")
    pe, dve, act, pool = m.pe, m.dve, m.act, m.pool
    xt = layernorm(m, m.xt_free)
    if m.arriving:
        m.arriving.close()
    with ExitStack() as scratch:
        def sb(name, shape):
            return m.sb(name, shape, F32, scratch)
        z = sb("z", [P, T, NE])
        zs = sb("z_sorted", [P, T, NE])
        zr = sb("z_rest", [P, T, NE])
        st, mv, rs = sb("z_st", [P, T, 6]), sb("z_mv", [P, T, 2]), sb("z_rs", [P, T])
        c1 = [sb(f"cum{i}", [P, T, NE]) for i in range(2)]
        c2 = [sb(f"cumsq{i}", [P, T, NE]) for i in range(2)]
        ik = sb("inv_count", [P, NE])
        mean, tau, hit = sb("mean", [P, T, NE]), sb("tau", [P, T, NE]), sb("hit", [P, T, NE])
        zt, sup = sb("z_top", [P, T]), sb("support", [P, T])
        aT = sb("a_t", [NE, T * P])
        g1, g2, z1 = sb("g1", [P, 2, GT]), sb("g2", [P, 2, GT]), sb("z1", [P, 2, GT])
        z2 = sb("z2", [P, 2, GT])
        shape = [P, T, NE]
        bank, logits = router_logits(m, m.XT, xt, m.small["proj2"], NE)
        m.wait(dve, logits)
        cp = m.VV(dve.tensor_copy(z[:, :, :], m.psum[:, bank, 0:T * NE].rearrange("p (t e) -> p t e", t=T)))
        m.banks.freed[bank] = (cp,)
        for t in range(T):
            s_ = dve.bn_stats(st[:, t, :], z[:, t, :])
        m.VV(s_)
        for t in range(T):
            s_ = dve.bn_aggr(mv[:, t, :], st[:, t, :])
        m.VV(s_)
        rsqrt(m, rs[:, :], mv[:, :, 1], LN_EPS, None)
        m.VV(dve.tensor_tensor(z[:, :, :], z[:, :, :], bcast(mv[:, :, 0:1], *shape), ALU.subtract))
        m.VV(dve.tensor_tensor(z[:, :, :], z[:, :, :], bcast(rs[:, :].unsqueeze(2), *shape), ALU.mult))
        m.VV(dve.tensor_scalar(z[:, :, :], z[:, :, :], 0.5, None, ALU.mult))
        m.VV(dve.tensor_reduce(zt[:, :], z[:, :, :], AX.X, ALU.max))
        m.VV(dve.tensor_tensor(z[:, :, :], z[:, :, :], bcast(zt[:, :].unsqueeze(2), *shape), ALU.subtract))
        for t in range(T):
            s_ = dve.max(zs[:, t, 0:8], z[:, t, :])
        m.VV(s_)
        for t in range(T):
            s_ = dve.match_replace(zr[:, t, :], zs[:, t, 0:8], z[:, t, :], LOWEST)
        m.VV(s_)
        for t in range(T):
            s_ = dve.max(zs[:, t, 8:16], zr[:, t, :])
        m.VV(s_)
        m.VV(dve.reciprocal(ik[:, :], m.count16[:, :]))
        m.VV(dve.tensor_copy(c1[0][:, :, :], zs[:, :, :]))
        m.VV(dve.tensor_tensor(c2[0][:, :, :], zs[:, :, :], zs[:, :, :], ALU.mult))
        for k in range(4):
            s = 1 << k
            for c in (c1, c2):
                x, y = c[k % 2], c[1 - k % 2]
                dve.tensor_copy(y[:, :, 0:s], x[:, :, 0:s])
                m.VV(dve.tensor_tensor(y[:, :, s:], x[:, :, s:], x[:, :, 0:NE - s], ALU.add))
        kb = bcast(m.count16[:, :].unsqueeze(1), *shape)
        ikb = bcast(ik[:, :].unsqueeze(1), *shape)
        m.VV(dve.tensor_tensor(mean[:, :, :], c1[0][:, :, :], ikb, ALU.mult))
        m.VV(dve.tensor_tensor(c2[0][:, :, :], c2[0][:, :, :], ikb, ALU.mult))
        m.VV(dve.tensor_tensor(c1[1][:, :, :], mean[:, :, :], mean[:, :, :], ALU.mult))
        m.VV(dve.tensor_tensor(c2[0][:, :, :], c2[0][:, :, :], c1[1][:, :, :], ALU.subtract))
        m.VV(dve.tensor_tensor(c2[0][:, :, :], c2[0][:, :, :], kb, ALU.mult))
        m.VV(dve.tensor_scalar(c2[0][:, :, :], c2[0][:, :, :], -1.0, 1.0, ALU.mult, ALU.add))
        m.VV(dve.tensor_tensor(c2[0][:, :, :], c2[0][:, :, :], ikb, ALU.mult))
        dl = m.V(dve.tensor_scalar(c2[0][:, :, :], c2[0][:, :, :], 0.0, None, ALU.max))
        m.wait(act, dl)
        m.wait(dve, m.A(act.activation(c2[1][:, :, :], c2[0][:, :, :], ACT.Sqrt)))
        m.VV(dve.tensor_tensor(tau[:, :, :], mean[:, :, :], c2[1][:, :, :], ALU.subtract))
        m.VV(dve.tensor_tensor(hit[:, :, :], tau[:, :, :], zs[:, :, :], ALU.is_le))
        m.VV(dve.tensor_reduce(sup[:, :], hit[:, :, :], AX.X, ALU.add))
        m.VV(dve.tensor_tensor(hit[:, :, :], kb, bcast(sup[:, :].unsqueeze(2), *shape), ALU.is_equal))
        m.VV(dve.tensor_tensor(hit[:, :, :], hit[:, :, :], tau[:, :, :], ALU.mult))
        m.VV(dve.tensor_reduce(zt[:, :], hit[:, :, :], AX.X, ALU.add))
        m.VV(dve.tensor_tensor(z[:, :, :], z[:, :, :], bcast(zt[:, :].unsqueeze(2), *shape), ALU.subtract))
        m.VV(dve.tensor_scalar(z[:, :, :], z[:, :, :], 0.0, None, ALU.max))
        ar = m.VV(dve.tensor_tensor(z[:, :, :], z[:, :, :], z[:, :, :], ALU.mult))
        for g in range(NG):
            bank, free = m.banks.take()
            m.wait(pe, ar, m.const_ready, *free)
            for j in range(G):
                mm = pe.transpose(m.psum[0:NE, bank, j * P:(j + 1) * P], z[:, g * G + j, :], m.ident[:, :])
            m.wait(act, m.M(mm))
            at = m.A(act.activation(aT[:, g * GT:(g + 1) * GT], m.psum[0:NE, bank, :], ACT.Copy))
            m.banks.freed[bank] = (at,)
        z2_free = [(), ()]
        for g in range(NG):
            i = g % 2
            tok = slice(g * GT, (g + 1) * GT)
            for w, dst in ((m.small["C1"], g1), (m.small["C2"], g2)):
                bank, free = m.banks.take()
                m.wait(pe, at, m.small_ready, *free)
                mm = pe.matmul(m.psum[:, bank, :], w[0:NE, :], aT[:, tok], start=True, stop=True)
                m.wait(act, m.M(mm), *z2_free[i])
                gr = m.A(act.activation(dst[:, i, :], m.psum[:, bank, :], ACT.Copy))
                m.banks.freed[bank] = (gr,)
            bank, free = m.banks.take()
            m.wait(pe, *free)
            for c in range(DC):
                mm = pe.matmul(m.psum[:, bank, :], m.small["Win1"][:, c, :], m.XT[:, c, tok], start=(c == 0), stop=(c == DC - 1))
            xt_used = m.M(mm)
            m.wait(dve, xt_used, gr, *z2_free[i])
            z1r = m.V(dve.scalar_tensor_tensor(out=z1[:, i, :], in0=m.psum[:, bank, :], scalar=m.small["win1_b"][:, 0:1],
                                               in1=g1[:, i, :], op0=ALU.add, op1=ALU.mult))
            m.banks.freed[bank] = (z1r,)
            h_slot, h_free = m.h_ring.take()
            m.wait(act, *h_free)
            hm = []
            for f in range(8):
                bank, free = m.banks.take()
                m.wait(pe, z1r, *free)
                mm = pe.matmul(m.psum[:, bank, :], m.small["Wout1"][:, f, :], z1[:, i, :], start=True, stop=True)
                m.wait(act, m.M(mm))
                hr = m.A(act.activation(m.H[:, h_slot, f, :], m.psum[:, bank, :], ACT.Gelu))
                m.banks.freed[bank] = (hr,)
                hm.append(hr)
            bank, free = m.banks.take()
            m.wait(pe, *free)
            for f in range(8):
                m.wait(pe, hm[f])
                mm = pe.matmul(m.psum[:, bank, :], m.small["Win2"][:, f, :], m.H[:, h_slot, f, :], start=(f == 0), stop=(f == 7))
            h_used = m.M(mm)
            m.h_ring.freed[h_slot] = (h_used,)
            m.wait(dve, h_used)
            z2r = m.V(dve.scalar_tensor_tensor(out=z2[:, i, :], in0=m.psum[:, bank, :], scalar=m.small["win2_b"][:, 0:1],
                                               in1=g2[:, i, :], op0=ALU.add, op1=ALU.mult))
            m.banks.freed[bank] = (z2r,)
            for half in range(2):
                bank, free = m.banks.take()
                m.wait(pe, z2r, *free)
                for j in range(2):
                    k = half * 2 + j
                    mm = pe.matmul(m.psum[:, bank, j * D:(j + 1) * D], z2[:, i, k * P:(k + 1) * P], m.small["Wout2"][:, :], start=True, stop=True)
                out = m.M(mm)
                t = g * G + half * 2
                m.wait(dve, out, m.x_ready[t], m.x_ready[t + 1])
                added = m.V(dve.tensor_tensor(m.X[:, t:t + 2, :], m.X[:, t:t + 2, :],
                                              m.psum[:, bank, :].rearrange("p (j d) -> p j d", j=2), ALU.add))
                m.banks.freed[bank] = (added,)
                m.x_ready[t:t + 2] = [added] * 2
            z2_free[i] = (out, added)
        m.xt_free = (xt_used,)
        m.barrier()



def layer3_mix(m, ins, scratch):
    SCALE = 64 ** -0.5
    KEYS = 2 * P
    m.layer("mix3")
    pe, dve, act, pool = m.pe, m.dve, m.act, m.pool
    xt = layernorm(m, m.xt_free)
    with ExitStack() as scratch:
        def sb(name, shape):
            return m.sb(name, shape, F32, scratch)
        qT, kT = sb("qT3", [P, 2, DC, GT]), sb("kT3", [P, 2, DC, GT])
        v = sb("v3", [P, 2, G, D])
        S = sb("scores3", [P, 2, 2, KEYS])
        mx, sm = sb("max3", [P, 2, 2]), sb("sum3", [P, 2, 2])
        sT = sb("scoresT3", [P, 2, 2, KEYS])
        free_g = [(), ()]
        n = 0
        s_free = [(), ()]
        for g in range(NG):
            i = g % 2
            tok = slice(g * GT, (g + 1) * GT)
            m.wait(pe, xt[g], m.small_ready)
            for w, bias, dst in (("q_w3", "q_b3", qT), ("k_w3", "k_b3", kT)):
                for o in range(DC):
                    bank, free = m.banks.take()
                    m.wait(pe, *free)
                    for c in range(DC):
                        mm = pe.matmul(m.psum[:, bank, :], m.small[w][:, c, o * P:(o + 1) * P], m.XT[:, c, tok], start=(c == 0), stop=(c == DC - 1))
                    m.wait(act, m.M(mm), m.small_ready, *free_g[i])
                    qk = m.A(act.activation(dst[:, i, o, :], m.psum[:, bank, :], ACT.Identity, bias=m.small[bias][:, o:o + 1]))
                    m.banks.freed[bank] = (qk,)
            for half in range(2):
                bank, free = m.banks.take()
                m.wait(pe, *free)
                for j in range(2):
                    t = g * G + half * 2 + j
                    for c in range(DC):
                        mm = pe.matmul(m.psum[:, bank, j * D:(j + 1) * D], m.XT[:, c, t * P:(t + 1) * P], m.small["v_w3"][:, c, :],
                                       start=(c == 0), stop=(c == DC - 1))
                xt_used = m.M(mm)
                m.wait(dve, xt_used, *free_g[i])
                vr = m.V(dve.tensor_tensor(v[:, i, half * 2:half * 2 + 2, :], m.psum[:, bank, :].rearrange("p (j d) -> p j d", j=2),
                                           bcast(m.small["v_b3"][:, :].unsqueeze(1), P, 2, D), ALU.add))
                m.banks.freed[bank] = (vr,)
            for half in range(2):
                s = n % 2
                n += 1
                bank, free = m.banks.take()
                m.wait(pe, qk, *free)
                for j in range(2):
                    k = half * 2 + j
                    loc = slice(k * P, (k + 1) * P)
                    glob = slice((g * G + k) * P, (g * G + k + 1) * P)
                    for part, keys in ((0, lambda c: m.CTXT[:, c, glob]), (1, lambda c: kT[:, i, c, loc])):
                        col = j * KEYS + part * P
                        for c in range(DC):
                            mm = pe.matmul(m.psum[:, bank, col:col + P], qT[:, i, c, loc], keys(c), start=(c == 0), stop=(c == DC - 1))
                m.wait(dve, m.M(mm))
                src = m.psum[:, bank, :].rearrange("p (j s) -> p j s", j=2)
                m.VV(dve.tensor_reduce(mx[:, s], src, AX.X, ALU.max))
                sub = m.V(dve.tensor_tensor(S[:, s], src, bcast(mx[:, s].unsqueeze(2), P, 2, KEYS), ALU.subtract))
                m.banks.freed[bank] = (sub,)
                m.wait(act, sub)
                ex = m.A(act.activation(S[:, s], S[:, s], ACT.Exp, scale=SCALE))
                m.wait(dve, ex)
                m.VV(dve.tensor_reduce(sm[:, s], S[:, s], AX.X, ALU.add))
                m.VV(dve.reciprocal(sm[:, s], sm[:, s]))
                bank, free = m.banks.take()
                m.wait(pe, ex, *free)
                for j in range(2):
                    for part in range(2):
                        col = j * KEYS + part * P
                        mm = pe.transpose(m.psum[:, bank, col:col + P], S[:, s, j, part * P:(part + 1) * P], m.ident[:, :])
                m.wait(act, m.M(mm))
                st = m.A(act.activation(sT[:, s].rearrange("p j s -> p (j s)"), m.psum[:, bank, :], ACT.Copy))
                m.banks.freed[bank] = (st,)
                bank, free = m.banks.take()
                m.wait(pe, st, vr, m.ctx_ready, *free)
                for j in range(2):
                    k = half * 2 + j
                    t = g * G + k
                    pe.matmul(m.psum[:, bank, j * D:(j + 1) * D], sT[:, s, j, 0:P], m.CTX[:, t, :], start=True, stop=False)
                    mm = pe.matmul(m.psum[:, bank, j * D:(j + 1) * D], sT[:, s, j, P:KEYS], v[:, i, k, :], start=False, stop=True)
                out = m.M(mm)
                m.wait(dve, out)
                for j in range(2):
                    t = g * G + half * 2 + j
                    m.wait(dve, m.x_ready[t])
                    m.x_ready[t] = m.V(dve.scalar_tensor_tensor(out=m.X[:, t, :], in0=m.psum[:, bank, j * D:(j + 1) * D],
                                                                scalar=sm[:, s, j:j + 1], in1=m.X[:, t, :], op0=ALU.mult, op1=ALU.add))
                m.banks.freed[bank] = (m.x_ready[t],)
            free_g[i] = (out,)
        m.xt_free = (xt_used,)
        m.barrier()


def wide_buffers(m, ins, name, queue):
    m.CTX = m.sb("CTX" + name, [P, T, D], F32, m.wide)
    m.XT = m.sb("XT" + name, [P, DC, T * P], F32, m.wide)
    m.W = Weights(m, name, m.wide, 2, 4608)
    m.ctx_ready = m.S_ctx.after(queue.dma_start(m.CTX[:, :, :], ins["ctx"]))


LAYERS = [layer0_mix, layer0_ffn, layer1_mix, layer1_ffn, layer2_mix, layer2_ffn, layer3_mix, layer3_ffn]
NLAYERS = 8


def build(nc, ins, out, x_table, y_table):
    with ExitStack() as ctx:
        m = Machine(nc, ctx)
        m.psum = ctx.enter_context(nc.psum_tensor("psum", [P, 8, BANK], F32))
        m.banks = Ring(8)
        constants(m, ins)
        m.CTXT = m.sb("CTXT", [P, DC, T * P])
        m.xt_free = ()
        m.ln_stats, m.ln_mv, m.ln_rstd = m.sb("ln_stats", [P, G, 6]), m.sb("ln_mv", [P, G, 2]), m.sb("ln_rstd", [P, G])
        NR = 64
        m.top_key, m.top_best = m.sb("top_key", [P, NR, 8]), m.sb("top_best", [P, NR])
        m.top_v, m.top_h = m.sb("top_v", [P, 2, NR]), m.sb("top_h", [P, 2, NR, 8])
        m.route, m.gates = m.sb("route", [P, T, 8]), m.sb("gates", [P, T, 8])
        m.pos = m.sb("pos", [P, 2, T], I32)
        m.arriving = None
        m.cum = m.sb("cum", [P, 2, T, 8])
        m.wide = ExitStack()
        wide_buffers(m, ins, "_a", m.act)
        m.x_table, m.y_table = x_table, y_table

        zeros = m.cum[:, :, :, :].rearrange("p k t e -> p (k t e)").unsqueeze(1)
        m.wait(m.act, m.V(m.dve.memset(zeros, 0.0)))
        S_zero = m.counter("zero_tables", 16)
        for table in (x_table, y_table):
            rows = table.rearrange("(n p a) d -> n p a d", a=16, p=P)
            for n in range(rows.shape[0]):
                m.zeroed = S_zero.after(m.act.dma_start(rows[n], bcast(zeros, P, 16, D)))

        def barrier():
            ends = tuple((s, s.value) for s in (m.S_pe, m.S_dve, m.S_act, m.S_pool) if s.value)
            for eng in (m.pe, m.dve, m.act, m.pool, m.sp):
                m.wait(eng, *ends)
        m.barrier = barrier
        for n, layer in enumerate(LAYERS[:NLAYERS]):
            with ExitStack() as part:
                if layer not in (layer0_ffn, layer1_mix, layer1_ffn, layer2_mix, layer3_ffn):
                    m.LN = m.sb(f"LN{n}", [P, 1, G, D], F32, part)
                    m.ln_ring = Ring(1)
                if layer is layer2_ffn:
                    m.H = m.sb(f"H{n}", [P, 1, 8, GT], F32, part)
                    m.h_ring = Ring(1)
                if layer in (layer2_mix, layer3_ffn):
                    m.gates_fm = m.sb(f"gates_fm{n}", [8, 1, 2 * P], F32, part)
                if m.arriving:
                    m.arriving.open()
                arriving = m.arriving
                layer(m, ins, part)
                m.barrier()
            if arriving and arriving is m.arriving:
                arriving.close()
            if layer is layer1_ffn:
                wide_buffers(m, ins, "_b", m.sp)
        S_out = m.counter("store", 16)
        ctx.push(m.wide)
        m.wait(m.sp, m.zeroed, m.small_ready, m.ctx_ready)
        if m.arriving:
            m.arriving.open()
        for g in range(NG):
            if m.arriving:
                m.arriving.need(g)
            tiles = slice(g * G, (g + 1) * G)
            m.wait(m.sp, *m.x_ready[tiles])
            stored = S_out.after(m.sp.dma_start(out[:, tiles, :], m.X[:, tiles, :]))
        m.wait(m.sp, stored)
        if m.arriving:
            m.arriving.close()


def chunks(w):
    n = w.shape[0] // P
    return w.reshape(n, P, w.shape[1]).transpose(1, 0, 2)


def kernel(**a):
    import numpy as np
    import concourse.bacc as bacc
    from concourse.bass_utils import run_bass_kernel_spmd

    a = {k: np.asarray(v) for k, v in a.items()}

    def tiles(x):
        return x.transpose(1, 0, 2)

    def ffn(w1, w2):
        E = w1.shape[0]
        w1 = np.stack([chunks(w1[e]).reshape(P, -1) for e in range(E)])
        w2 = np.stack([chunks(w2[e]).reshape(P, -1) for e in range(E)])
        return w1, w2

    h = {"x": tiles(a["x"]), "ctx": tiles(a["ctx_1024"]), "mask": a["mask_BxS2_bk0"].reshape(1, -1)}
    h["gate_w0"] = chunks(np.concatenate([a["L0_xattn_igate_w"], a["L0_xattn_fgate_w"]]).T)
    h["gate_b0"] = np.concatenate([a["L0_xattn_igate_b"], a["L0_xattn_fgate_b"]])[None]
    h["head_scale0"] = a["L0_xattn_out_w"][None]
    h["router_w0"] = chunks(a["L0_ffn_router_w"].T)
    h["ffn0_w1"], h["ffn0_w2"] = ffn(a["L0_ffn_fc1_w"].transpose(0, 2, 1), a["L0_ffn_fc2_w"].transpose(0, 2, 1))
    h["rms_scale"] = a["L1_xattn_rms_scale"][None]
    h["q_w1"] = chunks(a["L1_xattn_q_w"].transpose(1, 0, 2).reshape(D, D))
    h["kv_w1"] = chunks(a["L1_xattn_kv_w"][[0, 0, 1], 0].transpose(1, 0, 2).reshape(D, 3 * 64))
    h["out_w1"] = chunks(a["L1_xattn_out_w"].reshape(D, D))
    freq = np.float32(10000.0) ** (np.float32(2.0 / 64) * np.arange(32, dtype=np.float32))
    pos = np.arange(2 * P, dtype=np.float32).reshape(2, P, 1) / freq
    pos = pos[[1, 1, 1, 1, 0, 0]].transpose(1, 0, 2)
    h["cos"] = np.cos(pos).astype(np.float32)
    h["sin"] = np.stack([-np.sin(pos), np.sin(pos)], axis=2).astype(np.float32)
    h["sel_w1"] = chunks(np.concatenate([a["L1_ffn_sel_v_w"], a["L1_ffn_sel_o_w"]]).T)
    h["route_scale"] = a["L1_ffn_route_scale"][None]
    for k in "qk":
        w = a[f"L1_ffn_{k}_w"].reshape(8, P, D).transpose(0, 2, 1)
        h["ffn1_" + k] = np.stack([chunks(w[i]).reshape(P, -1) for i in range(8)])
    w = a["L1_ffn_v_w"].reshape(8, 8, D, P).transpose(0, 2, 1, 3).reshape(8, D, 8 * P)
    h["ffn1_v"] = np.stack([chunks(w[i]).reshape(P, -1) for i in range(8)])
    h["ffn1_o"] = a["L1_ffn_o_w"].reshape(8, 8, P, D).transpose(0, 2, 1, 3).reshape(8, P, 8 * D)
    h["router_w2"] = chunks(a["L2_xattn_Wg"])
    h["router_b2"] = a["L2_xattn_bg"][None]
    h["mix2_w1"], h["mix2_w2"] = ffn(a["L2_xattn_W1"], a["L2_xattn_W2"])
    h["b1_2"] = a["L2_xattn_b1"].reshape(8, 8, P).transpose(2, 0, 1)
    h["b2_2"] = a["L2_xattn_b2"]
    h["proj2"] = chunks(a["L2_ffn_proj"])
    h["C1"], h["C2"] = a["L2_ffn_C1"], a["L2_ffn_C2"]
    h["Win1"], h["win1_b"] = chunks(a["L2_ffn_Win1"][:D]), a["L2_ffn_Win1"][D][:, None]
    h["Wout1"] = a["L2_ffn_Wout1"].T.reshape(P, 8, P)
    h["Win2"], h["win2_b"] = chunks(a["L2_ffn_Win2"][:1024]), a["L2_ffn_Win2"][1024][:, None]
    h["Wout2"] = a["L2_ffn_Wout2"].T
    for k in "qkv":
        h[k + "_w3"] = chunks(a[f"L3_xattn_W{k}"].T)
    for k in "qk":
        h[k + "_b3"] = a[f"L3_xattn_b{k}"].reshape(DC, P).T
    h["v_b3"] = a["L3_xattn_bv"][None]
    h["router_w3"] = chunks(a["L3_ffn_gate_w"])
    h["router_b3"] = a["L3_ffn_gate_b"][None]
    w1 = np.concatenate([a["L3_ffn_sh_w1"][None], a["L3_ffn_ew1"]])
    w2 = np.concatenate([a["L3_ffn_sh_w2"][None], a["L3_ffn_ew2"]])
    h["ffn3_w1"], h["ffn3_w2"] = ffn(w1, w2)
    h["b1_3"] = np.concatenate([a["L3_ffn_sh_b1"][None], a["L3_ffn_eb1"]]).reshape(9, 8, P).transpose(2, 0, 1)
    h["b2_3"] = a["L3_ffn_eb2"]
    h["sh_b2_3"] = a["L3_ffn_sh_b2"][None]

    nc = bacc.Bacc("TRN2", target_bir_lowering=False, num_devices=1)
    arrays, ins = {}, {}
    for name, v in h.items():
        v = np.ascontiguousarray(v)
        arrays["in_" + name] = v
        ins[name] = nc.dram_tensor("in_" + name, v.shape, mybir.dt.from_np(v.dtype), kind="ExternalInput").ap()
    out = nc.dram_tensor("out", (P, T, D), F32, kind="ExternalOutput").ap()
    x_table, y_table = (nc.dram_tensor(n, (8 * T * P, D), F32, kind="Internal").ap() for n in ("x_table", "y_table"))
    build(nc, ins, out, x_table, y_table)
    r = run_bass_kernel_spmd(nc, [arrays], core_ids=[0])
    return np.ascontiguousarray(r.results[0]["out"].transpose(1, 0, 2))
```

```python
from contextlib import ExitStack

import concourse.bass as bass
from concourse import mybir

F32 = mybir.dt.float32
F32R = mybir.dt.float32r
U8 = mybir.dt.uint8
I32 = mybir.dt.int32
ALU = mybir.AluOpType
ACT = mybir.ActivationFunctionType
AX = mybir.AxisListType

P = 128
T = 16
D = 256
DC = D // P
G = 4
NG = T // G
GT = G * P
BANK = 512
LN_EPS = 1e-5
RMS_EPS = 1e-6
LOWEST = -3.0e38
MASK_FILL = -2.3819763e38


class Counter:

    def __init__(self, sem, step=1):
        self.sem, self.step, self.value = sem, step, 0

    def after(self, instruction):
        instruction.then_inc(self.sem, self.step)
        self.value += self.step
        return (self, self.value)


class Ring:

    def __init__(self, n):
        self.n, self.turn, self.freed = n, 0, [()] * n

    def take(self):
        for k in range(self.n):
            slot = (self.turn + k) % self.n
            if self.freed[slot] is not None:
                self.turn = slot + 1
                marks, self.freed[slot] = self.freed[slot], None
                return slot, marks
        raise AssertionError("every buffer is held")


def interleave(jobs, depth):
    jobs, live = list(jobs), []
    while jobs or live:
        if jobs and len(live) < depth:
            live.append(jobs.pop(0))
        for job in list(live):
            for _ in job:
                break
            else:
                live.remove(job)


class Machine:

    def __init__(self, nc, ctx):
        self.nc, self.ctx = nc, ctx
        self.pe, self.dve, self.act, self.pool, self.sp = nc.tensor, nc.vector, nc.scalar, nc.gpsimd, nc.sync
        self.seen = {}

    def sb(self, name, shape, dt=F32, ctx=None):
        return (ctx or self.ctx).enter_context(self.nc.sbuf_tensor(name, shape, dt))

    def counter(self, name, step=1):
        return Counter(self.ctx.enter_context(self.nc.semaphore(name)), step)

    def wait(self, engine, *marks):
        for counter, value in marks:
            key = (engine.engine, counter.sem.name)
            if self.seen.get(key, 0) < value:
                engine.wait_ge(counter.sem, value)
                self.seen[key] = value

    def layer(self, name):
        self.S_pe = self.counter(name + "_pe")
        self.S_dve = self.counter(name + "_dve")
        self.S_act = self.counter(name + "_act")
        self.S_pool = self.counter(name + "_pool")

    def V(self, instruction):
        return self.S_dve.after(instruction)

    def A(self, instruction):
        return self.S_act.after(instruction)

    def M(self, instruction):
        return self.S_pe.after(instruction)

    def Q(self, instruction):
        return self.S_pool.after(instruction)

    def VV(self, instruction):
        mark = self.V(instruction)
        self.wait(self.dve, mark)
        return mark


def bcast(ap, *shape):
    return ap.broadcast_to(list(shape))



def constants(m, ins):
    m.layer("const")
    pool, dve, sp = m.pool, m.dve, m.sp
    m.ident = m.sb("ident", [P, P])
    m.tri_incl = m.sb("tri_incl", [P, P])
    m.tri_excl = m.sb("tri_excl", [P, P])
    m.ones = m.sb("ones", [P, 1])
    m.minus_half = m.sb("minus_half", [P, T * 4])
    m.rank8 = m.sb("rank8", [P, 8])
    m.count16 = m.sb("count16", [P, 16])
    zero = dve.memset(m.ident[:, :], 0.0)
    dve.memset(m.tri_incl[:, :], 1.0)
    dve.memset(m.tri_excl[:, :], 1.0)
    dve.memset(m.ones[:, :], 1.0)
    for j in range(8):
        dve.memset(m.rank8[:, j:j + 1], float(8 - j))
    m.expert_row = m.sb("expert_row", [P, 8])
    for j in range(8):
        dve.memset(m.expert_row[:, j:j + 1], float(j * T * P))
    for j in range(16):
        dve.memset(m.count16[:, j:j + 1], float(j + 1))
    filled = m.V(dve.memset(m.minus_half[:, :], -0.5))
    m.wait(pool, filled)
    pool.affine_select(out=m.ident[:, :], in_=m.ident[:, :], compare_op=ALU.not_equal, fill=1.0,
                       base=0, pattern=[[-1, P]], channel_multiplier=1)
    pool.affine_select(out=m.tri_incl[:, :], in_=m.tri_incl[:, :], compare_op=ALU.is_ge, fill=0.0,
                       base=0, pattern=[[1, P]], channel_multiplier=-1)
    m.const_ready = m.Q(pool.affine_select(out=m.tri_excl[:, :], in_=m.tri_excl[:, :], compare_op=ALU.is_gt,
                                           fill=0.0, base=0, pattern=[[1, P]], channel_multiplier=-1))
    m.filled = filled
    S_in = m.counter("load_x", 16)
    m.S_ctx = m.counter("load_ctx", 16)
    S_small = m.counter("load_small", 16)
    m.X = m.sb("X", [P, T, D])
    m.x_ready = [S_in.after(sp.dma_start(m.X[:, :, :], ins["x"]))] * T
    S_first = m.counter("load_first", 16)
    m.small = {}
    for name, shape in SMALL:
        t = m.sb("w_" + name, [P] + list(shape))
        src = ins[name]
        if src.shape[0] == 1:
            src = src.partition_broadcast(P) if len(src.shape) == 1 else src[0].partition_broadcast(P)
        np_ = src.shape[0]
        mark = (S_first if name in FIRST else S_small).after(sp.dma_start(t[0:np_], src))
        if name in FIRST:
            m.first_ready = mark
        else:
            m.small_ready = mark
        m.small[name] = t


FIRST = ("gate_w0", "gate_b0", "head_scale0")
SMALL = [
    ("gate_w0", (6, 8)), ("gate_b0", (8,)), ("head_scale0", (D,)),
    ("router_w0", (DC, 8)),
    ("rms_scale", (D,)), ("q_w1", (DC, D)), ("kv_w1", (DC, 3 * 64)), ("out_w1", (DC, D)),
    ("cos", (6, 32)), ("sin", (6, 2, 32)),
    ("sel_w1", (DC, P)), ("route_scale", (1,)),
    ("router_w2", (DC, 8)), ("router_b2", (8,)), ("b1_2", (8, 8)), ("b2_2", (D,)),
    ("proj2", (DC, 16)), ("C1", (P,)), ("C2", (P,)), ("Win1", (DC, P)), ("win1_b", (1,)),
    ("Wout1", (8, P)), ("Win2", (8, P)), ("win2_b", (1,)), ("Wout2", (D,)),
    ("q_w3", (DC, D)), ("k_w3", (DC, D)), ("v_w3", (DC, D)), ("q_b3", (DC,)), ("k_b3", (DC,)), ("v_b3", (D,)),
    ("router_w3", (DC, 8)), ("router_b3", (8,)), ("b1_3", (9, 8)), ("b2_3", (D,)), ("sh_b2_3", (D,)),
]



def rsqrt(m, out, in_, eps, ready):
    n = out.shape[-1]
    e = m.VV(m.dve.tensor_scalar(out, in_, eps, None, ALU.add))
    m.wait(m.pool, e, m.filled)
    done = m.Q(m.pool.tensor_tensor(out, out, m.minus_half[:, 0:n], ALU.pow))
    m.wait(m.dve, done)
    return done


def transposed(m, dst, tiles, ready):
    last = None
    marks = []
    for c in range(DC):
        bank, free = m.banks.take()
        m.wait(m.pe, ready, m.const_ready, *free)
        for j in range(G):
            last = m.pe.transpose(m.psum[:, bank, j * P:(j + 1) * P], tiles[:, j, c * P:(c + 1) * P], m.ident[:, :])
        full = m.M(last)
        m.wait(m.act, full)
        last = m.A(m.act.activation(dst[:, c, :], m.psum[:, bank, :], ACT.Copy))
        m.banks.freed[bank] = (last,)
        marks.append(last)
    return marks[-1]


def layernorm(m, xt_free, keep=None, fm=True, add_back=False, to=None, each=None):
    dve, pool = m.dve, m.pool
    ready, m.ln_ready = [], []

    def stats(g):
        if m.arriving:
            m.arriving.need(g)
        m.wait(dve, *m.x_ready[g * G:(g + 1) * G])
        for j in range(G):
            st = dve.bn_stats(m.ln_stats[:, g % 2, j, :], m.X[:, g * G + j, :])
        m.VV(st)
        for j in range(G):
            ag = dve.bn_aggr(m.ln_mv[:, g % 2, j, :], m.ln_stats[:, g % 2, j, :])
        m.VV(ag)
        rstd = m.ln_rstd[:, g % 2, :]
        m.wait(pool, m.V(dve.tensor_scalar(rstd, m.ln_mv[:, g % 2, :, 1], LN_EPS, None, ALU.add)), m.filled)
        return m.Q(pool.tensor_tensor(rstd, rstd, m.minus_half[:, 0:G], ALU.pow))

    coming = stats(0)
    for g in range(NG):
        tiles = slice(g * G, (g + 1) * G)
        powered, coming = coming, stats(g + 1) if g + 1 < NG else None
        m.wait(dve, powered)
        if keep is None:
            slot, free = m.ln_ring.take()
            m.wait(dve, *free)
            dst = m.LN[:, slot]
        else:
            dst = keep[:, tiles, :]
        for j in range(G):
            done = m.V(dve.tensor_scalar(dst[:, j, :], m.X[:, g * G + j, :], m.ln_mv[:, g % 2, j, 0:1],
                                         m.ln_rstd[:, g % 2, j:j + 1], ALU.subtract, ALU.mult))
        m.ln_ready.append(done)
        if add_back:
            m.wait(dve, done)
            added = m.V(dve.tensor_tensor(m.X[:, tiles, :], m.X[:, tiles, :], dst, ALU.add))
            m.x_ready[g * G:(g + 1) * G] = [added] * G
        if fm:
            m.wait(m.act, *xt_free)
            ready.append(to(g, dst, done) if to else transposed(m, m.XT[:, :, g * GT:(g + 1) * GT], dst, done))
        if keep is None:
            m.ln_ring.freed[slot] = (ready[-1],)
        if each:
            each(g, ready[-1])
    return ready


def top2(m, probs, ready):
    dve = m.dve
    n = probs.shape[1]
    shape = [P, n, 8]
    m.wait(dve, ready, m.filled)
    rank = bcast(m.rank8[:, :].unsqueeze(1), *shape)
    key = m.top_key[:, 0:n, :]
    best = m.top_best[:, 0:n]
    for k in range(2):
        val, hot = m.top_v[:, k, 0:n], m.top_h[:, k, 0:n, :]
        m.VV(dve.tensor_reduce(val, probs, AX.X, ALU.max))
        m.VV(dve.tensor_tensor(key, probs, bcast(val.unsqueeze(2), *shape), ALU.is_equal))
        m.VV(dve.tensor_tensor(key, key, rank, ALU.mult))
        m.VV(dve.tensor_reduce(best, key, AX.X, ALU.max))
        m.VV(dve.tensor_tensor(hot, key, bcast(best.unsqueeze(2), *shape), ALU.is_equal))
        if k == 0:
            m.VV(dve.scalar_tensor_tensor(out=probs, in0=hot, scalar=LOWEST, in1=probs, op0=ALU.mult, op1=ALU.add))


def combine(m, out, n):
    dve = m.dve
    shape = [P, n, 8]
    m.VV(dve.tensor_tensor(m.top_key[:, 0:n, :], m.top_h[:, 0, 0:n, :], bcast(m.top_v[:, 0, 0:n].unsqueeze(2), *shape), ALU.mult))
    m.VV(dve.tensor_tensor(out, m.top_h[:, 1, 0:n, :], bcast(m.top_v[:, 1, 0:n].unsqueeze(2), *shape), ALU.mult))
    return m.VV(dve.tensor_tensor(out, out, m.top_key[:, 0:n, :], ALU.add))


class Logits:

    def __init__(self, m, n, sources, weights_ready):
        self.m, self.n, self.sources, self.weights_ready = m, n, sources, weights_ready
        self.bank, self.free = m.banks.take()
        self.turned = [(), ()]

    def group(self, g, ready):
        m, n = self.m, self.n
        bank, free = m.banks.take()
        m.wait(m.pe, ready, self.weights_ready, m.const_ready, *free, *self.free)
        for k, (tokens, weights) in enumerate(self.sources):
            mm = m.pe.matmul(m.psum[0:n, bank, :], weights, tokens[:, g * GT:(g + 1) * GT],
                             start=(k == 0), stop=(k == len(self.sources) - 1))
        rows = m.top_h[0:n, g % 2].rearrange("p r e -> p (r e)")
        m.wait(m.act, m.M(mm), *self.turned[g % 2])
        copied = m.A(m.act.activation(rows, m.psum[0:n, bank, :], ACT.Copy))
        m.banks.freed[bank] = (copied,)
        m.wait(m.pe, copied)
        for j in range(G):
            t = g * G + j
            mm = m.pe.transpose(m.psum[:, self.bank, t * n:(t + 1) * n], rows[:, j * P:(j + 1) * P], m.ident[0:n, 0:n])
        self.done = m.M(mm)
        self.turned[g % 2] = (self.done,)


def chunks_of(feature_major, weights, n):
    return [(feature_major[:, c, :], weights[:, c, 0:n]) for c in range(DC)]


def softmax8(m, logits):
    dve = m.dve
    shape = [P, T, 8]
    m.VV(dve.tensor_reduce(m.top_best[:, 0:T], logits, AX.X, ALU.max))
    sub = m.V(dve.tensor_tensor(logits, logits, bcast(m.top_best[:, 0:T].unsqueeze(2), *shape), ALU.subtract))
    m.wait(m.act, sub)
    ex = m.A(m.act.activation(logits, logits, ACT.Exp))
    m.wait(dve, ex)
    m.VV(dve.tensor_reduce(m.top_best[:, 0:T], logits, AX.X, ALU.add))
    m.VV(dve.reciprocal(m.top_best[:, 0:T], m.top_best[:, 0:T]))
    return m.VV(dve.tensor_tensor(logits, logits, bcast(m.top_best[:, 0:T].unsqueeze(2), *shape), ALU.mult))


class Weights:

    def __init__(self, m, name, ctx, slots, size):
        self.m, self.size = m, size
        self.buf = m.sb("weights" + name, [P, slots, size], F32, ctx)
        self.ring = Ring(slots)
        self.counters = [m.counter(f"load_w{name}{i}", 16) for i in range(slots)]

    def load(self, *sources):
        slot, free = self.ring.take()
        self.m.wait(self.m.sp, *free)
        at, views = 0, []
        for src in sources:
            n = src.shape[1]
            view = self.buf[:, slot, at:at + n]
            mark = self.counters[slot].after(self.m.sp.dma_start(view, src))
            views.append(view)
            at += n
        assert at <= self.size
        return slot, views, mark



def split(m, hi, lo, raw, ready, free, lo_engine):
    m.wait(m.act, ready, *free)
    high = m.A(m.act.activation(hi, raw, ACT.Copy))
    m.wait(lo_engine, high)
    rest = lo_engine.tensor_tensor(lo, raw, hi.bitcast(F32), ALU.subtract)
    return m.V(rest) if lo_engine is m.dve else m.Q(rest)


def product(m, out, left, right, start, stop):
    m.pe.matmul(out, left[1], right[0], start=start, stop=False)
    m.pe.matmul(out, left[0], right[0], start=False, stop=False)
    return m.pe.matmul(out, left[0], right[1], start=False, stop=stop)



STEP = 2 * P
NSTEP = T * P // STEP
ALWAYS = 2 * T * P // 8 // STEP


def skip(m, engine, counter, before):
    if before:
        engine.wait_ge(counter.sem, before)
    engine.sem_inc(counter.sem, counter.value - before)


class Sparse:

    def __init__(self, m, name, ctx, FC):
        self.m, self.name, self.FC = m, name, FC
        self.LN = m.sb(name + "_ln", [P, T, D], F32, ctx)
        self.posf = m.sb(name + "_posf", [P, 2, T], F32, ctx)
        self.count = m.sb(name + "_count", [P, 8], I32, ctx)
        self.S_scatter = m.counter(name + "_scatter", 16)

    def open(self, ctx):
        m, FC = self.m, self.FC

        def ring(n, count, shape, dt=F32):
            return m.sb(self.name + n, [P, count] + shape, dt, ctx), Ring(count)
        self.W1 = [m.sb(self.name + n, [P, DC, FC * P], F32R, ctx) for n in ("_w1_hi", "_w1_lo")]
        self.W2 = [m.sb(self.name + n, [P, FC, D], F32R, ctx) for n in ("_w2_hi", "_w2_lo")]
        self.Hraw, self.raw_ring = ring("_h", 3, [STEP])
        self.Hparts, self.h_ring = ring("_h_parts", 4, [2, STEP], F32R)
        self.XS, self.xs_ring = ring("_xs", 3, [2, D])
        self.XST, self.xst_ring = ring("_xst", 3, [2, DC, STEP], F32R)
        self.YS, self.ys_ring = ring("_ys", 2, [2, D])
        self.S_xs = [m.counter(f"{self.name}_load_x{i}", 16) for i in range(3)]
        self.S_ys = [m.counter(f"{self.name}_store_y{i}", 16) for i in range(2)]


def places(m, s):
    pe, dve = m.pe, m.dve
    hot = m.top_h[:, :, 0:T, :]
    mask = m.top_key[:, 0:T, :]
    flat = mask.rearrange("p t e -> p (t e)")
    picked = m.VV(dve.tensor_tensor(mask, hot[:, 0], hot[:, 1], ALU.add))
    bank, free = m.banks.take()
    m.wait(pe, picked, m.const_ready, *free)
    pe.matmul(m.psum[:, bank, 0:P], m.tri_excl[:, :], flat, start=True, stop=True)
    both = m.M(pe.matmul(m.psum[:, bank, P:2 * P], bcast(m.ones[:, :], P, P), flat, start=True, stop=True))
    m.wait(dve, both)
    total = m.psum[:, bank, P:2 * P].rearrange("p (t e) -> p t e", t=T)
    m.wait(dve, m.zeroed)
    cum = m.cum
    m.VV(dve.tensor_copy(cum[:, 0], total))
    for k in range(4):
        x, y, d = cum[:, k % 2], cum[:, 1 - k % 2], 1 << k
        dve.tensor_copy(y[:, 0:d, :], x[:, 0:d, :])
        m.VV(dve.tensor_tensor(y[:, d:, :], x[:, d:, :], x[:, 0:T - d, :], ALU.add))
    counted = m.VV(dve.tensor_copy(s.count[:, :], cum[:, 0, T - 1, :]))
    m.VV(dve.tensor_tensor(cum[:, 1], cum[:, 0], total, ALU.subtract))
    got = m.VV(dve.tensor_tensor(cum[:, 1], cum[:, 1], m.psum[:, bank, 0:P].rearrange("p (t e) -> p t e", t=T), ALU.add))
    m.banks.freed[bank] = (got,)
    m.VV(dve.tensor_tensor(cum[:, 1], cum[:, 1], bcast(m.expert_row[:, :].unsqueeze(1), P, T, 8), ALU.add))
    for k in range(2):
        m.VV(dve.tensor_tensor(cum[:, 0], cum[:, 1], hot[:, k], ALU.mult))
        m.VV(dve.tensor_reduce(s.posf[:, k, :], cum[:, 0], AX.X, ALU.add))
    return counted, m.VV(dve.tensor_copy(m.pos[:, :, :], s.posf[:, :, :]))


def scatter(m, s, pos_ready):
    m.wait(m.pool, m.zeroed, pos_ready)
    for t in range(T):
        m.wait(m.pool, m.ln_ready[t // G])
        for k in range(2):
            done = s.S_scatter.after(m.pool.indirect_dma_start(
                m.x_table, bass.IndirectOffsetOnAxis(m.pos[:, k, t:t + 1], 0), s.LN[:, t, :], None))
    return done


def sparse_experts(m, s, scattered, counted, sources, hidden):
    pe, act, dve, sp, FC = m.pe, m.act, m.dve, m.sp, s.FC
    x_rows = m.x_table.rearrange("(n a p) d -> n p a d", a=2, p=P)
    y_rows = m.y_table.rearrange("(n a p) d -> n p a d", a=2, p=P)
    engines = (pe, act, sp, m.pool, m.dve)
    m.wait(sp, m.zeroed)
    SHARED = len(sources) - 8
    for eng in engines:
        m.wait(eng, counted)
    counts = [m.nc.values_load(s.count[0:1, e:e + 1], engines=[eng.engine for eng in engines], min_val=0, max_val=T * P)
              for e in range(8)]
    banks, ybank = Ring(6), Ring(1)
    banks.freed = [m.banks.freed[b] for b in range(6)]
    ybank.freed = [tuple(m.banks.freed[6]) + tuple(m.banks.freed[7])]
    LAG = 2

    def load_rows(e, j):
        i, x_free = s.xs_ring.take()
        m.wait(sp, scattered, *x_free)
        return i, s.XS[:, i], s.S_xs[i].after(sp.dma_start(s.XS[:, i], x_rows[(e - SHARED) * NSTEP + j]))

    def own_rows(j):
        tiles = slice(j * STEP // P, (j + 1) * STEP // P)
        return None, s.LN[:, tiles, :], m.ln_ready[tiles.start // G]

    def turn_rows(i, rows, loaded):
        o, xst_free = s.xst_ring.take()
        bank, free = banks.take()
        m.wait(pe, loaded, m.const_ready, *free)
        for c in range(DC):
            for a in range(2):
                mm = pe.transpose(m.psum[:, bank, (c * 2 + a) * P:(c * 2 + a + 1) * P],
                                  rows[:, a, c * P:(c + 1) * P], m.ident[:, :])
        turned = m.M(mm)
        if i is not None:
            s.xs_ring.freed[i] = (turned,)
        m.wait(act, turned, *xst_free)
        hi, lo = (s.XST[:, o, k].rearrange("p c k -> p (c k)") for k in range(2))
        high = m.A(act.activation(hi, m.psum[:, bank, :], ACT.Copy))
        m.wait(dve, high)
        ready = m.V(dve.tensor_tensor(lo, m.psum[:, bank, :], hi.bitcast(F32), ALU.subtract))
        banks.freed[bank] = (ready,)
        return o, ready

    weights, w_free = [m.W.load(*sources[0])], ()
    first = [turn_rows(*(own_rows(0) if SHARED else load_rows(0, 0)))]
    second = [None if SHARED else load_rows(0, 1)]
    for e in range(len(sources)):
        shared = e < SHARED
        slot, (w1, w2), w_ready = weights[e]
        w1 = w1.rearrange("p (c f) -> p c f", c=DC)
        w2 = w2.rearrange("p (c d) -> p c d", c=FC)
        w1_parts, w2_parts = [], []

        def split_weights(q1, q2):
            for parts, until in ((w1_parts, q1), (w2_parts, q2)):
                for q in range(len(parts), min(until + 1, FC // 2)):
                    if parts is w1_parts:
                        f = slice(q * 2 * P, (q + 1) * 2 * P)
                        parts.append(split(m, s.W1[0][:, :, f], s.W1[1][:, :, f], w1[:, :, f], w_ready, w_free, dve))
                    else:
                        f = slice(q * 2, q * 2 + 2)
                        parts.append(split(m, s.W2[0][:, f, :], s.W2[1][:, f, :], w2[:, f, :], w_ready, w_free, m.pool))

        split_weights(0, -1)

        def body(j, x):
            o, x_ready = x
            if not shared:
                y, ys_free = s.ys_ring.take()
            yb, yb_free = ybank.take()
            rows = rows_first = None
            if shared:
                rows = own_rows(j + 1) if j + 1 < NSTEP else None
            elif j == 0:
                rows = second[e]
            elif j + 1 < NSTEP:
                rows = load_rows(e, j + 1)
            if j == (NSTEP - 1 if shared else 0) and e + 1 < len(sources):
                rows_first = load_rows(e + 1, 0)
                second.append(load_rows(e + 1, 1))
            m.wait(pe, x_ready)
            h_parts = []

            def down(f):
                h, ready = h_parts[f]
                m.wait(pe, ready, w2_parts[f // 2])
                for a in range(2):
                    mm = product(m, m.psum[:, 6 + a, 0:D], [s.Hparts[:, h, k, a * P:(a + 1) * P] for k in range(2)],
                                 [w[:, f, :] for w in s.W2], f == 0, f == FC - 1)
                done = m.M(mm)
                s.h_ring.freed[h] = (done,)
                return done

            for f in range(FC):
                bank, free = banks.take()
                if j == 0 and f % 2 == 0:
                    split_weights(f // 2 + 1, f // 2)
                m.wait(pe, w1_parts[f // 2], *free)
                for c in range(DC):
                    mm = product(m, m.psum[:, bank, 0:STEP], [w[:, c, f * P:(f + 1) * P] for w in s.W1],
                                 [s.XST[:, o, k, c, :] for k in range(2)], c == 0, c == DC - 1)
                up_done = m.M(mm)
                r, raw_free = s.raw_ring.take()
                m.wait(act, up_done, *raw_free)
                freed, done = hidden(m.psum[:, bank, 0:STEP], s.Hraw[:, r, :], e, f)
                banks.freed[bank] = (freed,)
                h, h_free = s.h_ring.take()
                ready = split(m, s.Hparts[:, h, 0, :], s.Hparts[:, h, 1, :], s.Hraw[:, r, :], done, h_free, dve)
                s.raw_ring.freed[r] = (ready,)
                h_parts.append((h, ready))
                if f >= LAG:
                    if f == LAG:
                        m.wait(pe, *yb_free)
                    down(f - LAG)
            s.xst_ring.freed[o] = (up_done,)
            if j == 0:
                m.W.ring.freed[slot] = (w1_parts[-1], w2_parts[-1])
                if e + 1 < len(sources):
                    weights.append(m.W.load(*sources[e + 1]))
            coming = turn_rows(*rows) if rows else None
            if rows_first:
                first.append(turn_rows(*rows_first))
            for f in range(FC - LAG, FC):
                y_full = down(f)
            if shared:
                tiles = slice(j * STEP // P, (j + 1) * STEP // P)
                m.wait(dve, y_full, *m.x_ready[tiles])
                added = m.V(dve.tensor_tensor(m.X[:, tiles, :], m.X[:, tiles, :], m.psum[:, 6:8, 0:D], ALU.add))
                m.x_ready[tiles] = [added] * (STEP // P)
                ybank.freed[yb] = (added,)
                return coming, y_full
            m.wait(dve, y_full, *ys_free)
            y_out = m.V(dve.tensor_copy(s.YS[:, y], m.psum[:, 6:8, 0:D]))
            ybank.freed[yb] = (y_out,)
            m.wait(sp, y_out)
            s.ys_ring.freed[y] = (s.S_ys[y].after(sp.dma_start(y_rows[(e - SHARED) * NSTEP + j], s.YS[:, y])),)
            return coming, y_full

        def branch(j, x):
            counting = [(pe, m.S_pe), (act, m.S_act), (dve, m.S_dve)] + [(sp, c) for c in s.S_xs] + [(sp, c) for c in s.S_ys]
            before = [c.value for _, c in counting]
            with m.nc.If(counts[e - SHARED] > j * STEP):
                x, y_full = body(j, x)
                if j + 1 < NSTEP:
                    y_full = branch(j + 1, x)
            with m.nc.Else():
                for (engine, counter), value in zip(counting, before):
                    if counter.value > value:
                        skip(m, engine, counter, value)
            return y_full

        x = first[e]
        for j in range(NSTEP if shared else ALWAYS):
            x, y_full = body(j, x)
        if not shared:
            seen = dict(m.seen)
            y_full = branch(ALWAYS, x)
            m.seen = seen
        w_free = (y_full,)
    m.banks.freed = banks.freed + [ybank.freed[0]] * 2
    return y_full, (s.ys_ring.freed[0] + s.ys_ring.freed[1])


class Gather:

    SLOTS = 4 * G

    def __init__(self, m, name, stores):
        self.m, self.name, self.stores, self.asked, self.added = m, name, stores, 0, 0

    def open(self):
        m = self.m
        ctx = self.stack = ExitStack()
        self.rows = m.sb(self.name + "_rows", [P, self.SLOTS, D], F32, ctx)
        self.counters = [m.counter(f"{self.name}_gather{i}", 16) for i in range(self.SLOTS)]
        self.freed = [()] * self.SLOTS
        m.wait(m.pool, *self.stores)
        self.ask(0)

    def close(self):
        self.m.barrier()
        self.stack.close()
        self.m.arriving = None

    def slot(self, t, k):
        return (2 * t + k) % self.SLOTS

    def ask(self, g):
        m = self.m
        for t in range(g * G, min((g + 1) * G, T)):
            for k in range(2):
                i = self.slot(t, k)
                m.wait(m.pool, *self.freed[i])
                self.freed[i] = (self.counters[i].after(m.pool.indirect_dma_start(
                    self.rows[:, i, :], None, m.y_table, bass.IndirectOffsetOnAxis(m.pos[:, k, t:t + 1], 0))),)

    def need(self, g):
        m = self.m
        for n in range(self.added, g + 1):
            self.ask(n + 1)
            for k in range(2):
                for t in range(n * G, (n + 1) * G):
                    i = self.slot(t, k)
                    m.wait(m.dve, *self.freed[i], m.x_ready[t])
                    m.x_ready[t] = m.V(m.dve.scalar_tensor_tensor(out=m.X[:, t, :], in0=self.rows[:, i, :], scalar=m.top_v[:, k, t:t + 1],
                                                                  in1=m.X[:, t, :], op0=ALU.mult, op1=ALU.add))
                    self.freed[i] = (m.x_ready[t],)
            self.added = n + 1


def layer0_ffn(m, ins, scratch):
    m.layer("ffn0")
    s = Sparse(m, "ffn0", scratch, 4)
    router = Logits(m, 8, chunks_of(m.XT, m.small["router_w0"], 8), m.small_ready)
    xt = layernorm(m, m.xt_free, keep=s.LN, each=router.group)
    bank, logits = router.bank, router.done
    m.wait(m.dve, logits)
    probs = m.route[:, :, :]
    copied = m.VV(m.dve.tensor_copy(probs, m.psum[:, bank, 0:T * 8].rearrange("p (t e) -> p t e", t=T)))
    m.banks.freed[bank] = (copied,)
    top2(m, probs, softmax8(m, probs))
    counted, pos_ready = places(m, s)
    scattered = scatter(m, s, pos_ready)
    v = m.top_v
    m.VV(m.dve.tensor_tensor(m.top_best[:, 0:T], v[:, 0, 0:T], v[:, 1, 0:T], ALU.add))
    m.VV(m.dve.reciprocal(m.top_best[:, 0:T], m.top_best[:, 0:T]))
    m.VV(m.dve.tensor_tensor(v[:, :, 0:T], v[:, :, 0:T], bcast(m.top_best[:, 0:T].unsqueeze(1), P, 2, T), ALU.mult))

    def hidden(src, out, e, f):
        relu = m.A(m.act.activation(out, src, ACT.Relu))
        m.wait(m.act, relu)
        return relu, m.A(m.act.activation(out, out, ACT.Square))

    s.open(scratch)
    end, stores = sparse_experts(m, s, scattered, counted, [(ins["ffn0_w1"][e], ins["ffn0_w2"][e]) for e in range(8)], hidden)
    m.arriving = Gather(m, "ffn0", stores)
    m.xt_free = (end,)


def gate_bias(m, b2, ready):
    pair = Ring(2)
    for t in range(0, T, 2):
        i, pair_free = pair.take()
        bank, free = m.banks.take()
        m.wait(m.pe, ready, m.const_ready, *free)
        for j in range(2):
            mm = m.pe.transpose(m.psum[0:8, bank, j * P:(j + 1) * P], m.gates[:, t + j, :], m.ident[:, :])
        m.wait(m.dve, m.M(mm), *pair_free)
        gt = m.V(m.dve.tensor_copy(m.gates_fm[:, i, :], m.psum[0:8, bank, 0:2 * P]))
        m.banks.freed[bank] = (gt,)
        bank, free = m.banks.take()
        m.wait(m.pe, gt, m.small_ready, *free)
        for j in range(2):
            mm = m.pe.matmul(m.psum[:, bank, j * D:(j + 1) * D], m.gates_fm[:, i, j * P:(j + 1) * P], b2[0:8, :],
                             start=True, stop=True)
        used = m.M(mm)
        pair.freed[i] = (used,)
        m.wait(m.dve, used, m.x_ready[t], m.x_ready[t + 1])
        added = m.V(m.dve.tensor_tensor(m.X[:, t:t + 2, :], m.X[:, t:t + 2, :],
                                        m.psum[:, bank, :].rearrange("p (j d) -> p j d", j=2), ALU.add))
        m.banks.freed[bank] = (added,)
        m.x_ready[t:t + 2] = [added] * 2


def layer2_mix(m, ins, scratch):
    m.layer("mix2")
    s = Sparse(m, "mix2", scratch, 8)
    router = Logits(m, 8, chunks_of(m.CTXT, m.small["router_w2"], 8), m.small_ready)
    for g in range(NG):
        router.group(g, m.ctxt_ready[g])
    bank, logits = router.bank, router.done
    m.wait(m.dve, logits)
    lg = m.route[:, :, :]
    added = m.VV(m.dve.tensor_tensor(lg, m.psum[:, bank, 0:T * 8].rearrange("p (t e) -> p t e", t=T),
                                     bcast(m.small["router_b2"][:, :].unsqueeze(1), P, T, 8), ALU.add))
    m.banks.freed[bank] = (added,)
    top2(m, lg, added)
    counted, pos_ready = places(m, s)
    layernorm(m, (), keep=s.LN, fm=False)
    scattered = scatter(m, s, pos_ready)
    v = m.top_v
    m.VV(m.dve.tensor_tensor(v[:, 1, 0:T], v[:, 1, 0:T], v[:, 0, 0:T], ALU.subtract))
    m.wait(m.act, m.VV(m.dve.tensor_tensor(v[:, 0, 0:T], v[:, 0, 0:T], v[:, 0, 0:T], ALU.subtract)))
    m.wait(m.dve, m.A(m.act.activation(v[:, :, 0:T], v[:, :, 0:T], ACT.Exp)))
    m.VV(m.dve.tensor_tensor(m.top_best[:, 0:T], v[:, 0, 0:T], v[:, 1, 0:T], ALU.add))
    m.VV(m.dve.reciprocal(m.top_best[:, 0:T], m.top_best[:, 0:T]))
    m.VV(m.dve.tensor_tensor(v[:, :, 0:T], v[:, :, 0:T], bcast(m.top_best[:, 0:T].unsqueeze(1), P, 2, T), ALU.mult))
    gates_ready = combine(m, m.gates[:, :, :], T)
    gate_bias(m, m.small["b2_2"], gates_ready)

    def hidden(src, out, e, f):
        done = m.A(m.act.activation(out, src, ACT.Relu, bias=m.small["b1_2"][:, e, f:f + 1]))
        return done, done

    s.open(scratch)
    end, stores = sparse_experts(m, s, scattered, counted, [(ins["mix2_w1"][e], ins["mix2_w2"][e]) for e in range(8)], hidden)
    m.arriving = Gather(m, "mix2", stores)


def layer3_ffn(m, ins, scratch):
    m.layer("ffn3")
    s = Sparse(m, "ffn3", scratch, 8)
    router = Logits(m, 8, chunks_of(m.XT, m.small["router_w3"], 8), m.small_ready)
    xt = layernorm(m, m.xt_free, keep=s.LN, add_back=True, each=router.group)
    bank, logits = router.bank, router.done
    m.wait(m.dve, logits)
    probs = m.route[:, :, :]
    added = m.VV(m.dve.tensor_tensor(probs, m.psum[:, bank, 0:T * 8].rearrange("p (t e) -> p t e", t=T),
                                     bcast(m.small["router_b3"][:, :].unsqueeze(1), P, T, 8), ALU.add))
    m.banks.freed[bank] = (added,)
    top2(m, probs, softmax8(m, probs))
    counted, pos_ready = places(m, s)
    scattered = scatter(m, s, pos_ready)
    v = m.top_v
    m.VV(m.dve.tensor_tensor(m.top_best[:, 0:T], v[:, 0, 0:T], v[:, 1, 0:T], ALU.add))
    m.VV(m.dve.tensor_scalar(m.top_best[:, 0:T], m.top_best[:, 0:T], 1e-9, None, ALU.add))
    m.VV(m.dve.reciprocal(m.top_best[:, 0:T], m.top_best[:, 0:T]))
    m.VV(m.dve.tensor_tensor(v[:, :, 0:T], v[:, :, 0:T], bcast(m.top_best[:, 0:T].unsqueeze(1), P, 2, T), ALU.mult))
    gates_ready = combine(m, m.gates[:, :, :], T)
    gate_bias(m, m.small["b2_3"], gates_ready)
    for t in range(T):
        m.wait(m.dve, m.x_ready[t])
        m.x_ready[t] = m.V(m.dve.tensor_tensor(m.X[:, t, :], m.X[:, t, :], m.small["sh_b2_3"][:, :], ALU.add))

    def hidden(src, out, e, f):
        done = m.A(m.act.activation(out, src, ACT.Gelu_apprx_tanh, bias=m.small["b1_3"][:, e, f:f + 1]))
        return done, done

    s.open(scratch)
    end, stores = sparse_experts(m, s, scattered, counted, [(ins["ffn3_w1"][e], ins["ffn3_w2"][e]) for e in range(9)], hidden)
    m.arriving = Gather(m, "ffn3", stores)
    m.xt_free = (end,)



def layer0_mix(m, ins, scratch):
    NH, DH, HB = 4, 64, T * 4
    DEPTH = 5
    m.layer("mix0")
    pe, dve, act, pool = m.pe, m.dve, m.act, m.pool
    with ExitStack() as scratch:
        def sb(name, shape):
            return m.sb(name, shape, F32, scratch)
        gf = sb("gate_pre", [P, T, 8])
        fneg, fexp, lf, a, cs = (sb(n, [P, T, NH]) for n in ("f_neg", "f_exp", "log_f", "a_col", "cs_col"))
        floor = sb("norm_floor", [P, T, NH])
        PAD = 64
        scan = [sb(f"scan{i}", [HB, PAD + P]) for i in range(2)]
        minus_mean = sb("minus_mean", [P, DEPTH, NH])
        E = sb("decay", [P, DEPTH, NH, P])
        C = sb("weights_t", [P, DEPTH, NH, P])
        sums, nrm = sb("c_sum", [P, DEPTH, NH]), sb("normaliser", [P, DEPTH, NH])
        h = sb("h_tile", [P, DEPTH, NH, DH])
        hst, hmv, hr = sb("h_stats", [P, DEPTH, NH, 6]), sb("h_mv", [P, DEPTH, NH, 2]), sb("h_rstd", [P, DEPTH, NH])
        scale1 = sb("out_scale", [P, D])

        m.ctxt_ready = []
        for g in range(NG):
            m.ctxt_ready.append(transposed(m, m.CTXT[:, :, g * GT:(g + 1) * GT], m.CTX[:, g * G:(g + 1) * G, :], m.ctx_ready))
        gate_sources = [(src[:, c, :], m.small["gate_w0"][:, k * DC + c, :]) for k, src in enumerate((m.XT, m.CTXT, m.CTXT)) for c in range(DC)]
        router = Logits(m, 8, gate_sources, m.first_ready)
        xt = layernorm(m, m.xt_free, each=router.group)

        bank = router.bank
        m.wait(dve, router.done, m.first_ready)
        m.VV(dve.tensor_scalar(scale1[:, :], m.small["head_scale0"][:, :], 1.0, None, ALU.add))
        added = m.VV(dve.tensor_tensor(gf[:, :, :], m.psum[:, bank, 0:T * 8].rearrange("p (t e) -> p t e", t=T),
                                       bcast(m.small["gate_b0"][:, :].unsqueeze(1), P, T, 8), ALU.add))
        m.banks.freed[bank] = (added,)
        f = gf[:, :, NH:2 * NH]
        neg = m.V(dve.scalar_tensor_tensor(out=fneg[:, :, :], in0=f, scalar=-1.0, in1=f, op0=ALU.mult, op1=ALU.min))
        m.wait(act, neg)
        m.wait(act, m.A(act.activation(fexp[:, :, :], fneg[:, :, :], ACT.Exp)))
        log = m.A(act.activation(fexp[:, :, :], fexp[:, :, :], ACT.Ln, bias=1.0))
        m.wait(dve, log)
        lfr = m.V(dve.scalar_tensor_tensor(out=lf[:, :, :], in0=f, scalar=0.0, in1=fexp[:, :, :], op0=ALU.min, op1=ALU.subtract))
        bank, free = m.banks.take()
        m.wait(pe, lfr, m.const_ready, *free)
        flat = lf[:, :, :].rearrange("p t h -> p (t h)")
        pe.matmul(m.psum[:, bank, 0:HB], m.tri_incl[:, :], flat, start=True, stop=True)
        m.wait(dve, m.M(pe.matmul(m.psum[:, bank, HB:2 * HB], m.tri_excl[:, :], flat, start=True, stop=True)))
        dve.tensor_copy(cs[:, :, :], m.psum[:, bank, 0:HB].rearrange("p (t h) -> p t h", t=T))
        ar = m.VV(dve.tensor_tensor(a[:, :, :], gf[:, :, 0:NH],
                                    m.psum[:, bank, HB:2 * HB].rearrange("p (t h) -> p t h", t=T), ALU.subtract))
        m.banks.freed[bank] = (ar,)
        bank, free = m.banks.take()
        m.wait(pe, ar, *free)
        tr = m.M(pe.transpose(m.psum[0:HB, bank, 0:P], a[:, :, :].rearrange("p t h -> p (t h)"), m.ident[:, :]))
        dve.memset(scan[0][:, 0:PAD], LOWEST)
        dve.memset(scan[1][:, 0:PAD], LOWEST)
        m.wait(dve, tr)
        got = m.VV(dve.tensor_copy(scan[0][:, PAD:], m.psum[0:HB, bank, 0:P]))
        m.banks.freed[bank] = (got,)
        for k in range(7):
            x, y, s = scan[k % 2], scan[1 - k % 2], 1 << k
            got = m.VV(dve.tensor_tensor(y[:, PAD:], x[:, PAD:], x[:, PAD - s:PAD - s + P], ALU.max))
        top = scan[7 % 2][:, PAD:]
        bank, free = m.banks.take()
        m.wait(pe, got, *free)
        tr = m.M(pe.transpose(m.psum[:, bank, 0:HB], top, m.ident[0:HB, 0:HB]))
        m.wait(dve, tr)
        fl = m.V(dve.tensor_tensor(floor[:, :, :], cs[:, :, :], m.psum[:, bank, 0:HB].rearrange("p (t h) -> p t h", t=T), ALU.add))
        m.banks.freed[bank] = (fl,)
        m.wait(act, fl)
        floor_ready = m.A(act.activation(floor[:, :, :], floor[:, :, :], ACT.Exp, scale=-1.0))

        tail = [()] * DEPTH

        def batch(b):
            i = b % DEPTH
            tok = slice(b * P, (b + 1) * P)
            bm, free = m.banks.take()
            m.wait(pe, got, *free)
            for hd in range(NH):
                r = b * NH + hd
                mm = pe.matmul(m.psum[:, bm, hd * P:(hd + 1) * P], bcast(m.ident[0:HB, r:r + 1], HB, P), top, start=True, stop=True)
            max_full = m.M(mm)
            yield
            m.wait(act, max_full, ar, *tail[i])
            for hd in range(NH):
                ex = m.A(act.activation(E[:, i, hd, :], m.psum[:, bm, hd * P:(hd + 1) * P], ACT.Exp, scale=-1.0, bias=a[:, b, hd:hd + 1]))
            m.banks.freed[bm] = (ex,)
            m.wait(pool, ex)
            cut = m.Q(pool.affine_select(out=E[:, i], in_=E[:, i], compare_op=ALU.is_ge, fill=0.0,
                                         base=0, pattern=[[0, NH], [1, P]], channel_multiplier=-1))
            qk = []
            for lo in range(2):
                bq, free = m.banks.take()
                m.wait(pe, *free)
                for c in range(DC):
                    part = slice(lo * DH, (lo + 1) * DH)
                    mm = pe.matmul(m.psum[:, bq, c * P:(c + 1) * P], m.CTXT[part, c, tok], m.XT[part, c, tok], start=True, stop=True)
                qk.append((bq, m.M(mm)))
            yield
            m.wait(dve, cut)
            for lo, (bq, full) in enumerate(qk):
                m.wait(dve, full)
                c_ready = m.V(dve.scalar_tensor_tensor(
                    out=C[:, i, lo::2, :], in0=m.psum[:, bq, 0:2 * P].rearrange("p (c s) -> p c s", c=DC),
                    scalar=DH ** -0.5, in1=E[:, i, lo::2, :], op0=ALU.mult, op1=ALU.mult))
                m.banks.freed[bq] = (c_ready,)
            bo, free = m.banks.take()
            m.wait(pe, c_ready, *free)
            for hd in range(NH):
                pe.matmul(m.psum[:, bo, hd * DH:(hd + 1) * DH], C[:, i, hd, :], m.CTX[:, b, hd * DH:(hd + 1) * DH], start=True, stop=True)
                mm = pe.matmul(m.psum[:, bo, D + hd:D + hd + 1], C[:, i, hd, :], m.ones[:, :], start=True, stop=True)
            c_used = m.M(mm)
            tail[i] = (c_used,)
            yield
            m.wait(dve, c_used, floor_ready)
            m.VV(dve.tensor_copy(sums[:, i], m.psum[:, bo, D:D + NH]))
            m.VV(dve.scalar_tensor_tensor(out=nrm[:, i], in0=sums[:, i], scalar=-1.0, in1=sums[:, i], op0=ALU.mult, op1=ALU.max))
            m.VV(dve.tensor_tensor(nrm[:, i], nrm[:, i], floor[:, b, :], ALU.max))
            m.VV(dve.tensor_scalar(nrm[:, i], nrm[:, i], 1e-8, None, ALU.add))
            m.VV(dve.reciprocal(nrm[:, i], nrm[:, i]))
            hv = m.VV(dve.tensor_tensor(h[:, i], m.psum[:, bo, 0:D].rearrange("p (h d) -> p h d", h=NH),
                                        bcast(nrm[:, i].unsqueeze(2), P, NH, DH), ALU.mult))
            m.banks.freed[bo] = (hv,)
            for hd in range(NH):
                st = dve.bn_stats(hst[:, i, hd, :], h[:, i, hd, :])
            m.VV(st)
            for hd in range(NH):
                ag = dve.bn_aggr(hmv[:, i, hd, :], hst[:, i, hd, :])
            m.VV(ag)
            e = m.V(dve.tensor_scalar(hr[:, i, :], hmv[:, i, :, 1], LN_EPS, None, ALU.add))
            m.wait(pool, e, m.filled)
            powered = m.Q(pool.tensor_tensor(hr[:, i, :], hr[:, i, :], m.minus_half[:, 0:NH], ALU.pow))
            yield
            m.wait(dve, powered)
            m.wait(act, m.V(dve.scalar_tensor_tensor(out=minus_mean[:, i], in0=hmv[:, i, :, 0], scalar=-1.0, in1=hr[:, i],
                                                     op0=ALU.mult, op1=ALU.mult)))
            for hd in range(NH):
                nm = m.A(act.activation(h[:, i, hd, :], h[:, i, hd, :], ACT.Identity, bias=minus_mean[:, i, hd:hd + 1],
                                        scale=hr[:, i, hd:hd + 1]))
            m.wait(pool, nm)
            hf = h[:, i].rearrange("p h d -> p (h d)")
            scaled = m.Q(pool.tensor_tensor(hf, hf, scale1[:, :], ALU.mult))
            yield
            m.wait(dve, scaled)
            m.x_ready[b] = m.V(dve.tensor_tensor(m.X[:, b, :], m.X[:, b, :], hf, ALU.add))

        interleave([batch(b) for b in range(T)], DEPTH)
        c_used = tail[(T - 1) % DEPTH][0]
        m.xt_free = (c_used,)
        m.barrier()



def layer1_mix(m, ins, scratch):
    NH, DH = 4, 64
    HALF = DH // 2
    HK = NH + 2
    DEPTH = 4
    m.layer("mix1")
    pe, dve, act, pool = m.pe, m.dve, m.act, m.pool

    def sb(name, shape, dt=F32):
        return m.sb(name, shape, dt, scratch)
    S_mask = m.counter("load_mask", 16)
    mask8 = sb("mask8", [P, T * P], U8)
    fill = sb("fill", [P, DEPTH, P])
    scale1 = sb("rms_scale1", [P, D])
    ms = sb("mean_sq", [P, T, 2])
    xn = sb("xn", [P, DEPTH, 2, D])
    xnT = sb("xnT", [P, DEPTH, 2, DC, P])
    qr = sb("q_rot", [P, DEPTH, HK, 2, HALF])
    rot = sb("rot", [P, DEPTH, HK, 2, HALF])
    v = sb("v_tok", [P, DEPTH, DH])
    qT = sb("q_t", [P, DEPTH, 3, P])
    L = sb("logits", [P, DEPTH, NH, P])
    mx, sm = sb("row_max", [P, DEPTH, NH]), sb("row_sum", [P, DEPTH, NH])
    pT = sb("probs_t", [P, DEPTH, NH, P])
    st, mv, rs = sb("l_st", [P, T, 6]), sb("l_mv", [P, T, 2]), sb("l_rs", [P, T])

    mask_ready = S_mask.after(m.sp.dma_start(mask8[:, :], ins["mask"][0].partition_broadcast(P)))
    m.wait(dve, m.small_ready)
    m.VV(dve.tensor_scalar(scale1[:, :], m.small["rms_scale"][:, :], 1.0, None, ALU.add))
    rstd_ready = []

    def prepare(g):
        tiles = slice(g * G, (g + 1) * G)
        if m.arriving:
            m.arriving.need(g)
        m.wait(dve, *m.x_ready[tiles])
        for t in range(g * G, (g + 1) * G):
            s_ = dve.bn_stats(st[:, t, :], m.X[:, t, :])
        m.VV(s_)
        for t in range(g * G, (g + 1) * G):
            s_ = dve.bn_aggr(mv[:, t, :], st[:, t, :])
        m.VV(s_)
        m.wait(pool, m.V(dve.tensor_scalar(rs[:, tiles], mv[:, tiles, 1], LN_EPS, None, ALU.add)), m.filled)
        rstd_ready.append(m.Q(pool.tensor_tensor(rs[:, tiles], rs[:, tiles], m.minus_half[:, 0:G], ALU.pow)))

    prepare(0)
    m.wait(act, m.ctx_ready)

    def batch(b):
        i = b % DEPTH
        tok = slice(b * P, (b + 1) * P)
        if b % G == 1 and b // G + 1 < NG:
            prepare(b // G + 1)
        m.wait(dve, m.ctx_ready, rstd_ready[b // G])
        xl = m.V(dve.tensor_scalar(xn[:, i, 0, :], m.X[:, b, :], mv[:, b, 0:1], rs[:, b:b + 1], ALU.subtract, ALU.mult))
        act.activation(L[:, i, 2:4, :].rearrange("p h s -> p (h s)"), m.CTX[:, b, :], ACT.Square, accum_out=ms[:, b, 1:2])
        m.wait(act, xl)
        squared = m.A(act.activation(L[:, i, 0:2, :].rearrange("p h s -> p (h s)"), xn[:, i, 0, :], ACT.Square, accum_out=ms[:, b, 0:1]))
        yield
        m.wait(dve, squared)
        m.wait(pool, m.V(dve.tensor_scalar(ms[:, b, :], ms[:, b, :], 1.0 / D, RMS_EPS, ALU.mult, ALU.add)))
        powered = m.Q(pool.tensor_tensor(ms[:, b, :], ms[:, b, :], m.minus_half[:, 0:2], ALU.pow))
        yield
        m.wait(dve, powered)
        for k, src in enumerate((xn[:, i, 0, :], m.CTX[:, b, :])):
            nx = m.V(dve.scalar_tensor_tensor(out=xn[:, i, k, :], in0=src, scalar=ms[:, b, k:k + 1], in1=scale1[:, :],
                                              op0=ALU.mult, op1=ALU.mult))
        bank, free = m.banks.take()
        m.wait(pe, nx, m.const_ready, *free)
        for k in range(2):
            for c in range(DC):
                mm = pe.transpose(m.psum[:, bank, (k * DC + c) * P:(k * DC + c + 1) * P], xn[:, i, k, c * P:(c + 1) * P], m.ident[:, :])
        xn_used = m.M(mm)
        yield
        m.wait(act, xn_used)
        xt = m.A(act.activation(xnT[:, i].rearrange("p k c s -> p (k c s)"), m.psum[:, bank, :], ACT.Copy))
        m.banks.freed[bank] = (xt,)
        bank, free = m.banks.take()
        m.wait(pe, xt, m.small_ready, *free)
        for c in range(DC):
            pe.matmul(m.psum[:, bank, 0:D], xnT[:, i, 0, c, :], m.small["q_w1"][:, c, :], start=(c == 0), stop=(c == DC - 1))
        for c in range(DC):
            mm = pe.matmul(m.psum[:, bank, D:D + 3 * DH], xnT[:, i, 1, c, :], m.small["kv_w1"][:, c, :], start=(c == 0), stop=(c == DC - 1))
        qkv = m.M(mm)
        yield
        m.wait(dve, qkv)
        x = m.psum[:, bank, 0:HK * DH].rearrange("p (h t d) -> p h t d", h=HK, t=2)
        cos = bcast(m.small["cos"][:, :, :].unsqueeze(2), P, HK, 2, HALF)
        m.V(dve.tensor_tensor(qr[:, i], x, cos, ALU.mult))
        for half in range(2):
            m.V(dve.tensor_tensor(rot[:, i, :, half, :], x[:, :, 1 - half, :], m.small["sin"][:, :, half, :], ALU.mult))
        vr = m.VV(dve.tensor_copy(v[:, i, :], m.psum[:, bank, HK * DH:(HK + 1) * DH]))
        m.banks.freed[bank] = (vr,)
        qr_ready = m.V(dve.tensor_tensor(qr[:, i], qr[:, i], rot[:, i], ALU.add))
        bank, free = m.banks.take()
        m.wait(pe, qr_ready, *free)
        flat = qr[:, i].rearrange("p h t d -> p (h t d)")
        for c in range(3):
            mm = pe.transpose(m.psum[:, bank, c * P:(c + 1) * P], flat[:, c * P:(c + 1) * P], m.ident[:, :])
        turned = m.M(mm)
        yield
        m.wait(act, turned)
        qt = m.A(act.activation(qT[:, i].rearrange("p c s -> p (c s)"), m.psum[:, bank, 0:3 * P], ACT.Copy))
        m.banks.freed[bank] = (qt,)
        full = []
        for lo in range(2):
            bank, free = m.banks.take()
            m.wait(pe, qt, *free)
            part = slice(lo * DH, (lo + 1) * DH)
            for c in range(DC):
                mm = pe.matmul(m.psum[:, bank, c * P:(c + 1) * P], qT[part, i, c, :], qT[part, i, 2, :], start=True, stop=True)
            full.append((bank, m.M(mm)))
        m.wait(pool, mask_ready, squared)
        filled = m.Q(pool.tensor_scalar(fill[:, i, :], mask8[:, tok], -1.0, -MASK_FILL, ALU.add, ALU.mult))
        yield
        m.wait(dve, squared, mask_ready, filled)
        for lo, (bank, mark) in enumerate(full):
            m.wait(dve, mark)
            lg = m.V(dve.scalar_tensor_tensor(out=L[:, i, lo::2, :], in0=m.psum[:, bank, 0:2 * P].rearrange("p (c s) -> p c s", c=DC),
                                              scalar=DH ** -0.5, in1=bcast(mask8[:, tok].unsqueeze(1), P, 2, P),
                                              op0=ALU.mult, op1=ALU.mult))
            m.banks.freed[bank] = (lg,)
        m.wait(dve, lg)
        m.VV(dve.tensor_tensor(L[:, i], L[:, i], bcast(fill[:, i, :].unsqueeze(1), P, NH, P), ALU.add))
        top = m.V(dve.tensor_reduce(mx[:, i], L[:, i], AX.X, ALU.max, negate=True))
        m.wait(act, top)
        for hd in range(NH):
            ex = m.A(act.activation(L[:, i, hd, :], L[:, i, hd, :], ACT.Exp, bias=mx[:, i, hd:hd + 1], accum_out=sm[:, i, hd:hd + 1]))
        bank, free = m.banks.take()
        m.wait(pe, ex, *free)
        for hd in range(NH):
            mm = pe.transpose(m.psum[:, bank, hd * P:(hd + 1) * P], L[:, i, hd, :], m.ident[:, :])
        turned = m.M(mm)
        yield
        m.wait(dve, ex)
        m.V(dve.reciprocal(sm[:, i], sm[:, i]))
        m.wait(act, turned)
        pt = m.A(act.activation(pT[:, i].rearrange("p h s -> p (h s)"), m.psum[:, bank, :], ACT.Copy))
        m.banks.freed[bank] = (pt,)
        bank, free = m.banks.take()
        m.wait(pe, pt, vr, *free)
        for hd in range(NH):
            mm = pe.matmul(m.psum[:, bank, hd * DH:(hd + 1) * DH], pT[:, i, hd, :], v[:, i, :], start=True, stop=True)
        heads = m.M(mm)
        yield
        enc, encT = xn[:, i, 0, :], xnT[:, i, 0]
        m.wait(dve, heads, (m.S_dve, m.S_dve.value))
        en = m.V(dve.tensor_tensor(enc.rearrange("p (h d) -> p h d", h=NH), m.psum[:, bank, 0:D].rearrange("p (h d) -> p h d", h=NH),
                                   bcast(sm[:, i].unsqueeze(2), P, NH, DH), ALU.mult))
        m.banks.freed[bank] = (en,)
        bank, free = m.banks.take()
        m.wait(pe, en, *free)
        for c in range(DC):
            mm = pe.transpose(m.psum[:, bank, c * P:(c + 1) * P], enc[:, c * P:(c + 1) * P], m.ident[:, :])
        turned = m.M(mm)
        yield
        m.wait(act, turned)
        et = m.A(act.activation(encT.rearrange("p c s -> p (c s)"), m.psum[:, bank, 0:D], ACT.Copy))
        m.banks.freed[bank] = (et,)
        bank, free = m.banks.take()
        m.wait(pe, et, *free)
        for c in range(DC):
            mm = pe.matmul(m.psum[:, bank, 0:D], encT[:, c, :], m.small["out_w1"][:, c, :], start=(c == 0), stop=(c == DC - 1))
        out = m.M(mm)
        yield
        m.wait(dve, out)
        m.x_ready[b] = m.V(dve.tensor_tensor(m.X[:, b, :], m.X[:, b, :], m.psum[:, bank, 0:D], ALU.add))
        m.banks.freed[bank] = (m.x_ready[b],)
        m.wait(act, out)

    interleave([batch(b) for b in range(T)], DEPTH)
    m.barrier()



def layer1_ffn(m, ins, scratch):
    NH, NE, DP = 8, 8, 128
    SCALE = 1.0 / float(DP) ** 0.5
    NQ, NV = 2 * DC * DP, DC * NE * DP
    CH = 512
    m.layer("ffn1")
    pe, dve, act, pool = m.pe, m.dve, m.act, m.pool

    m.wide.close()

    def sb(name, shape, dt=F32):
        return m.sb(name, shape, dt, scratch)
    xt_hi, xt_lo = sb("xt_hi", [P, DC, T * P], F32R), sb("xt_lo", [P, DC, T * P], F32R)
    xt_raw = sb("xt_raw", [P, DC, GT])
    m.LN, m.ln_ring = sb("LN_ffn1", [P, 1, G, D]), Ring(1)
    qk_hi, qk_lo = sb("qk_hi", [P, 2, NQ], F32R), sb("qk_lo", [P, 2, NQ], F32R)
    w_hi, w_lo = sb("w_hi", [P, 2 * NV], F32R), sb("w_lo", [P, 2 * NV], F32R)
    RAW = 6
    raw = sb("w_raw", [P, RAW, CH])
    raw_ring = Ring(RAW)
    S_raw = [m.counter(f"load_raw{k}", 16) for k in range(RAW)]
    gates = sb("gates1", [P, T, 2 * NH, NE])
    den = sb("den1", [P, G * 2 * NH])
    qT, kT = sb("qT1", [P, GT]), sb("kT1", [P, GT])
    v = sb("v1", [P, G, DP])
    cT_hi, cT_lo = sb("cT_hi", [P, GT], F32R), sb("cT_lo", [P, GT], F32R)
    S = sb("scores1", [P, G, P])
    sT = sb("scoresT1", [P, G * P])
    mx, sm = sb("max1", [P, 2, G]), sb("sum1", [P, 2, G])
    out_gate = sb("out_gate", [P, 2, G, NE])
    part_out = sb("part_out", [P, 2, 2, D])
    part_v = sb("part_v", [P, 1, 4, DP])

    gate_pre, raw_free = [], [()]

    def to_parts(g, tiles, ready):
        m.wait(act, *raw_free[-1])
        xt = transposed(m, xt_raw[:, :, :], tiles, ready)
        bank, free = m.banks.take()
        m.wait(pe, m.small_ready, xt, *free)
        for j in range(G):
            for c in range(DC):
                mm = pe.matmul(m.psum[:, bank, j * P:(j + 1) * P], xt_raw[:, c, j * P:(j + 1) * P], m.small["sel_w1"][:, c, :],
                               start=(c == 0), stop=(c == DC - 1))
        read = m.M(mm)
        tok = slice(g * GT, (g + 1) * GT)
        parts = split(m, xt_hi[:, :, tok], xt_lo[:, :, tok], xt_raw[:, :, :], xt, (), pool)
        m.wait(act, read)
        sg = m.A(act.activation(gates[:, g * G:(g + 1) * G].rearrange("p t h e -> p (t h e)"), m.psum[:, bank, :], ACT.Sigmoid))
        m.banks.freed[bank] = (sg,)
        gate_pre.append(sg)
        raw_free.append((read, parts))
        return parts

    def route(g):
        n = G * 2 * NH
        part = gates[:, g * G:(g + 1) * G].rearrange("p t h e -> p (t h) e")
        top2(m, part, gate_pre[g])
        v2 = m.top_v
        m.VV(dve.tensor_tensor(den[:, :], v2[:, 0, 0:n], v2[:, 1, 0:n], ALU.add))
        m.VV(dve.tensor_scalar(den[:, :], den[:, :], 1e-9, None, ALU.max))
        m.VV(dve.reciprocal(den[:, :], den[:, :]))
        m.wait(dve, m.small_ready)
        m.VV(dve.tensor_scalar(den[:, :], den[:, :], m.small["route_scale"][:, 0:1], None, ALU.mult))
        m.VV(dve.tensor_tensor(v2[:, :, 0:n], v2[:, :, 0:n], bcast(den[:, :].unsqueeze(1), P, 2, n), ALU.mult))
        return combine(m, part, n)

    qk_w, v_w, o_w = {}, {}, {}
    used = dict(qk=[(), ()], v=(), o=[()] * (NV // CH))

    pieces = []
    for hd in range(NH):
        pieces.append((ins["ffn1_q"][hd], ins["ffn1_k"][hd]))
        for src in (ins["ffn1_v"][hd], ins["ffn1_o"][hd]):
            pieces += [(src[:, at:at + CH],) for at in range(0, NV, CH)]
    on_way = []

    def fetch():
        if pieces:
            k, free = raw_ring.take()
            m.wait(m.sp, *free)
            at = 0
            for src in pieces.pop(0):
                mark = S_raw[k].after(m.sp.dma_start(raw[:, k, at:at + src.shape[1]], src))
                at += src.shape[1]
            on_way.append((k, mark))

    def split_piece(hi, lo, free, lo_engine):
        k, loaded = on_way.pop(0)
        done = split(m, hi, lo, raw[:, k, :], loaded, free, lo_engine)
        raw_ring.freed[k] = (done,)
        fetch()
        return done

    def split_qk(hd):
        qk_w[hd] = split_piece(qk_hi[:, hd % 2, :], qk_lo[:, hd % 2, :], used["qk"][hd % 2], pool)

    def split_v(hd):
        v_w[hd] = [split_piece(w_hi[:, at:at + CH], w_lo[:, at:at + CH], used["v"], dve if at // CH % 2 else pool)
                   for at in range(0, NV, CH)]

    def split_o(hd):
        o_w[hd] = [split_piece(w_hi[:, NV + k * CH:NV + (k + 1) * CH], w_lo[:, NV + k * CH:NV + (k + 1) * CH],
                               used["o"][k], dve if k % 2 else pool) for k in range(NV // CH)]

    for _ in range(RAW):
        fetch()
    x_split = layernorm(m, (), to=to_parts)

    last = dict(scores=(), av=(), cT=())
    parts, v_parts = Ring(2), Ring(1)

    def queries_keys(hd, g):
        tok = slice(g * GT, (g + 1) * GT)
        m.wait(pe, x_split[g], qk_w[hd])
        for at, dst in ((0, qT), (DC * DP, kT)):
            bank, free = m.banks.take()
            m.wait(pe, *free)
            for c in range(DC):
                col = slice(at + c * DP, at + (c + 1) * DP)
                mm = product(m, m.psum[:, bank, :], (qk_hi[:, hd % 2, col], qk_lo[:, hd % 2, col]),
                             (xt_hi[:, c, tok], xt_lo[:, c, tok]), c == 0, c == DC - 1)
            full = m.M(mm)
            m.wait(act, full, *last["scores"])
            qk = m.A(act.activation(dst[:, :], m.psum[:, bank, :], ACT.Copy))
            m.banks.freed[bank] = (qk,)
        used["qk"][hd % 2] = (full,)
        return qk

    def scores(hd, g, i, qk):
        bank, free = m.banks.take()
        m.wait(pe, qk, *free)
        for j in range(G):
            tok = slice(j * P, (j + 1) * P)
            mm = pe.matmul(m.psum[:, bank, tok], qT[:, tok], kT[:, tok], start=True, stop=True)
        full = m.M(mm)
        last["scores"] = (full,)
        m.wait(dve, full)
        m.VV(dve.tensor_reduce(mx[:, i], m.psum[:, bank, :].rearrange("p (j s) -> p j s", j=G), AX.X, ALU.max, negate=True))
        top = m.V(dve.tensor_scalar(mx[:, i], mx[:, i], SCALE, None, ALU.mult))
        m.wait(act, top, *last["S"])
        for j in range(G):
            ex = m.A(act.activation(S[:, j, :], m.psum[:, bank, j * P:(j + 1) * P], ACT.Exp, bias=mx[:, i, j:j + 1],
                                    scale=SCALE, accum_out=sm[:, i, j:j + 1]))
        m.banks.freed[bank] = (ex,)
        return ex

    def out_gates(hd, g, i, ex):
        m.wait(dve, ex)
        m.VV(dve.reciprocal(sm[:, i], sm[:, i]))
        return m.V(dve.tensor_tensor(out_gate[:, i], gates[:, g * G:(g + 1) * G, NH + hd, :],
                                     bcast(sm[:, i].unsqueeze(2), P, G, NE), ALU.mult))

    def values(hd, g, j):
        t = g * G + j
        for half in range(2):
            bank, free = m.banks.take()
            m.wait(pe, *free)
            for c in range(DC):
                at = (c * 2 + half) * CH
                m.wait(pe, v_w[hd][c * 2 + half])
                tok = slice(t * P, (t + 1) * P)
                mm = product(m, m.psum[:, bank, :], (xt_hi[:, c, tok], xt_lo[:, c, tok]),
                             (w_hi[:, at:at + CH], w_lo[:, at:at + CH]), c == 0, c == DC - 1)
            full = m.M(mm)
            src = [m.psum[:, bank, q * DP:(q + 1) * DP] for q in range(4)]
            gate = [gates[:, t, hd, e:e + 1] for e in range(half * 4, half * 4 + 4)]
            if half == 0:
                m.wait(dve, full, gates_ready[g], *last["av"])
                vr = m.VV(dve.tensor_scalar(v[:, j, :], src[0], gate[0], None, ALU.mult))
                for q in range(1, 4):
                    vr = m.VV(dve.scalar_tensor_tensor(out=v[:, j, :], in0=src[q], scalar=gate[q], in1=v[:, j, :],
                                                       op0=ALU.mult, op1=ALU.add))
                m.banks.freed[bank] = (vr,)
            else:
                b, part_free = v_parts.take()
                m.wait(act, full, gates_ready[g], *part_free)
                for q in range(4):
                    scaled = m.A(act.activation(part_v[:, b, q, :], src[q], ACT.Copy, scale=gate[q]))
                m.banks.freed[bank] = (scaled,)
                m.wait(pool, scaled)
                m.wait(pool, m.Q(pool.tensor_tensor(part_v[:, b, 0:2, :], part_v[:, b, 0:2, :], part_v[:, b, 2:4, :], ALU.add)))
                m.wait(pool, m.Q(pool.tensor_tensor(part_v[:, b, 0, :], part_v[:, b, 0, :], part_v[:, b, 1, :], ALU.add)), vr)
                vr = m.Q(pool.tensor_tensor(v[:, j, :], v[:, j, :], part_v[:, b, 0, :], ALU.add))
                v_parts.freed[b] = (vr,)
        used["v"] = (full,)
        return vr

    def turn(ex):
        bank, free = m.banks.take()
        m.wait(pe, ex, *free)
        for j in range(G):
            mm = pe.transpose(m.psum[:, bank, j * P:(j + 1) * P], S[:, j, :], m.ident[:, :])
        full = m.M(mm)
        last["S"] = (full,)
        m.wait(act, full, *last["av"])
        st = m.A(act.activation(sT[:, :], m.psum[:, bank, :], ACT.Copy))
        m.banks.freed[bank] = (st,)
        return st

    def attend(st, vr):
        bank, free = m.banks.take()
        m.wait(pe, st, vr, *free)
        for j in range(G):
            mm = pe.matmul(m.psum[:, bank, j * P:(j + 1) * P], v[:, j, :], sT[:, j * P:(j + 1) * P], start=True, stop=True)
        full = m.M(mm)
        last["av"] = (full,)
        m.wait(act, full, *last["cT"])
        high = m.A(act.activation(cT_hi[:, :], m.psum[:, bank, :], ACT.Copy))
        m.wait(dve, high)
        low = m.V(dve.tensor_tensor(cT_lo[:, :], m.psum[:, bank, :], cT_hi[:, :].bitcast(F32), ALU.subtract))
        m.banks.freed[bank] = (low,)
        return low

    def outputs(hd, g, i, j, ct, og):
        t = g * G + j
        tok = slice(j * P, (j + 1) * P)
        m.wait(pe, ct)
        for k in range(4):
            bank, free = m.banks.take()
            m.wait(pe, o_w[hd][k], *free)
            at = NV + k * CH
            mm = product(m, m.psum[:, bank, :], (cT_hi[:, tok], cT_lo[:, tok]),
                         (w_hi[:, at:at + CH], w_lo[:, at:at + CH]), True, True)
            full = m.M(mm)
            used["o"][k] = (full,)
            gate = [out_gate[:, i, j, e:e + 1] for e in (2 * k, 2 * k + 1)]
            src = [m.psum[:, bank, q * D:(q + 1) * D] for q in range(2)]
            if k < 3:
                m.wait(dve, full, og, m.x_ready[t])
                for q in range(2):
                    added = m.VV(dve.scalar_tensor_tensor(out=m.X[:, t, :], in0=src[q], scalar=gate[q], in1=m.X[:, t, :],
                                                          op0=ALU.mult, op1=ALU.add))
                m.banks.freed[bank] = (added,)
            else:
                b, part_free = parts.take()
                m.wait(act, full, og, *part_free)
                for q in range(2):
                    scaled = m.A(act.activation(part_out[:, b, q, :], src[q], ACT.Copy, scale=gate[q]))
                m.banks.freed[bank] = (scaled,)
                m.wait(pool, scaled)
                summed = m.Q(pool.tensor_tensor(part_out[:, b, 0, :], part_out[:, b, 0, :], part_out[:, b, 1, :], ALU.add))
                m.wait(pool, summed, added)
                m.x_ready[t] = m.Q(pool.tensor_tensor(m.X[:, t, :], m.X[:, t, :], part_out[:, b, 0, :], ALU.add))
                parts.freed[b] = (m.x_ready[t],)
        last["cT"] = (full,)
        return full

    last["S"] = ()
    split_qk(0)
    split_v(0)
    split_o(0)
    gates_ready = [route(0)]
    before = None
    for n in range(NH * NG):
        hd, g, i = n // NG, n % NG, n % 2

        def out(j):
            return outputs(*before[:3], j, *before[3:]) if before else None

        qk = queries_keys(hd, g)
        out(0)
        ex = scores(hd, g, i, qk)
        values(hd, g, 0)
        out(1)
        og = out_gates(hd, g, i, ex)
        values(hd, g, 1)
        st = turn(ex)
        values(hd, g, 2)
        out(2)
        vr = values(hd, g, 3)
        if g == NG - 1 and hd + 1 < NH:
            split_v(hd + 1)
        done = out(3)
        if g == 0:
            if hd:
                split_o(hd)
        if g == 2 and hd + 1 < NH:
            split_qk(hd + 1)
        if len(gates_ready) < NG:
            gates_ready.append(route(len(gates_ready)))
        before = (hd, g, i, attend(st, vr), og)
    for j in range(G):
        done = out(j)
    m.xt_free = ()
    m.barrier()



def layer2_ffn(m, ins, scratch):
    NE = 16
    m.layer("ffn2")
    pe, dve, act, pool = m.pe, m.dve, m.act, m.pool
    router = Logits(m, NE, chunks_of(m.XT, m.small["proj2"], NE), m.small_ready)
    xt = layernorm(m, m.xt_free, each=router.group)
    bank, logits = router.bank, router.done
    if m.arriving:
        m.arriving.close()
    with ExitStack() as scratch:
        def sb(name, shape):
            return m.sb(name, shape, F32, scratch)
        z = sb("z", [P, T, NE])
        zs = sb("z_sorted", [P, T, NE])
        zr = sb("z_rest", [P, T, NE])
        st, mv, rs = sb("z_st", [P, T, 6]), sb("z_mv", [P, T, 2]), sb("z_rs", [P, T])
        c1 = [sb(f"cum{i}", [P, T, NE]) for i in range(2)]
        c2 = [sb(f"cumsq{i}", [P, T, NE]) for i in range(2)]
        ik = sb("inv_count", [P, NE])
        mean, tau, hit = sb("mean", [P, T, NE]), sb("tau", [P, T, NE]), sb("hit", [P, T, NE])
        zt, sup = sb("z_top", [P, T]), sb("support", [P, T])
        aT = sb("a_t", [NE, T * P])
        g1, g2, z1 = sb("g1", [P, 2, GT]), sb("g2", [P, 2, GT]), sb("z1", [P, 2, GT])
        z2 = sb("z2", [P, 2, GT])
        shape = [P, T, NE]
        m.wait(dve, logits)
        cp = m.VV(dve.tensor_copy(z[:, :, :], m.psum[:, bank, 0:T * NE].rearrange("p (t e) -> p t e", t=T)))
        m.banks.freed[bank] = (cp,)
        for t in range(T):
            s_ = dve.bn_stats(st[:, t, :], z[:, t, :])
        m.VV(s_)
        for t in range(T):
            s_ = dve.bn_aggr(mv[:, t, :], st[:, t, :])
        m.VV(s_)
        rsqrt(m, rs[:, :], mv[:, :, 1], LN_EPS, None)
        m.VV(dve.tensor_tensor(z[:, :, :], z[:, :, :], bcast(mv[:, :, 0:1], *shape), ALU.subtract))
        m.VV(dve.tensor_tensor(z[:, :, :], z[:, :, :], bcast(rs[:, :].unsqueeze(2), *shape), ALU.mult))
        m.VV(dve.tensor_scalar(z[:, :, :], z[:, :, :], 0.5, None, ALU.mult))
        m.VV(dve.tensor_reduce(zt[:, :], z[:, :, :], AX.X, ALU.max))
        m.VV(dve.tensor_tensor(z[:, :, :], z[:, :, :], bcast(zt[:, :].unsqueeze(2), *shape), ALU.subtract))
        for t in range(T):
            s_ = dve.max(zs[:, t, 0:8], z[:, t, :])
        m.VV(s_)
        for t in range(T):
            s_ = dve.match_replace(zr[:, t, :], zs[:, t, 0:8], z[:, t, :], LOWEST)
        m.VV(s_)
        for t in range(T):
            s_ = dve.max(zs[:, t, 8:16], zr[:, t, :])
        m.VV(s_)
        m.VV(dve.reciprocal(ik[:, :], m.count16[:, :]))
        m.VV(dve.tensor_copy(c1[0][:, :, :], zs[:, :, :]))
        m.VV(dve.tensor_tensor(c2[0][:, :, :], zs[:, :, :], zs[:, :, :], ALU.mult))
        for k in range(4):
            s = 1 << k
            for c in (c1, c2):
                x, y = c[k % 2], c[1 - k % 2]
                dve.tensor_copy(y[:, :, 0:s], x[:, :, 0:s])
                m.VV(dve.tensor_tensor(y[:, :, s:], x[:, :, s:], x[:, :, 0:NE - s], ALU.add))
        kb = bcast(m.count16[:, :].unsqueeze(1), *shape)
        ikb = bcast(ik[:, :].unsqueeze(1), *shape)
        m.VV(dve.tensor_tensor(mean[:, :, :], c1[0][:, :, :], ikb, ALU.mult))
        m.VV(dve.tensor_tensor(c2[0][:, :, :], c2[0][:, :, :], ikb, ALU.mult))
        m.VV(dve.tensor_tensor(c1[1][:, :, :], mean[:, :, :], mean[:, :, :], ALU.mult))
        m.VV(dve.tensor_tensor(c2[0][:, :, :], c2[0][:, :, :], c1[1][:, :, :], ALU.subtract))
        m.VV(dve.tensor_tensor(c2[0][:, :, :], c2[0][:, :, :], kb, ALU.mult))
        m.VV(dve.tensor_scalar(c2[0][:, :, :], c2[0][:, :, :], -1.0, 1.0, ALU.mult, ALU.add))
        m.VV(dve.tensor_tensor(c2[0][:, :, :], c2[0][:, :, :], ikb, ALU.mult))
        dl = m.V(dve.tensor_scalar(c2[0][:, :, :], c2[0][:, :, :], 0.0, None, ALU.max))
        m.wait(act, dl)
        m.wait(dve, m.A(act.activation(c2[1][:, :, :], c2[0][:, :, :], ACT.Sqrt)))
        m.VV(dve.tensor_tensor(tau[:, :, :], mean[:, :, :], c2[1][:, :, :], ALU.subtract))
        m.VV(dve.tensor_tensor(hit[:, :, :], tau[:, :, :], zs[:, :, :], ALU.is_le))
        m.VV(dve.tensor_reduce(sup[:, :], hit[:, :, :], AX.X, ALU.add))
        m.VV(dve.tensor_tensor(hit[:, :, :], kb, bcast(sup[:, :].unsqueeze(2), *shape), ALU.is_equal))
        m.VV(dve.tensor_tensor(hit[:, :, :], hit[:, :, :], tau[:, :, :], ALU.mult))
        m.VV(dve.tensor_reduce(zt[:, :], hit[:, :, :], AX.X, ALU.add))
        m.VV(dve.tensor_tensor(z[:, :, :], z[:, :, :], bcast(zt[:, :].unsqueeze(2), *shape), ALU.subtract))
        m.VV(dve.tensor_scalar(z[:, :, :], z[:, :, :], 0.0, None, ALU.max))
        ar = m.VV(dve.tensor_tensor(z[:, :, :], z[:, :, :], z[:, :, :], ALU.mult))
        for g in range(NG):
            bank, free = m.banks.take()
            m.wait(pe, ar, m.const_ready, *free)
            for j in range(G):
                mm = pe.transpose(m.psum[0:NE, bank, j * P:(j + 1) * P], z[:, g * G + j, :], m.ident[:, :])
            m.wait(act, m.M(mm))
            at = m.A(act.activation(aT[:, g * GT:(g + 1) * GT], m.psum[0:NE, bank, :], ACT.Copy))
            m.banks.freed[bank] = (at,)
        z2_free = [(), ()]
        for g in range(NG):
            i = g % 2
            tok = slice(g * GT, (g + 1) * GT)
            for w, dst in ((m.small["C1"], g1), (m.small["C2"], g2)):
                bank, free = m.banks.take()
                m.wait(pe, at, m.small_ready, *free)
                mm = pe.matmul(m.psum[:, bank, :], w[0:NE, :], aT[:, tok], start=True, stop=True)
                m.wait(act, m.M(mm), *z2_free[i])
                gr = m.A(act.activation(dst[:, i, :], m.psum[:, bank, :], ACT.Copy))
                m.banks.freed[bank] = (gr,)
            bank, free = m.banks.take()
            m.wait(pe, *free)
            for c in range(DC):
                mm = pe.matmul(m.psum[:, bank, :], m.small["Win1"][:, c, :], m.XT[:, c, tok], start=(c == 0), stop=(c == DC - 1))
            xt_used = m.M(mm)
            m.wait(dve, xt_used, gr, *z2_free[i])
            z1r = m.V(dve.scalar_tensor_tensor(out=z1[:, i, :], in0=m.psum[:, bank, :], scalar=m.small["win1_b"][:, 0:1],
                                               in1=g1[:, i, :], op0=ALU.add, op1=ALU.mult))
            m.banks.freed[bank] = (z1r,)
            h_slot, h_free = m.h_ring.take()
            m.wait(act, *h_free)
            hm = []
            for f in range(8):
                bank, free = m.banks.take()
                m.wait(pe, z1r, *free)
                mm = pe.matmul(m.psum[:, bank, :], m.small["Wout1"][:, f, :], z1[:, i, :], start=True, stop=True)
                m.wait(act, m.M(mm))
                hr = m.A(act.activation(m.H[:, h_slot, f, :], m.psum[:, bank, :], ACT.Gelu))
                m.banks.freed[bank] = (hr,)
                hm.append(hr)
            bank, free = m.banks.take()
            m.wait(pe, *free)
            for f in range(8):
                m.wait(pe, hm[f])
                mm = pe.matmul(m.psum[:, bank, :], m.small["Win2"][:, f, :], m.H[:, h_slot, f, :], start=(f == 0), stop=(f == 7))
            h_used = m.M(mm)
            m.h_ring.freed[h_slot] = (h_used,)
            m.wait(dve, h_used)
            z2r = m.V(dve.scalar_tensor_tensor(out=z2[:, i, :], in0=m.psum[:, bank, :], scalar=m.small["win2_b"][:, 0:1],
                                               in1=g2[:, i, :], op0=ALU.add, op1=ALU.mult))
            m.banks.freed[bank] = (z2r,)
            for half in range(2):
                bank, free = m.banks.take()
                m.wait(pe, z2r, *free)
                for j in range(2):
                    k = half * 2 + j
                    mm = pe.matmul(m.psum[:, bank, j * D:(j + 1) * D], z2[:, i, k * P:(k + 1) * P], m.small["Wout2"][:, :], start=True, stop=True)
                out = m.M(mm)
                t = g * G + half * 2
                m.wait(dve, out, m.x_ready[t], m.x_ready[t + 1])
                added = m.V(dve.tensor_tensor(m.X[:, t:t + 2, :], m.X[:, t:t + 2, :],
                                              m.psum[:, bank, :].rearrange("p (j d) -> p j d", j=2), ALU.add))
                m.banks.freed[bank] = (added,)
                m.x_ready[t:t + 2] = [added] * 2
            z2_free[i] = (out, added)
        m.xt_free = (xt_used,)
        m.barrier()



def layer3_mix(m, ins, scratch):
    SCALE = 64 ** -0.5
    KEYS = 2 * P
    m.layer("mix3")
    pe, dve, act, pool = m.pe, m.dve, m.act, m.pool
    load_context(m, ins, "_b", scratch, m.sp)
    xt = layernorm(m, m.xt_free)
    with ExitStack() as scratch:
        def sb(name, shape):
            return m.sb(name, shape, F32, scratch)
        qT, kT = sb("qT3", [P, 2, DC, GT]), sb("kT3", [P, 2, DC, GT])
        v = sb("v3", [P, 2, G, D])
        S = sb("scores3", [P, 2, 2, KEYS])
        mx, sm = sb("max3", [P, 2, 2]), sb("sum3", [P, 2, 2])
        sT = sb("scoresT3", [P, 2, 2, KEYS])
        free_g = [(), ()]
        ready = {}

        def products(g):
            i = g % 2
            tok = slice(g * GT, (g + 1) * GT)
            m.wait(pe, xt[g], m.small_ready)
            for w, bias, dst in (("q_w3", "q_b3", qT), ("k_w3", "k_b3", kT)):
                for o in range(DC):
                    bank, free = m.banks.take()
                    m.wait(pe, *free)
                    for c in range(DC):
                        mm = pe.matmul(m.psum[:, bank, :], m.small[w][:, c, o * P:(o + 1) * P], m.XT[:, c, tok], start=(c == 0), stop=(c == DC - 1))
                    m.wait(act, m.M(mm), m.small_ready, *free_g[i])
                    qk = m.A(act.activation(dst[:, i, o, :], m.psum[:, bank, :], ACT.Identity, bias=m.small[bias][:, o:o + 1]))
                    m.banks.freed[bank] = (qk,)
            for half in range(2):
                bank, free = m.banks.take()
                m.wait(pe, *free)
                for j in range(2):
                    t = g * G + half * 2 + j
                    for c in range(DC):
                        mm = pe.matmul(m.psum[:, bank, j * D:(j + 1) * D], m.XT[:, c, t * P:(t + 1) * P], m.small["v_w3"][:, c, :],
                                       start=(c == 0), stop=(c == DC - 1))
                xt_used = m.M(mm)
                m.wait(dve, xt_used, *free_g[i])
                vr = m.V(dve.tensor_tensor(v[:, i, half * 2:half * 2 + 2, :], m.psum[:, bank, :].rearrange("p (j d) -> p j d", j=2),
                                           bcast(m.small["v_b3"][:, :].unsqueeze(1), P, 2, D), ALU.add))
                m.banks.freed[bank] = (vr,)
            ready[g] = qk, vr, xt_used

        def attend(n):
            g, half, s, i = n // 2, n % 2, n % 2, n // 2 % 2
            if half == 0:
                products(g)
            qk, vr, _ = ready[g]
            bank, free = m.banks.take()
            m.wait(pe, qk, *free)
            for j in range(2):
                k = half * 2 + j
                loc = slice(k * P, (k + 1) * P)
                glob = slice((g * G + k) * P, (g * G + k + 1) * P)
                for part, keys in ((0, lambda c: m.CTXT[:, c, glob]), (1, lambda c: kT[:, i, c, loc])):
                    col = j * KEYS + part * P
                    for c in range(DC):
                        mm = pe.matmul(m.psum[:, bank, col:col + P], qT[:, i, c, loc], keys(c), start=(c == 0), stop=(c == DC - 1))
            full = m.M(mm)
            yield
            m.wait(dve, full)
            src = m.psum[:, bank, :].rearrange("p (j s) -> p j s", j=2)
            m.VV(dve.tensor_reduce(mx[:, s], src, AX.X, ALU.max))
            sub = m.V(dve.tensor_tensor(S[:, s], src, bcast(mx[:, s].unsqueeze(2), P, 2, KEYS), ALU.subtract))
            m.banks.freed[bank] = (sub,)
            m.wait(act, sub)
            ex = m.A(act.activation(S[:, s], S[:, s], ACT.Exp, scale=SCALE))
            yield
            m.wait(dve, ex)
            m.VV(dve.tensor_reduce(sm[:, s], S[:, s], AX.X, ALU.add))
            m.VV(dve.reciprocal(sm[:, s], sm[:, s]))
            bank, free = m.banks.take()
            m.wait(pe, ex, *free)
            for j in range(2):
                for part in range(2):
                    col = j * KEYS + part * P
                    mm = pe.transpose(m.psum[:, bank, col:col + P], S[:, s, j, part * P:(part + 1) * P], m.ident[:, :])
            full = m.M(mm)
            yield
            m.wait(act, full)
            st = m.A(act.activation(sT[:, s].rearrange("p j s -> p (j s)"), m.psum[:, bank, :], ACT.Copy))
            m.banks.freed[bank] = (st,)
            bank, free = m.banks.take()
            m.wait(pe, st, vr, m.ctx_ready, *free)
            for j in range(2):
                k = half * 2 + j
                t = g * G + k
                pe.matmul(m.psum[:, bank, j * D:(j + 1) * D], sT[:, s, j, 0:P], m.CTX[:, t, :], start=True, stop=False)
                mm = pe.matmul(m.psum[:, bank, j * D:(j + 1) * D], sT[:, s, j, P:KEYS], v[:, i, k, :], start=False, stop=True)
            out = m.M(mm)
            free_g[i] = (out,)
            yield
            m.wait(dve, out)
            for j in range(2):
                t = g * G + half * 2 + j
                m.wait(dve, m.x_ready[t])
                m.x_ready[t] = m.V(dve.scalar_tensor_tensor(out=m.X[:, t, :], in0=m.psum[:, bank, j * D:(j + 1) * D],
                                                            scalar=sm[:, s, j:j + 1], in1=m.X[:, t, :], op0=ALU.mult, op1=ALU.add))
            m.banks.freed[bank] = (m.x_ready[t],)

        interleave([attend(n) for n in range(2 * NG)], 2)
        xt_used = ready[NG - 1][2]
        m.xt_free = (xt_used,)
        m.barrier()


def wide_buffers(m, name, size):
    m.XT = m.sb("XT" + name, [P, DC, T * P], F32, m.wide)
    m.W = Weights(m, name, m.wide, 1, size)


def load_context(m, ins, name, ctx, queue):
    m.CTX = m.sb("CTX" + name, [P, T, D], F32, ctx)
    m.ctx_ready = m.S_ctx.after(queue.dma_start(m.CTX[:, :, :], ins["ctx"]))


LAYERS = [layer0_mix, layer0_ffn, layer1_mix, layer1_ffn, layer2_mix, layer2_ffn, layer3_mix, layer3_ffn]
NLAYERS = 8


def build(nc, ins, out, x_table, y_table):
    with ExitStack() as ctx:
        m = Machine(nc, ctx)
        m.psum = ctx.enter_context(nc.psum_tensor("psum", [P, 8, BANK], F32))
        m.banks = Ring(8)
        constants(m, ins)
        m.CTXT = m.sb("CTXT", [P, DC, T * P])
        m.xt_free = ()
        m.ln_stats, m.ln_mv, m.ln_rstd = m.sb("ln_stats", [P, 2, G, 6]), m.sb("ln_mv", [P, 2, G, 2]), m.sb("ln_rstd", [P, 2, G])
        NR = 64
        m.top_key, m.top_best = m.sb("top_key", [P, NR, 8]), m.sb("top_best", [P, NR])
        m.top_v, m.top_h = m.sb("top_v", [P, 2, NR]), m.sb("top_h", [P, 2, NR, 8])
        m.route, m.gates = m.sb("route", [P, T, 8]), m.sb("gates", [P, T, 8])
        m.pos = m.sb("pos", [P, 2, T], I32)
        m.arriving = None
        m.cum = m.sb("cum", [P, 2, T, 8])
        m.wide = ExitStack()
        load_context(m, ins, "_a", m.wide, m.act)
        wide_buffers(m, "_a", 2048)
        m.x_table, m.y_table = x_table, y_table

        zeros = m.cum[:, :, :, :].rearrange("p k t e -> p (k t e)").unsqueeze(1)
        m.wait(m.act, m.V(m.dve.memset(zeros, 0.0)))
        S_zero = m.counter("zero_tables", 16)
        for table in (x_table, y_table):
            rows = table.rearrange("(n p a) d -> n p a d", a=16, p=P)
            for n in range(rows.shape[0]):
                m.zeroed = S_zero.after(m.act.dma_start(rows[n], bcast(zeros, P, 16, D)))

        def barrier():
            ends = tuple((s, s.value) for s in (m.S_pe, m.S_dve, m.S_act, m.S_pool) if s.value)
            for eng in (m.pe, m.dve, m.act, m.pool, m.sp):
                m.wait(eng, *ends)
        m.barrier = barrier
        for n, layer in enumerate(LAYERS[:NLAYERS]):
            with ExitStack() as part:
                if layer not in (layer0_ffn, layer1_mix, layer1_ffn, layer2_mix, layer3_ffn):
                    m.LN = m.sb(f"LN{n}", [P, 1, G, D], F32, part)
                    m.ln_ring = Ring(1)
                if layer is layer2_ffn:
                    m.H = m.sb(f"H{n}", [P, 1, 8, GT], F32, part)
                    m.h_ring = Ring(1)
                if layer in (layer2_mix, layer3_ffn):
                    m.gates_fm = m.sb(f"gates_fm{n}", [8, 2, 2 * P], F32, part)
                if m.arriving:
                    m.arriving.open()
                arriving = m.arriving
                layer(m, ins, part)
                m.barrier()
            if arriving and arriving is m.arriving:
                arriving.close()
            if layer is layer1_ffn:
                wide_buffers(m, "_b", 4096)
        S_out = m.counter("store", 16)
        ctx.push(m.wide)
        m.wait(m.sp, m.zeroed, m.small_ready, m.ctx_ready)
        if m.arriving:
            m.arriving.open()
        for g in range(NG):
            if m.arriving:
                m.arriving.need(g)
            tiles = slice(g * G, (g + 1) * G)
            m.wait(m.sp, *m.x_ready[tiles])
            stored = S_out.after(m.sp.dma_start(out[:, tiles, :], m.X[:, tiles, :]))
        m.wait(m.sp, stored)
        if m.arriving:
            m.arriving.close()


def chunks(w):
    n = w.shape[0] // P
    return w.reshape(n, P, w.shape[1]).transpose(1, 0, 2)


def kernel(**a):
    import numpy as np
    import concourse.bacc as bacc
    from concourse.bass_utils import run_bass_kernel_spmd

    a = {k: np.asarray(v) for k, v in a.items()}

    def tiles(x):
        return x.transpose(1, 0, 2)

    def ffn(w1, w2):
        E = w1.shape[0]
        w1 = np.stack([chunks(w1[e]).reshape(P, -1) for e in range(E)])
        w2 = np.stack([chunks(w2[e]).reshape(P, -1) for e in range(E)])
        return w1, w2

    h = {"x": tiles(a["x"]), "ctx": tiles(a["ctx_1024"]), "mask": a["mask_BxS2_bk0"].reshape(1, -1)}
    h["gate_w0"] = chunks(np.concatenate([a["L0_xattn_igate_w"], a["L0_xattn_fgate_w"]]).T)
    h["gate_b0"] = np.concatenate([a["L0_xattn_igate_b"], a["L0_xattn_fgate_b"]])[None]
    h["head_scale0"] = a["L0_xattn_out_w"][None]
    h["router_w0"] = chunks(a["L0_ffn_router_w"].T)
    h["ffn0_w1"], h["ffn0_w2"] = ffn(a["L0_ffn_fc1_w"].transpose(0, 2, 1), a["L0_ffn_fc2_w"].transpose(0, 2, 1))
    h["rms_scale"] = a["L1_xattn_rms_scale"][None]
    h["q_w1"] = chunks(a["L1_xattn_q_w"].transpose(1, 0, 2).reshape(D, D))
    h["kv_w1"] = chunks(a["L1_xattn_kv_w"][[0, 0, 1], 0].transpose(1, 0, 2).reshape(D, 3 * 64))
    h["out_w1"] = chunks(a["L1_xattn_out_w"].reshape(D, D))
    freq = np.float32(10000.0) ** (np.float32(2.0 / 64) * np.arange(32, dtype=np.float32))
    pos = np.arange(2 * P, dtype=np.float32).reshape(2, P, 1) / freq
    pos = pos[[1, 1, 1, 1, 0, 0]].transpose(1, 0, 2)
    h["cos"] = np.cos(pos).astype(np.float32)
    h["sin"] = np.stack([-np.sin(pos), np.sin(pos)], axis=2).astype(np.float32)
    h["sel_w1"] = chunks(np.concatenate([a["L1_ffn_sel_v_w"], a["L1_ffn_sel_o_w"]]).T)
    h["route_scale"] = a["L1_ffn_route_scale"][None]
    for k in "qk":
        w = a[f"L1_ffn_{k}_w"].reshape(8, P, D).transpose(0, 2, 1)
        h["ffn1_" + k] = np.stack([chunks(w[i]).reshape(P, -1) for i in range(8)])
    w = a["L1_ffn_v_w"].reshape(8, 8, D, P).transpose(0, 2, 1, 3).reshape(8, D, 8 * P)
    h["ffn1_v"] = np.stack([chunks(w[i]).reshape(P, -1) for i in range(8)])
    h["ffn1_o"] = a["L1_ffn_o_w"].reshape(8, 8, P, D).transpose(0, 2, 1, 3).reshape(8, P, 8 * D)
    h["router_w2"] = chunks(a["L2_xattn_Wg"])
    h["router_b2"] = a["L2_xattn_bg"][None]
    h["mix2_w1"], h["mix2_w2"] = ffn(a["L2_xattn_W1"], a["L2_xattn_W2"])
    h["b1_2"] = a["L2_xattn_b1"].reshape(8, 8, P).transpose(2, 0, 1)
    h["b2_2"] = a["L2_xattn_b2"]
    h["proj2"] = chunks(a["L2_ffn_proj"])
    h["C1"], h["C2"] = a["L2_ffn_C1"], a["L2_ffn_C2"]
    h["Win1"], h["win1_b"] = chunks(a["L2_ffn_Win1"][:D]), a["L2_ffn_Win1"][D][:, None]
    h["Wout1"] = a["L2_ffn_Wout1"].T.reshape(P, 8, P)
    h["Win2"], h["win2_b"] = chunks(a["L2_ffn_Win2"][:1024]), a["L2_ffn_Win2"][1024][:, None]
    h["Wout2"] = a["L2_ffn_Wout2"].T
    for k in "qkv":
        h[k + "_w3"] = chunks(a[f"L3_xattn_W{k}"].T)
    for k in "qk":
        h[k + "_b3"] = a[f"L3_xattn_b{k}"].reshape(DC, P).T
    h["v_b3"] = a["L3_xattn_bv"][None]
    h["router_w3"] = chunks(a["L3_ffn_gate_w"])
    h["router_b3"] = a["L3_ffn_gate_b"][None]
    w1 = np.concatenate([a["L3_ffn_sh_w1"][None], a["L3_ffn_ew1"]])
    w2 = np.concatenate([a["L3_ffn_sh_w2"][None], a["L3_ffn_ew2"]])
    h["ffn3_w1"], h["ffn3_w2"] = ffn(w1, w2)
    h["b1_3"] = np.concatenate([a["L3_ffn_sh_b1"][None], a["L3_ffn_eb1"]]).reshape(9, 8, P).transpose(2, 0, 1)
    h["b2_3"] = a["L3_ffn_eb2"]
    h["sh_b2_3"] = a["L3_ffn_sh_b2"][None]

    nc = bacc.Bacc("TRN2", target_bir_lowering=False, num_devices=1)
    arrays, ins = {}, {}
    for name, v in h.items():
        v = np.ascontiguousarray(v)
        arrays["in_" + name] = v
        ins[name] = nc.dram_tensor("in_" + name, v.shape, mybir.dt.from_np(v.dtype), kind="ExternalInput").ap()
    out = nc.dram_tensor("out", (P, T, D), F32, kind="ExternalOutput").ap()
    x_table, y_table = (nc.dram_tensor(n, (8 * T * P, D), F32, kind="Internal").ap() for n in ("x_table", "y_table"))
    build(nc, ins, out, x_table, y_table)
    r = run_bass_kernel_spmd(nc, [arrays], core_ids=[0])
    return np.ascontiguousarray(r.results[0]["out"].transpose(1, 0, 2))
```
